# Optimizing a Trainium2 kernel written in Bass

```python
import numpy as np
import jax
import jax.numpy as jnp

def _softmax(x, axis=-1):
    return jax.nn.softmax(x, axis=axis)

def _gelu(x):
    return jax.nn.gelu(x, approximate=True)

def _silu(x):
    return jax.nn.silu(x)

def _sigmoid(x):
    return jax.nn.sigmoid(x)

def _layernorm(x, axis=-1, eps=1e-05):
    m = jnp.mean(x, axis=axis, keepdims=True)
    v = jnp.var(x, axis=axis, keepdims=True)
    return (x - m) / jnp.sqrt(v + eps)

def _scatter_add(tgt, idx, src, axis=0):
    return tgt.at[idx].add(src)

def _segment_sum(src, seg, n):
    return jax.ops.segment_sum(src, seg, n)
kernel_name = 'mk_adaln_d1_jaxref_r8_e7e124'

def setup_inputs(seed: int=0):
    np.random.seed(seed)
    _w = jnp.asarray

    def _L0_attn_setup():
        import jax, jax.numpy as jnp
        import numpy as np
        HID = 128
        NH = 16
        HD = HID // NH
        WIN = 64
        EPS = 1e-05

        def layernorm(x, g, b):
            m = jnp.mean(x, axis=-1, keepdims=True)
            v = jnp.mean((x - m) ** 2, axis=-1, keepdims=True)
            return (x - m) / jnp.sqrt(v + EPS) * g + b

        def windowed_attention(q, k, v, window_size):
            bh, S, D = q.shape
            scale = float(D) ** (-0.5)
            w2, w4 = (window_size // 2, window_size // 4)
            out = jnp.zeros_like(q)
            for i in range(0, S, w2):
                start = max(0, i - w4)
                end = min(S, i + window_size - w4)
                qw = q[:, start:end] * scale
                kw = k[:, start:end]
                vw = v[:, start:end]
                attn = jax.nn.softmax(jnp.einsum('bqd,bkd->bqk', qw, kw), axis=-1)
                wo = jnp.einsum('bqk,bkd->bqd', attn, vw)
                if i == 0:
                    out = out.at[:, start:end].set(wo)
                else:
                    oe = min(i + w4, S)
                    n = oe - start
                    alphas = jnp.linspace(0.0, 1.0, n).reshape(1, -1, 1)
                    blended = (1 - alphas) * out[:, start:oe] + alphas * wo[:, :n]
                    out = out.at[:, start:oe].set(blended)
                    out = out.at[:, oe:end].set(wo[:, n:end - start])
            return out
        key = jax.random.key(seed)
        ks = jax.random.split(key, 12)
        s = 0.02
        d = {'hidden_states': jax.random.normal(ks[0], (4, 256, HID), jnp.float32), 'ln1_g': jnp.ones((HID,), jnp.float32), 'ln1_b': jnp.zeros((HID,), jnp.float32), 'wq': jax.random.normal(ks[1], (HID, HID), jnp.float32) * s, 'bq': jnp.zeros((HID,), jnp.float32), 'wk': jax.random.normal(ks[2], (HID, HID), jnp.float32) * s, 'bk': jnp.zeros((HID,), jnp.float32), 'wv': jax.random.normal(ks[3], (HID, HID), jnp.float32) * s, 'bv': jnp.zeros((HID,), jnp.float32), 'wproj': jax.random.normal(ks[4], (HID, HID), jnp.float32) * s, 'bproj': jnp.zeros((HID,), jnp.float32), 'ln2_g': jnp.ones((HID,), jnp.float32), 'ln2_b': jnp.zeros((HID,), jnp.float32), 'w1': jax.random.normal(ks[5], (HID, 4 * HID), jnp.float32) * s, 'b1': jnp.zeros((4 * HID,), jnp.float32), 'w2': jax.random.normal(ks[6], (4 * HID, HID), jnp.float32) * s, 'b2': jnp.zeros((HID,), jnp.float32)}
        return d
    _L0_attn_in = _L0_attn_setup()

    def _L0_ffn_setup():
        import jax, jax.numpy as jnp
        import numpy as np
        import math
        GOLDEN_CENTER = 1.0 / math.e
        GOLDEN_LOWER = 0.5 - math.log(4.0 / 3.0)
        GOLDEN_UPPER = 0.5
        B, T, D = (4, 256, 128)
        E = 8
        I = 512 // (E // 2)

        def _routing_weights(x, Wr, temperature):
            inh = jax.nn.sigmoid(x @ Wr / temperature)
            in_zone = (inh >= GOLDEN_LOWER) & (inh <= GOLDEN_UPPER)
            dist = jnp.abs(inh - GOLDEN_CENTER)
            w = jnp.exp(-dist / 0.1) * in_zone.astype(x.dtype)
            wsum = w.sum(axis=-1, keepdims=True)
            no_expert = wsum < 1e-08
            fb = jnp.exp(-dist / 0.3)
            _, top2 = jax.lax.top_k(fb, 2)
            fb_mask = jax.nn.one_hot(top2, E, dtype=x.dtype).sum(axis=-2)
            fb_w = fb * fb_mask
            fb_w = fb_w / jnp.clip(fb_w.sum(axis=-1, keepdims=True), 1e-08)
            w = jnp.where(no_expert, fb_w, w)
            wsum = w.sum(axis=-1, keepdims=True)
            return w / jnp.clip(wsum, 1e-08)
        key = jax.random.key(seed)
        k = jax.random.split(key, 6)
        s_d = 1.0 / math.sqrt(D)
        s_i = 1.0 / math.sqrt(I)
        return {'x': jax.random.normal(k[0], (B, T, D), jnp.float32), 'Wg': jax.random.normal(k[1], (E, D, I), jnp.float32) * s_d, 'Wu': jax.random.normal(k[2], (E, D, I), jnp.float32) * s_d, 'Wd': jax.random.normal(k[3], (E, I, D), jnp.float32) * s_i, 'Wr': jax.random.normal(k[4], (D, E), jnp.float32) * s_d, 'temperature': jnp.ones((1,), jnp.float32)}
    _L0_ffn_in = _L0_ffn_setup()
    _L0_c = _w((lambda *s: np.random.randn(*s).astype(np.float32) * 0.05)(8, 128))
    _L0_wmod = _w((lambda *s: np.random.randn(*s).astype(np.float32) * 0.05)(128, 6 * 128) * 128 ** (-0.5))
    _d = {'L0_attn_hidden_states': _L0_attn_in['hidden_states'], 'L0_attn_ln1_g': _L0_attn_in['ln1_g'], 'L0_attn_ln1_b': _L0_attn_in['ln1_b'], 'L0_attn_wq': _L0_attn_in['wq'], 'L0_attn_bq': _L0_attn_in['bq'], 'L0_attn_wk': _L0_attn_in['wk'], 'L0_attn_bk': _L0_attn_in['bk'], 'L0_attn_wv': _L0_attn_in['wv'], 'L0_attn_bv': _L0_attn_in['bv'], 'L0_attn_wproj': _L0_attn_in['wproj'], 'L0_attn_bproj': _L0_attn_in['bproj'], 'L0_attn_ln2_g': _L0_attn_in['ln2_g'], 'L0_attn_ln2_b': _L0_attn_in['ln2_b'], 'L0_attn_w1': _L0_attn_in['w1'], 'L0_attn_b1': _L0_attn_in['b1'], 'L0_attn_w2': _L0_attn_in['w2'], 'L0_attn_b2': _L0_attn_in['b2'], 'L0_ffn_Wg': _L0_ffn_in['Wg'], 'L0_ffn_Wu': _L0_ffn_in['Wu'], 'L0_ffn_Wd': _L0_ffn_in['Wd'], 'L0_ffn_Wr': _L0_ffn_in['Wr'], 'L0_ffn_temperature': _L0_ffn_in['temperature'], 'L0_c': _L0_c, 'L0_wmod': _L0_wmod}
    _x0 = _d['L0_attn_hidden_states']
    _d['L0_attn_hidden_states'] = jax.random.normal(jax.random.fold_in(jax.random.key(seed), 1), (8, 256, 128), dtype=_x0.dtype)
    del _x0
    return _d

def reference(L0_attn_hidden_states, L0_attn_ln1_g, L0_attn_ln1_b, L0_attn_wq, L0_attn_bq, L0_attn_wk, L0_attn_bk, L0_attn_wv, L0_attn_bv, L0_attn_wproj, L0_attn_bproj, L0_attn_ln2_g, L0_attn_ln2_b, L0_attn_w1, L0_attn_b1, L0_attn_w2, L0_attn_b2, L0_ffn_Wg, L0_ffn_Wu, L0_ffn_Wd, L0_ffn_Wr, L0_ffn_temperature, L0_c, L0_wmod):

    def _L0_attn_ref(hidden_states, ln1_g, ln1_b, wq, bq, wk, bk, wv, bv, wproj, bproj, ln2_g, ln2_b, w1, b1, w2, b2):
        import jax, jax.numpy as jnp
        import numpy as np
        HID = 128
        NH = 16
        HD = HID // NH
        WIN = 64
        EPS = 1e-05

        def layernorm(x, g, b):
            m = jnp.mean(x, axis=-1, keepdims=True)
            v = jnp.mean((x - m) ** 2, axis=-1, keepdims=True)
            return (x - m) / jnp.sqrt(v + EPS) * g + b

        def windowed_attention(q, k, v, window_size):
            bh, S, D = q.shape
            scale = float(D) ** (-0.5)
            w2, w4 = (window_size // 2, window_size // 4)
            out = jnp.zeros_like(q)
            for i in range(0, S, w2):
                start = max(0, i - w4)
                end = min(S, i + window_size - w4)
                qw = q[:, start:end] * scale
                kw = k[:, start:end]
                vw = v[:, start:end]
                attn = jax.nn.softmax(jnp.einsum('bqd,bkd->bqk', qw, kw), axis=-1)
                wo = jnp.einsum('bqk,bkd->bqd', attn, vw)
                if i == 0:
                    out = out.at[:, start:end].set(wo)
                else:
                    oe = min(i + w4, S)
                    n = oe - start
                    alphas = jnp.linspace(0.0, 1.0, n).reshape(1, -1, 1)
                    blended = (1 - alphas) * out[:, start:oe] + alphas * wo[:, :n]
                    out = out.at[:, start:oe].set(blended)
                    out = out.at[:, oe:end].set(wo[:, n:end - start])
            return out
        B, S, _ = hidden_states.shape
        residual = hidden_states
        x = layernorm(hidden_states, ln1_g, ln1_b)
        q = (x @ wq + bq).reshape(B, S, NH, HD).transpose(0, 2, 1, 3).reshape(B * NH, S, HD)
        k = (x @ wk + bk).reshape(B, S, NH, HD).transpose(0, 2, 1, 3).reshape(B * NH, S, HD)
        v = (x @ wv + bv).reshape(B, S, NH, HD).transpose(0, 2, 1, 3).reshape(B * NH, S, HD)
        ctx = windowed_attention(q, k, v, WIN)
        ctx = ctx.reshape(B, NH, S, HD).transpose(0, 2, 1, 3).reshape(B, S, HID)
        out = ctx @ wproj + bproj + residual
        residual2 = out
        h = layernorm(out, ln2_g, ln2_b)
        h = jax.nn.gelu(h @ w1 + b1, approximate=False)
        h = h @ w2 + b2
        return h + residual2

    def _L0_ffn_ref(x, Wg, Wu, Wd, Wr, temperature):
        import jax, jax.numpy as jnp
        import numpy as np
        import math
        GOLDEN_CENTER = 1.0 / math.e
        GOLDEN_LOWER = 0.5 - math.log(4.0 / 3.0)
        GOLDEN_UPPER = 0.5
        B, T, D = (4, 256, 128)
        E = 8
        I = 512 // (E // 2)

        def _routing_weights(x, Wr, temperature):
            inh = jax.nn.sigmoid(x @ Wr / temperature)
            in_zone = (inh >= GOLDEN_LOWER) & (inh <= GOLDEN_UPPER)
            dist = jnp.abs(inh - GOLDEN_CENTER)
            w = jnp.exp(-dist / 0.1) * in_zone.astype(x.dtype)
            wsum = w.sum(axis=-1, keepdims=True)
            no_expert = wsum < 1e-08
            fb = jnp.exp(-dist / 0.3)
            _, top2 = jax.lax.top_k(fb, 2)
            fb_mask = jax.nn.one_hot(top2, E, dtype=x.dtype).sum(axis=-2)
            fb_w = fb * fb_mask
            fb_w = fb_w / jnp.clip(fb_w.sum(axis=-1, keepdims=True), 1e-08)
            w = jnp.where(no_expert, fb_w, w)
            wsum = w.sum(axis=-1, keepdims=True)
            return w / jnp.clip(wsum, 1e-08)
        weights = _routing_weights(x, Wr, temperature)
        gate = jnp.einsum('btd,edi->beti', x, Wg)
        up = jnp.einsum('btd,edi->beti', x, Wu)
        h = jax.nn.silu(gate) * up
        e_out = jnp.einsum('beti,eid->betd', h, Wd)
        out = jnp.einsum('bte,betd->btd', weights, e_out)
        return out
    x = L0_attn_hidden_states
    mod = (_silu(L0_c) @ L0_wmod).reshape(L0_c.shape[0], 6, 1, -1)
    sa, ca, ga, sb, cb, gb = (mod[:, 0], mod[:, 1], mod[:, 2], mod[:, 3], mod[:, 4], mod[:, 5])
    ga = (2 * (ga >= 0) - 1) * jnp.maximum(jnp.abs(ga), 0.25)
    gb = (2 * (gb >= 0) - 1) * jnp.maximum(jnp.abs(gb), 0.25)
    h = _layernorm(x, axis=-1) * (1 + ca) + sa
    x = x + ga * _L0_attn_ref(h, L0_attn_ln1_g, L0_attn_ln1_b, L0_attn_wq, L0_attn_bq, L0_attn_wk, L0_attn_bk, L0_attn_wv, L0_attn_bv, L0_attn_wproj, L0_attn_bproj, L0_attn_ln2_g, L0_attn_ln2_b, L0_attn_w1, L0_attn_b1, L0_attn_w2, L0_attn_b2)
    h = _layernorm(x, axis=-1) * (1 + cb) + sb
    x = x + gb * _L0_ffn_ref(h, L0_ffn_Wg, L0_ffn_Wu, L0_ffn_Wd, L0_ffn_Wr, L0_ffn_temperature)
    return x

_drawn_inputs = setup_inputs


def setup_inputs(seed=0):
    import zlib

    import numpy as np

    out = dict(_drawn_inputs(seed))
    spreads = {'L0_attn_ln1_g': (1.0, 0.6),
     'L0_attn_ln1_b': (0.0, 0.8),
     'L0_attn_bq': (0.0, 0.8),
     'L0_attn_bk': (0.0, 0.8),
     'L0_attn_bv': (0.0, 0.8),
     'L0_attn_bproj': (0.0, 0.27),
     'L0_attn_ln2_g': (1.0, 0.6),
     'L0_attn_ln2_b': (0.0, 0.8),
     'L0_attn_b1': (0.0, 0.8),
     'L0_attn_b2': (0.0, 0.271)}
    factors = {'L0_attn_wq': 8.0,
     'L0_attn_wk': 8.0,
     'L0_attn_wv': 8.0,
     'L0_attn_wproj': 7.839,
     'L0_attn_w1': 3.568,
     'L0_attn_w2': 3.311}
    for name, (base, spread) in spreads.items():
        noise = np.random.default_rng([zlib.crc32(name.encode()), seed]).standard_normal(out[name].shape)
        drawn = base * np.exp(spread * noise) if base else spread * noise
        out[name] = jnp.asarray(drawn.astype(out[name].dtype))
    for name, factor in factors.items():
        out[name] = (out[name] * factor).astype(out[name].dtype)
    return out
```

```python
from contextlib import ExitStack

import concourse.bass as bass
from concourse import mybir
from concourse.alu_op_type import AluOpType as ALU

F32 = mybir.dt.float32
BF16 = mybir.dt.bfloat16
ACT = mybir.ActivationFunctionType
AX_X = mybir.AxisListType.X

P = 128
B, S, D = 8, 256, 128
TPB = S // P
NT = B * TPB
NH, HD = 16, 8
H2 = NH // 2
WIN = 64
PAD = WIN // 4
LINE = S + 2 * PAD
TERMS = 6
ROWS = HD * TERMS
VC = HD + 1
FF = 4
E = 8
GT = 4
NG = NT // GT
GW = GT * P
EPS = 1e-5
SCALE = float(HD) ** -0.5
CA, SA, GA, GB = range(4)
LN1G, LN1B, BQ, BK, BV, LN2G, LN2B, B1 = range(8)
ZONE_MID = 0.36787944117144233
ZONE_LOW = 0.21231792754821915
ZONE_HIGH = 0.5


def build(nc, x, wqkvp, w1, w2, wg, wu, wd, wr, temp, c_t, wmod, cols, rows, ident, alpha, vmask,
          mones, selw, earlier, out):
    ctx = ExitStack()

    def sb(name, shape, dt=F32):
        return ctx.enter_context(nc.sbuf_tensor(name, shape, dt))

    def sem(name):
        return ctx.enter_context(nc.semaphore(name))

    ahead_by = {}

    def counts_from(s, n):
        ahead_by[s.name] = n
        return s

    def after(s, n):
        return (max(n, 0) if isinstance(n, int) else n) + ahead_by.get(s.name, 0)

    def apart(eng):
        eng.sem_inc(waits_met, 1)

    def ds(i, n):
        return slice(i, i + n) if isinstance(i, int) else bass.ds(i, n)

    with ctx:
        wa = sb("wa", [P, 4, D])
        w1s = sb("w1s", [P, FF, P])
        w2s = sb("w2s", [P, FF, D])
        wgs = sb("wgs", [P, E, P])
        wus = sb("wus", [P, E, P])
        wds = sb("wds", [P, E, D])
        wrs = sb("wrs", [P, E])
        temps = sb("temps", [P, 1])
        rtemp = sb("rtemp", [P, 1])
        cts = sb("cts", [P, B])
        wms = sb("wms", [P, 6, D])
        col = sb("col", [P, 7 + FF])
        row = sb("row", [P, 2, D])
        idf = sb("idf", [P, P])
        idb = sb("idb", [P, P], BF16)
        alph = sb("alph", [P, 2, 4])
        vmsk = sb("vmsk", [P, 2, 2])
        monesf = sb("monesf", [4, P])
        monesb = sb("monesb", [4, P], BF16)
        selwf = sb("selwf", [3 * E, E, P])
        selwb = sb("selwb", [3 * E, E, P], BF16)
        earl = sb("earl", [P, E, E])
        bqs = sb("bqs", [P, 1])
        mhalf = sb("mhalf", [P, NT])
        sce = sb("sce", [P, 4, B])
        scb = sb("scb", [P, P])
        modb = sb("modb", [P, B, 4, D])
        modt = sb("modt", [P, 2, B])
        xs = sb("xs", [P, NT, D])
        res = sb("res", [P, NT, D])
        st = sb("st", [P, GT, 6])
        mv = sb("mv", [P, GT, 2])
        ve = sb("ve", [P, GT])
        rs = sb("rs", [P, GT])
        xh = sb("xh", [P, TPB, D])
        h1 = sb("h1", [P, TPB, D])
        x1h = sb("x1h", [P, TPB, D])
        st2 = sb("st2", [P, TPB, 6])
        mv2 = sb("mv2", [P, TPB, 2])
        mean2 = sb("mean2", [P, NT])
        ve2 = sb("ve2", [P, NT])
        rs2 = sb("rs2", [P, NT])
        x1t = [sb(f"x1t{i}", [P, LINE]) for i in range(2)]
        x1v = [sb(f"x1v{i}", [P, LINE]) for i in range(2)]
        qk = sb("qk", [P, 2, LINE])
        qkr = sb("qkr", [P, 2, LINE])
        parts = sb("parts", [P, 3, 2, LINE], BF16)
        qst = [sb(f"qst{i}", [P, H2, LINE], BF16) for i in range(2)]
        kst = [sb(f"kst{i}", [P, H2, LINE], BF16) for i in range(2)]
        nm = sb("nm", [P, 8, H2])
        mp = sb("mp", [P, 2, 4 * H2], BF16)
        mt = sb("mt", [2 * 4 * H2, P], BF16)
        mrow = [sb(f"mrow{i}", [4, 8 * H2, WIN], BF16) for i in range(2)]
        prob = [sb(f"prob{i}", [P, H2, 2, WIN]) for i in range(2)]
        vb = [sb(f"vb{i}", [P, 2, NH, 2, 2, VC]) for i in range(2)]
        rsum = sb("rsum", [P, H2, 4])
        fac = sb("fac", [P, H2, 4])
        ctxn = sb("ctxn", [P, 2, 2, D])
        ctxt = sb("ctxt", [P, S])
        xh2 = [sb(f"xh2{i}", [P, GT, D]) for i in range(2)]
        h2t = sb("h2t", [P, NT * P])
        gt = sb("gt", [P, FF, GW])
        resb = sb("resb", [P, GT, D])
        comb = sb("comb", [P, GT, D])
        h3t = sb("h3t", [P, NT * P])
        wt = sb("wt", [3 * E, NT * P], BF16)
        rt = [sb(f"rt{i}", [P, NT, E]) for i in range(5)]
        rc = [sb(f"rc{i}", [P, NT, E, E]) for i in range(2)]
        rsm = [sb(f"rsm{i}", [P, NT]) for i in range(3)]
        wp = sb("wp", [P, NT, 3, E], BF16)
        sg = [sb(f"sg{i}", [P, GW]) for i in range(2)]
        sw = sb("sw", [P, GW])
        hh = [sb(f"hh{i}", [P, GW]) for i in range(2)]
        fin = [sb(f"fin{i}", [P, GT, D]) for i in range(2)]

        bk = [ctx.enter_context(nc.psum_tensor(f"bank{i}", [P, 512], F32)) for i in range(8)]
        psa, psb, psv, (w0b, w1b) = bk[0:2], bk[2:4], bk[4:6], bk[6:8]

        scr = nc.dram_tensor("stack_scratch", [B, P, TERMS, 2, LINE], BF16, kind="Internal").ap()
        scr_rows = scr.rearrange("b (r h d) t k n -> b r k (d t) h n", r=2, h=H2)

        waits_met = sem("waits_met")
        x_first, x_rest = sem("x_first"), sem("x_rest")
        c_loaded, small_loaded, wa_loaded = sem("c_loaded"), sem("small_loaded"), sem("wa_loaded")
        late_loaded = sem("late_loaded")
        consts = sem("consts")
        consts_pool = sem("consts_pool")
        sc_step, sc_exp = sem("sc_step"), sem("sc_exp")
        scb_ready = sem("scb_ready")
        mod_done = sem("mod_done")
        mod_ready = sem("mod_ready")
        modt_done, modt_ready = sem("modt_done"), sem("modt_ready")
        ln_dve, ln_pool = sem("ln_dve"), sem("ln_pool")
        xt_done = sem("xt_done")
        x1t_ready = sem("x1t_ready")
        x1v_ready = sem("x1v_ready")
        qk_done, qk_ready = sem("qk_done"), sem("qk_ready")
        parts_step = sem("parts_step")
        scr_written = sem("scr_written")
        stack_ready = sem("stack_ready")
        v_done, v_ready = sem("v_done"), sem("v_ready")
        a_done, max_done = sem("a_done"), sem("max_done")
        mp_step = sem("mp_step")
        mt_done, mt_ready = sem("mt_done"), sem("mt_ready")
        mrow_ready = sem("mrow_ready")
        b_done, exp_done = sem("b_done"), sem("exp_done")
        pv_done = sem("pv_done")
        norm_step = sem("norm_step")
        ctx_done, ctxt_ready = sem("ctx_done"), sem("ctxt_ready")
        proj_done, att_ready = sem("proj_done"), sem("att_ready")
        ln2_step, ln2_root = sem("ln2_step"), sem("ln2_root")
        gate_step = sem("gate_step")
        xh2_ready = sem("xh2_ready")
        t2_done, h2t_ready = sem("t2_done"), sem("h2t_ready")
        w1_done, gelu_done = sem("w1_done"), sem("gelu_done")
        w2_done = sem("w2_done")
        resb_ready = sem("resb_ready")
        comb_step = sem("comb_step")
        ln3_step, ln3_root = sem("ln3_step"), sem("ln3_root")
        t3_done, h3t_ready = sem("t3_done"), sem("h3t_ready")
        router_done = sem("router_done")
        rt_step, rt_exp = sem("rt_step"), sem("rt_exp")
        wt_done, wt_ready = sem("wt_done"), sem("wt_ready")
        gate_done, up_done, wb_done = sem("gate_done"), sem("up_done"), sem("wb_done")
        silu_done, sw_done, hh_ready = sem("silu_done"), sem("sw_done"), sem("hh_ready")
        down_done = sem("down_done")
        fin_step = sem("fin_step")
        out_stored = sem("out_stored")

        ahead = [att_ready, proj_done, ctx_done, norm_step, exp_done, pv_done, ln2_step, h2t_ready, t2_done,
                 gelu_done, comb_step, w2_done, t3_done, silu_done, hh_ready, fin_step, sw_done, down_done]
        for s in ahead:
            counts_from(s, 1)
        counts_from(out_stored, 16)

        block = ctx.enter_context(nc.Block())

        def steps(eng, step):
            with eng.Fori(0, (B - 2) // 2) as i:
                for n in range(2):
                    step(2 * i + n, n, True, True)
            step(B - 2, 0, False, True)
            step(B - 1, 1, False, False)

        @block.sync
        def _(sp):
            def write_parts(b):
                sp.wait_ge(parts_step, after(parts_step, 4 * (b + 1)))
                apart(sp)
                dst = scr[ds(b, 1)].rearrange("b p t k n -> (b p) t k n")
                for t0, n, k, src in ((0, 3, 0, parts[:, 0:1, 0, :].broadcast_to([P, 3, LINE])),
                                      (3, 2, 0, parts[:, 1:2, 0, :].broadcast_to([P, 2, LINE])),
                                      (5, 1, 0, parts[:, 2:3, 0, :]),
                                      (0, 3, 1, parts[:, :, 1, :]),
                                      (3, 2, 1, parts[:, 0:2, 1, :]),
                                      (5, 1, 1, parts[:, 0:1, 1, :])):
                    sp.dma_start(dst[:, t0:t0 + n, k, :], src).then_inc(scr_written, 16)

            def read_stacks(b, n):
                sp.wait_ge(scr_written, after(scr_written, 96 * (b + 1)))
                apart(sp)
                sp.wait_ge(b_done, after(b_done, 8 * (b - 1)))
                apart(sp)
                for k, stack in enumerate((qst[n], kst[n])):
                    for r in range(2):
                        src = scr_rows[ds(b, 1), r, k].rearrange("b r h n -> (b r) h n")
                        sp.dma_start(stack[64 * r:64 * r + ROWS], src).then_inc(stack_ready, 16)

            def write_mrow(b, n, hf):
                sp.wait_ge(mt_ready, after(mt_ready, 2 * b + hf + 1))
                apart(sp)
                for part in range(2):
                    for half in range(2):
                        r = 2 * part + half
                        sp.dma_start(mrow[n][r:r + 1, 32 * hf:32 * hf + 32, :],
                                     mt[32 * part:32 * part + 32, WIN * half:WIN * half + WIN]
                                     ).then_inc(mrow_ready, 16)

            x_v = x.rearrange("b (k p) d -> p (b k) d", p=P)
            sp.dma_start(xs[:, 0:2], x_v[:, 0:2]).then_inc(x_first, 16)
            sp.dma_start(cts[:], c_t).then_inc(c_loaded, 16)
            sp.dma_start(wms[:], wmod.rearrange("p (c d) -> p c d", c=6)).then_inc(c_loaded, 16)
            for dst, src in ((col, cols), (row, rows.rearrange("o (r d) -> o r d", r=2).broadcast_to([P, 2, D])),
                             (idf, ident)):
                sp.dma_start(dst[:], src).then_inc(small_loaded, 16)
            sp.dma_start(xs[:, 2:NT], x_v[:, 2:NT]).then_inc(x_rest, 16)
            sp.dma_start(wa[:], wqkvp.rearrange("p (c d) -> p c d", c=4)).then_inc(wa_loaded, 16)
            for dst, src in ((alph, alpha), (vmsk, vmask), (monesf, mones)):
                sp.dma_start(dst[:], src).then_inc(small_loaded, 16)

            for b in range(2):
                write_parts(b)
                read_stacks(b, b)
            for dst, src in ((w1s, w1.rearrange("p (c d) -> p c d", c=FF)),
                             (w2s, w2.rearrange("(c p) d -> p c d", p=P)),
                             (wgs, wg.rearrange("e p i -> p e i")), (wus, wu.rearrange("e p i -> p e i")),
                             (wds, wd.rearrange("e p i -> p e i")), (wrs, wr),
                             (temps, temp.rearrange("(o n) -> o n", o=1).broadcast_to([P, 1])),
                             (selwf, selw), (earl, earlier.rearrange("o e f -> o e f").broadcast_to([P, E, E]))):
                sp.dma_start(dst[:], src).then_inc(late_loaded, 16)
            write_mrow(0, 0, 0)
            write_mrow(0, 0, 1)

            def step(b, n, prep, ahead):
                if ahead:
                    write_mrow(b + 1, 1 - n, 0)
                if prep:
                    write_parts(b + 2)
                if ahead:
                    write_mrow(b + 1, 1 - n, 1)
                if prep:
                    read_stacks(b + 2, n)

            steps(sp, step)

            out_v = out.rearrange("b (k p) d -> p (b k) d", p=P)
            with sp.Fori(0, NG // 2) as i:
                for n in range(2):
                    g = 2 * i + n
                    sp.wait_ge(fin_step, after(fin_step, 2 * g + 2))
                    apart(sp)
                    sp.dma_start(out_v[:, ds(GT * g, GT)], fin[n][:]).then_inc(out_stored, 16)
            sp.wait_ge(out_stored, after(out_stored, 16 * NG))

        @block.tensor
        def _(pe):
            def modulation(b, bank):
                pe.wait_ge(scb_ready, after(scb_ready, b + 1))
                pe.matmul(bank[:], scb[:], wms[:, 0:4, :], start=True, stop=True).then_inc(mod_done, 1)

            def transpose_x(b):
                pe.wait_ge(ln_dve, after(ln_dve, 14 * (b + 1)))
                for k in range(TPB):
                    m = pe.transpose(w0b[:, k * P:(k + 1) * P], x1h[:, k, :], idf[:])
                m.then_inc(xt_done, 1)

            def project_qk(b, n):
                pe.wait_ge(x1t_ready, after(x1t_ready, 2 * (b + 1)))
                pe.matmul(w0b[:, 0:LINE], wa[:, 0, :], x1t[n][:], start=True, stop=True)
                pe.matmul(w1b[:, 0:LINE], wa[:, 1, :], x1t[n][:], start=True, stop=True
                          ).then_inc(qk_done, 1)

            def project_v(b, n):
                pe.wait_ge(x1v_ready, after(x1v_ready, b + 1))
                for eo in range(2):
                    for sel in range(2):
                        j, at = 2 * eo + sel, 32 * eo + P * sel
                        m = pe.matmul(w0b[:, j * P:(j + 1) * P], x1v[n][:, at:at + P], wa[:, 2, :],
                                      start=True, stop=True)
                m.then_inc(v_done, 1)

            def spans(g):
                eo, par, sel = g // 4, g // 2 % 2, g % 2
                return par, [(half, 32 * (4 * sel + 2 * half + eo)) for half in range(2)]

            def scores_a(b, n, g):
                pe.wait_ge(stack_ready, after(stack_ready, 64 * (b + 1)))
                pe.wait_ge(max_done, after(max_done, 8 * b + g - 1))
                apart(pe)
                par, halves = spans(g)
                rows_ = slice(64 * par, 64 * par + ROWS)
                for h2 in range(H2):
                    for half, at in halves:
                        m = pe.matmul(psa[g % 2][WIN * half:WIN * half + WIN, WIN * h2:WIN * h2 + WIN],
                                      qst[n][rows_, h2, at:at + WIN], kst[n][rows_, h2, at:at + WIN],
                                      start=True, stop=True)
                m.then_inc(a_done, 1)

            def scores_b(b, n, g):
                pe.wait_ge(mrow_ready, after(mrow_ready, 128 * b + 64 * (g // 4 + 1)))
                if g:
                    pe.wait_ge(exp_done, after(exp_done, 8 * b + g - 1))
                par, halves = spans(g)
                bank = psb[g % 2]
                pe.matmul(bank[:], monesb[:], mrow[n][:, H2 * g:H2 * g + H2, :], start=True, stop=False,
                          skip_group_check=True)
                rows_ = slice(64 * par, 64 * par + ROWS)
                for h2 in range(H2):
                    for half, at in halves:
                        m = pe.matmul(bank[WIN * half:WIN * half + WIN, WIN * h2:WIN * h2 + WIN],
                                      kst[n][rows_, h2, at:at + WIN], qst[n][rows_, h2, at:at + WIN],
                                      start=False, stop=True, skip_group_check=True)
                m.then_inc(b_done, 1)

            def transpose_m(b, hf):
                pe.wait_ge(mp_step, after(mp_step, 4 * b + 2 * hf + 2))
                apart(pe)
                pe.transpose(w1b[0:64, 0:64].bitcast(BF16), mp[:].rearrange("p a c -> p (a c)"), idb[:]
                             ).then_inc(mt_done, 1)

            def probs_v(b, n, gp):
                pe.wait_ge(exp_done, after(exp_done, 8 * b + 2 * gp + 2))
                pe.wait_ge(v_ready, after(v_ready, 4 * (b + 1)))
                if gp:
                    pe.wait_ge(norm_step, after(norm_step, 4 * (4 * b + gp - 1)))
                eo, par = gp // 2, gp % 2
                for h2 in range(H2):
                    m = pe.matmul(psv[gp % 2][:, 4 * VC * h2:4 * VC * (h2 + 1)], prob[gp % 2][:, h2, :, :],
                                  vb[n][:, eo, H2 * par + h2, :, :, :], start=True, stop=True)
                m.then_inc(pv_done, 1)

            def gather_context(b):
                pe.wait_ge(norm_step, after(norm_step, 16 * (b + 1)))
                for eo in range(2):
                    for half in range(2):
                        at = 32 * eo + WIN * half
                        dst = w1b[:, at:at + 2 * P].rearrange("p (s q) -> p s q", s=2)[:, :, 0:WIN]
                        m = pe.matmul(dst, ctxn[:, eo, half, :], idf[:], start=(eo == half == 0), stop=True,
                                      skip_group_check=True)
                m.then_inc(ctx_done, 1)

            def project_out(b):
                pe.wait_ge(ctxt_ready, after(ctxt_ready, b + 1))
                for k in range(TPB):
                    m = pe.matmul(w0b[:, k * P:(k + 1) * P], ctxt[:, k * P:(k + 1) * P], wa[:, 3, :],
                                  start=True, stop=True)
                m.then_inc(proj_done, 1)

            for s in ahead:
                pe.sem_inc(s, 1)
            pe.sem_inc(out_stored, 16)
            pe.wait_ge(c_loaded, after(c_loaded, 32))
            modulation(0, w1b)
            modulation(1, w0b)
            pe.wait_ge(sc_step, after(sc_step, 3))
            for j in range(2):
                m = pe.matmul(psa[0][:, B * j:B * j + B], wms[:, 4 + j, :], sce[:, 3, :], start=True, stop=True)
            m.then_inc(modt_done, 1)
            pe.wait_ge(small_loaded, after(small_loaded, 96))
            pe.wait_ge(wa_loaded, after(wa_loaded, 16))
            pe.wait_ge(consts, after(consts, 3))
            pe.wait_ge(mod_ready, after(mod_ready, 4))
            transpose_x(0)
            project_qk(0, 0)
            pe.wait_ge(qk_ready, after(qk_ready, 2))
            project_v(0, 0)
            pe.wait_ge(v_ready, after(v_ready, 4))
            transpose_x(1)
            project_qk(1, 1)
            pe.wait_ge(modt_ready, after(modt_ready, 2))
            for g in range(4):
                scores_a(0, 0, g)
            pe.wait_ge(qk_ready, after(qk_ready, 4))
            transpose_m(0, 0)
            for g in range(4, 8):
                scores_a(0, 0, g)
            pe.wait_ge(mt_ready, after(mt_ready, 1))
            transpose_m(0, 1)

            def step(b, n, prep, ahead):
                def a(g):
                    if ahead:
                        scores_a(b + 1, 1 - n, g)

                scores_b(b, n, 0)
                if prep:
                    pe.wait_ge(mt_ready, after(mt_ready, 2 * (b + 1)))
                    modulation(b + 2, w1b)
                if ahead:
                    pe.wait_ge(att_ready, after(att_ready, b))
                    pe.wait_ge(qk_ready, after(qk_ready, 2 * (b + 2)))
                    project_v(b + 1, 1 - n)
                scores_b(b, n, 1)
                a(0)
                scores_b(b, n, 2)
                a(1)
                probs_v(b, n, 0)
                scores_b(b, n, 3)
                a(2)
                scores_b(b, n, 4)
                a(3)
                probs_v(b, n, 1)
                scores_b(b, n, 5)
                a(4)
                if ahead:
                    if prep:
                        pe.wait_ge(mod_ready, after(mod_ready, 2 * (b + 3)))
                    else:
                        pe.wait_ge(mt_ready, after(mt_ready, 2 * (b + 1)))
                    transpose_m(b + 1, 0)
                scores_b(b, n, 6)
                a(5)
                probs_v(b, n, 2)
                scores_b(b, n, 7)
                a(6)
                if prep:
                    pe.wait_ge(v_ready, after(v_ready, 4 * (b + 2)))
                    transpose_x(b + 2)
                a(7)
                probs_v(b, n, 3)
                if prep:
                    pe.wait_ge(mt_ready, after(mt_ready, 2 * b + 3))
                    project_qk(b + 2, n)
                    pe.wait_ge(qk_ready, after(qk_ready, 2 * (b + 3)))
                elif ahead:
                    pe.wait_ge(mt_ready, after(mt_ready, 2 * b + 3))
                    pe.wait_ge(v_ready, after(v_ready, 4 * (b + 2)))
                else:
                    pe.wait_ge(mt_ready, after(mt_ready, 2 * (b + 1)))
                    pe.wait_ge(att_ready, after(att_ready, b))
                gather_context(b)
                project_out(b)
                if ahead:
                    transpose_m(b + 1, 1)

            steps(pe, step)

            with pe.Fori(0, NG // 2) as i:
                for n in range(2):
                    g = 2 * i + n
                    pe.wait_ge(xh2_ready, after(xh2_ready, g + 1))
                    pe.wait_ge(h2t_ready, after(h2t_ready, 2 * i))
                    for k in range(GT):
                        m = pe.transpose(psa[n][:, k * P:(k + 1) * P], xh2[n][:, k, :], idf[:])
                    m.then_inc(t2_done, 1)

            pe.wait_ge(late_loaded, after(late_loaded, 144))
            pe.wait_ge(norm_step, after(norm_step, 16 * B))
            with pe.Fori(0, NG) as g:
                pe.wait_ge(h2t_ready, after(h2t_ready, g + 1))
                for c in range(FF):
                    pe.wait_ge(gelu_done, after(gelu_done, FF * g))
                    pe.matmul(bk[2 + c][:], w1s[:, c, :], h2t[:, ds(GW * g, GW)], start=True, stop=True
                              ).then_inc(w1_done, 1)
                pe.wait_ge(comb_step, after(comb_step, 3 * g))
                pe.wait_ge(att_ready, after(att_ready, B))
                for c in range(FF):
                    pe.wait_ge(gelu_done, after(gelu_done, FF * g + c + 1))
                    for k in range(GT):
                        m = pe.matmul(bk[6][:, k * P:(k + 1) * P], gt[:, c, k * P:(k + 1) * P], w2s[:, c, :],
                                      start=(c == 0 and k == 0), stop=(c == FF - 1), skip_group_check=True)
                m.then_inc(w2_done, 1)

            def router(g):
                pe.wait_ge(h3t_ready, after(h3t_ready, 2 * (g + 1)))
                for k in range(GT):
                    t = GT * g + k
                    m = pe.matmul(bk[7][:, E * t:E * t + E], h3t[:, t * P:(t + 1) * P], wrs[:], start=True, stop=True)
                m.then_inc(router_done, 1)

            for g in range(NG):
                pe.wait_ge(ln3_step, after(ln3_step, 13 * (g + 1)))
                if g >= 2:
                    pe.wait_ge(h3t_ready, after(h3t_ready, 2 * (g - 1)))
                for k in range(GT):
                    m = pe.transpose(psa[g % 2][:, k * P:(k + 1) * P], xh2[g % 2][:, k, :], idf[:])
                m.then_inc(t3_done, 1)
                if g:
                    router(g - 1)
            router(NG - 1)

            pe.wait_ge(rt_step, after(rt_step, RT_PARTS))
            wt_ps = [bk[6].bitcast(BF16), bk[7].bitcast(BF16)]
            for t in range(NT):
                m = pe.transpose(wt_ps[t // 8][0:3 * E, (t % 8) * P:(t % 8 + 1) * P],
                                 wp[:, t, :, :].rearrange("p a e -> p (a e)"), idb[:])
            m.then_inc(wt_done, 1)
            pe.wait_ge(wt_ready, after(wt_ready, 2))

            def down(g, e):
                pe.wait_ge(hh_ready, after(hh_ready, E * g + e + 1))
                if e == 0:
                    pe.wait_ge(fin_step, after(fin_step, 2 * g))
                for k in range(GT):
                    m = pe.matmul(bk[6][:, k * P:(k + 1) * P], hh[e % 2][:, k * P:(k + 1) * P], wds[:, e, :],
                                  start=(e == 0 and k == 0), stop=(e == E - 1), skip_group_check=True)
                m.then_inc(down_done, 1)

            with pe.Fori(0, NG) as g:
                for e in range(E):
                    tokens = h3t[:, ds(GW * g, GW)]
                    pe.wait_ge(silu_done, after(silu_done, E * g + e - 1)) if e else pe.wait_ge(silu_done, after(silu_done, E * g))
                    pe.matmul(bk[e % 2][:], wgs[:, e, :], tokens, start=True, stop=True).then_inc(gate_done, 1)
                    pe.wait_ge(hh_ready, after(hh_ready, E * g + e - 1)) if e else pe.wait_ge(hh_ready, after(hh_ready, E * g))
                    apart(pe)
                    pe.matmul(bk[4 + e % 2][:], selwb[:, e, :], wt[:, ds(GW * g, GW)], start=True, stop=True
                              ).then_inc(wb_done, 1)
                    pe.matmul(bk[2 + e % 2][:], wus[:, e, :], tokens, start=True, stop=True).then_inc(up_done, 1)
                    if e:
                        down(g, e - 1)
                down(g, E - 1)

        @block.scalar
        def _(act):
            def copy_mod(b, bank):
                act.wait_ge(mod_done, after(mod_done, b + 1))
                act.activation(modb[:, ds(b, 1), CA, :], bank[:, 0:D], ACT.Identity, bias=1.0).then_inc(mod_ready, 1)
                act.activation(modb[:, ds(b, 1), SA:, :], bank[:, D:4 * D], ACT.Copy).then_inc(mod_ready, 1)

            def copy_xt(b, n):
                act.wait_ge(xt_done, after(xt_done, b + 1))
                act.wait_ge(qk_done, after(qk_done, b - 1))
                act.activation(x1t[n][:, PAD:PAD + S], w0b[:, 0:S], ACT.Identity, bias=col[:, LN1B:LN1B + 1],
                               scale=col[:, LN1G:LN1G + 1]).then_inc(x1t_ready, 1)
                ends = w0b[:, 0:2 * (S - PAD)].rearrange("p (a c) -> p a c", a=2)[:, :, 0:PAD]
                pads = x1t[n][:].rearrange("p (a c) -> p a c", a=2)
                act.activation(pads[:, 0, 0:PAD], ends[:, 0, :], ACT.Identity, bias=col[:, LN1B:LN1B + 1],
                               scale=col[:, LN1G:LN1G + 1])
                act.activation(pads[:, 1, LINE // 2 - PAD:], ends[:, 1, :], ACT.Identity,
                               bias=col[:, LN1B:LN1B + 1], scale=col[:, LN1G:LN1G + 1]).then_inc(x1t_ready, 1)

            def copy_qk(b):
                act.wait_ge(qk_done, after(qk_done, b + 1))
                act.wait_ge(parts_step, after(parts_step, 4 * b))
                act.activation(qk[:, 0, :], w0b[:, 0:LINE], ACT.Identity, bias=bqs[:], scale=SCALE
                               ).then_inc(qk_ready, 1)
                act.activation(qk[:, 1, :], w1b[:, 0:LINE], ACT.Identity, bias=col[:, BK:BK + 1]
                               ).then_inc(qk_ready, 1)

            def copy_v(b, n):
                act.wait_ge(v_done, after(v_done, b + 1))
                act.wait_ge(pv_done, after(pv_done, 4 * (b - 1)))
                for eo in range(2):
                    for half in range(2):
                        p = slice(WIN * half, WIN * half + WIN)
                        src = w0b[p, 2 * P * eo:2 * P * (eo + 1)].rearrange("p (s h d) -> p s h d", s=2, d=HD)
                        dst = vb[n][p, eo, :, :, half, 0:HD].rearrange("p h s d -> p s h d")
                        act.activation(dst, src, ACT.Copy).then_inc(v_ready, 1)

            def exp(b, n, g):
                act.wait_ge(b_done, after(b_done, 8 * b + g + 1))
                if g >= 2:
                    act.wait_ge(pv_done, after(pv_done, 4 * b + g // 2 - 1))
                act.activation(prob[g // 2 % 2][:, :, g % 2, :], psb[g % 2][:].rearrange("p (h q) -> p h q", h=H2),
                               ACT.Exp).then_inc(exp_done, 1)

            act.wait_ge(c_loaded, after(c_loaded, 32))
            act.activation(sce[:, 0, :], cts[:], ACT.Exp, scale=-1.0).then_inc(sc_exp, 1)
            copy_mod(0, w1b)
            copy_mod(1, w0b)
            act.wait_ge(modt_done, after(modt_done, 1))
            act.activation(modt[:, 0, :], psa[0][:, 0:B], ACT.Copy).then_inc(modt_ready, 1)
            act.activation(modt[:, 1, :], psa[0][:, B:2 * B], ACT.Identity, bias=1.0).then_inc(modt_ready, 1)
            act.wait_ge(small_loaded, after(small_loaded, 96))
            act.wait_ge(consts, after(consts, 11))
            act.wait_ge(consts_pool, after(consts_pool, 5))
            copy_xt(0, 0)
            copy_qk(0)
            copy_v(0, 0)
            copy_xt(1, 1)
            copy_qk(1)

            def step(b, n, prep, ahead):
                exp(b, n, 0)
                if prep:
                    copy_mod(b + 2, w1b)
                if ahead:
                    copy_v(b + 1, 1 - n)
                for g in range(1, 8):
                    exp(b, n, g)
                if prep:
                    copy_xt(b + 2, n)
                    copy_qk(b + 2)
                act.wait_ge(ctx_done, after(ctx_done, b + 1))
                act.wait_ge(proj_done, after(proj_done, b))
                act.activation(ctxt[:], w1b[:, PAD:PAD + S], ACT.Identity, bias=col[:, BV:BV + 1]
                               ).then_inc(ctxt_ready, 1)

            steps(act, step)

            act.wait_ge(gate_step, after(gate_step, 4))
            with act.Fori(0, NG // 2) as i:
                for n in range(2):
                    g = 2 * i + n
                    act.wait_ge(t2_done, after(t2_done, g + 1))
                    act.activation(h2t[:, ds(GW * g, GW)], psa[n][:], ACT.Identity, bias=col[:, LN2B:LN2B + 1],
                                   scale=col[:, LN2G:LN2G + 1]).then_inc(h2t_ready, 1)

            with act.Fori(0, NG) as g:
                act.wait_ge(w2_done, after(w2_done, g))
                for c in range(FF):
                    act.wait_ge(w1_done, after(w1_done, FF * g + c + 1))
                    act.activation(gt[:, c, :], bk[2 + c][:], ACT.Gelu, bias=col[:, B1 + c:B1 + c + 1]
                                   ).then_inc(gelu_done, 1)

            for g in range(NG):
                act.wait_ge(t3_done, after(t3_done, g + 1))
                for j in range(2):
                    b = 2 * g + j
                    act.activation(h3t[:, S * b:S * (b + 1)], psa[g % 2][:, S * j:S * (j + 1)], ACT.Identity,
                                   bias=modt[:, 0, b:b + 1], scale=modt[:, 1, b:b + 1]).then_inc(h3t_ready, 1)

            act.wait_ge(rt_step, after(rt_step, 1))
            act.activation(rt[1][:], rt[0][:], ACT.Exp, scale=-1.0).then_inc(rt_exp, 1)
            act.wait_ge(rt_step, after(rt_step, RT_DIST))
            act.activation(rt[2][:], rt[0][:], ACT.Exp, scale=-1.0 / 0.1).then_inc(rt_exp, 1)
            act.activation(rt[3][:], rt[0][:], ACT.Exp, scale=-1.0 / 0.3).then_inc(rt_exp, 1)

            with act.Fori(0, NG) as g:
                for e in range(E):
                    act.wait_ge(gate_done, after(gate_done, E * g + e + 1))
                    act.wait_ge(sw_done, after(sw_done, E * g + e - 1)) if e else act.wait_ge(sw_done, after(sw_done, E * g))
                    act.activation(sg[e % 2][:], bk[e % 2][:], ACT.Silu).then_inc(silu_done, 1)

        @block.gpsimd
        def _(pool):
            def root(dst, src, n, s):
                pool.tensor_tensor(dst, src, mhalf[:, 0:n], ALU.pow).then_inc(s, 1)

            def two(ap):
                return ap.rearrange("p (o d) -> p o d", o=1).broadcast_to([P, TPB, D])

            def norm_x(b):
                pool.wait_ge(ln_dve, after(ln_dve, 14 * b + 5))
                root(rs[:, 0:TPB], ve[:, 0:TPB], TPB, ln_pool)
                pool.wait_ge(ln_dve, after(ln_dve, 14 * b + 7))
                pool.wait_ge(mod_ready, after(mod_ready, 2 * (b + 1)))
                pool.tensor_tensor(h1[:], xh[:], modb[:, ds(b, 1), CA, :].broadcast_to([P, TPB, D]), ALU.mult
                                   ).then_inc(ln_pool, 1)
                pool.wait_ge(ln_pool, after(ln_pool, 5 * b + 2))
                pool.tensor_tensor(h1[:], h1[:], modb[:, ds(b, 1), SA, :].broadcast_to([P, TPB, D]), ALU.add
                                   ).then_inc(ln_pool, 1)
                pool.wait_ge(ln_pool, after(ln_pool, 5 * b + 3))
                pool.tensor_tensor(res[:, ds(TPB * b, TPB), :], h1[:], two(row[:, 0, :]), ALU.add
                                   ).then_inc(ln_pool, 1)
                pool.wait_ge(ln_dve, after(ln_dve, 14 * b + 12))
                root(rs[:, 0:TPB], ve[:, 0:TPB], TPB, ln_pool)

            def copy_x1v(b, n):
                pool.wait_ge(x1t_ready, after(x1t_ready, 2 * (b + 1)))
                pool.wait_ge(v_done, after(v_done, b - 1))
                apart(pool)
                pool.tensor_copy(x1v[n][:, PAD:PAD + S], x1t[n][:, PAD:PAD + S]).then_inc(x1v_ready, 1)

            def cut_m(b, hf):
                pool.wait_ge(max_done, after(max_done, 8 * b + 4 * hf + 4))
                pool.wait_ge(mt_done, after(mt_done, 2 * b + hf))
                apart(pool)
                src = nm[:, 4 * hf:4 * hf + 4, :].rearrange("p g h -> p (g h)")
                pool.tensor_copy(mp[:, 0, :], src).then_inc(mp_step, 1)
                pool.wait_ge(mp_step, after(mp_step, 4 * b + 2 * hf + 1))
                pool.tensor_tensor(mp[:, 1, :], src, mp[:, 0, :], ALU.subtract).then_inc(mp_step, 1)

            pool.memset(mhalf[:], -0.5).then_inc(consts_pool, 1)
            pool.memset(x1v[0][:], 0.0).then_inc(consts_pool, 1)
            pool.memset(x1v[1][:], 0.0).then_inc(consts_pool, 1)
            pool.memset(vb[0][:], 0.0).then_inc(consts_pool, 1)
            pool.memset(vb[1][:], 0.0).then_inc(consts_pool, 1)
            pool.wait_ge(consts_pool, after(consts_pool, 5))
            pool.wait_ge(small_loaded, after(small_loaded, 96))
            norm_x(0)
            norm_x(1)
            copy_x1v(0, 0)
            copy_x1v(1, 1)
            cut_m(0, 0)
            cut_m(0, 1)

            def step(b, n, prep, ahead):
                if prep:
                    norm_x(b + 2)
                if ahead:
                    cut_m(b + 1, 0)
                    cut_m(b + 1, 1)
                if prep:
                    copy_x1v(b + 2, n)
                pool.wait_ge(ln2_step, after(ln2_step, 6 * (b + 1)))
                pool.tensor_tensor(rs2[:, ds(TPB * b, TPB)], ve2[:, ds(TPB * b, TPB)], mhalf[:, 0:TPB], ALU.pow
                                   ).then_inc(ln2_root, 1)

            steps(pool, step)

            pool.wait_ge(att_ready, after(att_ready, B))
            with pool.Fori(0, NG) as g:
                pool.wait_ge(comb_step, after(comb_step, 3 * g))
                pool.tensor_tensor(resb[:], res[:, ds(GT * g, GT), :],
                                   row[:, 1:2, :].broadcast_to([P, GT, D]), ALU.add).then_inc(resb_ready, 1)
                pool.wait_ge(ln3_step, after(ln3_step, 13 * g + 9))
                root(rs[:, 0:GT], ve[:, 0:GT], GT, ln3_root)

        @block.vector
        def _(dve):
            def stats(src_of, s, base, n, st_, mv_, ve_):
                apart(dve)
                for k in range(n):
                    dve.bn_stats(st_[:, k, :], src_of(k)).then_inc(s, 1)
                dve.wait_ge(s, after(s, base + n))
                apart(dve)
                for k in range(n):
                    dve.bn_aggr(mv_[:, k, :], st_[:, k, :]).then_inc(s, 1)
                dve.wait_ge(s, after(s, base + 2 * n))
                dve.tensor_scalar(ve_, mv_[:, 0:n, 1], EPS, None, ALU.add).then_inc(s, 1)

            def standard(dst, src, mean, r):
                return dve.tensor_scalar(dst, src, mean, r, ALU.subtract, ALU.mult)

            def ln_a(b):
                stats(lambda k: xs[:, ds(TPB * b + k, 1), :], ln_dve, 14 * b, TPB, st, mv, ve[:, 0:TPB])

            def ln_b(b):
                dve.wait_ge(ln_pool, after(ln_pool, 5 * b + 1))
                for k in range(TPB):
                    standard(xh[:, k, :], xs[:, ds(TPB * b + k, 1), :], mv[:, k, 0:1], rs[:, k:k + 1]
                             ).then_inc(ln_dve, 1)

            def ln_c(b):
                dve.wait_ge(ln_dve, after(ln_dve, 14 * b + 7))
                dve.wait_ge(ln_pool, after(ln_pool, 5 * b + 3))
                stats(lambda k: h1[:, k, :], ln_dve, 14 * b + 7, TPB, st, mv, ve[:, 0:TPB])

            def ln_d(b):
                dve.wait_ge(ln_pool, after(ln_pool, 5 * b + 5))
                dve.wait_ge(xt_done, after(xt_done, b))
                for k in range(TPB):
                    standard(x1h[:, k, :], h1[:, k, :], mv[:, k, 0:1], rs[:, k:k + 1]).then_inc(ln_dve, 1)

            def spread_sc(b):
                dve.wait_ge(mod_done, after(mod_done, b))
                dve.tensor_copy(scb[:], sce[:, 3, ds(b, 1)].broadcast_to([P, P])).then_inc(scb_ready, 1)

            def cut_qk(b):
                dve.wait_ge(qk_ready, after(qk_ready, 2 * (b + 1)))
                dve.wait_ge(scr_written, after(scr_written, 96 * b))
                dve.tensor_copy(parts[:, 0], qk[:]).then_inc(parts_step, 1)
                dve.wait_ge(parts_step, after(parts_step, 4 * b + 1))
                dve.tensor_tensor(qkr[:], qk[:], parts[:, 0], ALU.subtract).then_inc(parts_step, 1)
                dve.wait_ge(parts_step, after(parts_step, 4 * b + 2))
                dve.tensor_copy(parts[:, 1], qkr[:]).then_inc(parts_step, 1)
                dve.wait_ge(parts_step, after(parts_step, 4 * b + 3))
                dve.tensor_tensor(parts[:, 2], qkr[:], parts[:, 1], ALU.subtract).then_inc(parts_step, 1)

            def maxima(b, g):
                dve.wait_ge(a_done, after(a_done, 8 * b + g + 1))
                dve.wait_ge(mp_step, after(mp_step, 4 * (b - 1) + 2 * (g // 4) + 2))
                dve.tensor_reduce(nm[:, g, :], psa[g % 2][:].rearrange("p (h k) -> p h k", h=H2), AX_X, ALU.max,
                                  negate=True).then_inc(max_done, 1)

            def copy_mt(b, hf):
                dve.wait_ge(mt_done, after(mt_done, 2 * b + hf + 1))
                dve.wait_ge(mrow_ready, after(mrow_ready, 64 * (2 * b + hf)))
                dve.tensor_copy(mt[:], w1b[0:64, 0:64].bitcast(BF16)).then_inc(mt_ready, 1)

            def normalise(b, gp):
                dve.wait_ge(pv_done, after(pv_done, 4 * b + gp + 1))
                eo, par = gp // 2, gp % 2
                base = 16 * b + 4 * gp
                sums = psv[gp % 2][:, 0:4 * VC * H2].rearrange("p (h w v) -> p h w v", h=H2, v=VC)
                dve.wait_ge(norm_step, after(norm_step, base))
                dve.reciprocal(rsum[:], sums[:, :, :, HD]).then_inc(norm_step, 1)
                dve.wait_ge(norm_step, after(norm_step, base + 1))
                dve.tensor_tensor(fac[:], rsum[:], alph[:, eo:eo + 1, :].broadcast_to([P, H2, 4]), ALU.mult
                                  ).then_inc(norm_step, 1)
                dve.wait_ge(norm_step, after(norm_step, base + 2))
                dve.wait_ge(ctx_done, after(ctx_done, b))
                for sel in range(2):
                    p = slice(WIN * sel, WIN * sel + WIN)
                    dst = ctxn[p, eo, :, WIN * par:WIN * par + WIN].rearrange("p f (h d) -> p f h d", d=HD)
                    src = sums[p, :, 2 * sel:2 * sel + 2, 0:HD].rearrange("p h f d -> p f h d")
                    f = fac[p, :, 2 * sel:2 * sel + 2].rearrange("p h (f o) -> p f h o", o=1)
                    dve.tensor_tensor(dst, src, f.broadcast_to([WIN, 2, H2, HD]), ALU.mult
                                      ).then_inc(norm_step, 1)

            def attention_out(b):
                dve.wait_ge(proj_done, after(proj_done, b + 1))
                dve.wait_ge(ln_pool, after(ln_pool, 5 * b + 4))
                tiles = res[:, ds(TPB * b, TPB), :]
                dve.tensor_tensor(tiles, w0b[:, 0:S].rearrange("p (k d) -> p k d", k=TPB), tiles, ALU.add
                                  ).then_inc(att_ready, 1)

            def ln2(b):
                dve.wait_ge(att_ready, after(att_ready, b + 1))
                dve.wait_ge(ln2_step, after(ln2_step, 6 * b))
                stats(lambda k: res[:, ds(TPB * b + k, 1), :], ln2_step, 6 * b, TPB, st2, mv2,
                      ve2[:, ds(TPB * b, TPB)])
                dve.tensor_copy(mean2[:, ds(TPB * b, TPB)], mv2[:, :, 0]).then_inc(ln2_step, 1)

            dve.wait_ge(sc_exp, after(sc_exp, 1))
            dve.tensor_scalar(sce[:, 1, :], sce[:, 0, :], 1.0, None, ALU.add).then_inc(sc_step, 1)
            dve.wait_ge(sc_step, after(sc_step, 1))
            dve.reciprocal(sce[:, 2, :], sce[:, 1, :]).then_inc(sc_step, 1)
            dve.wait_ge(sc_step, after(sc_step, 2))
            dve.tensor_tensor(sce[:, 3, :], sce[:, 2, :], cts[:], ALU.mult).then_inc(sc_step, 1)
            dve.wait_ge(sc_step, after(sc_step, 3))
            spread_sc(0)
            dve.wait_ge(x_first, after(x_first, 16))
            ln_a(0)
            spread_sc(1)
            dve.wait_ge(consts_pool, after(consts_pool, 1))
            ln_b(0)
            dve.wait_ge(small_loaded, after(small_loaded, 96))
            dve.tensor_copy(idb[:], idf[:]).then_inc(consts, 1)
            dve.tensor_copy(monesb[:], monesf[:]).then_inc(consts, 1)
            dve.tensor_scalar(bqs[:], col[:, BQ:BQ + 1], SCALE, None, ALU.mult).then_inc(consts, 1)
            ln_c(0)
            dve.wait_ge(consts_pool, after(consts_pool, 5))
            for n in range(2):
                for half in range(2):
                    p = slice(WIN * half, WIN * half + WIN)
                    for sel in range(2):
                        dve.tensor_copy(vb[n][p, :, :, sel, half, HD],
                                        vmsk[p, :, sel:sel + 1].broadcast_to([WIN, 2, NH])).then_inc(consts, 1)
            ln_d(0)
            dve.wait_ge(x_rest, after(x_rest, 16))
            ln_a(1)
            ln_b(1)
            ln_c(1)
            cut_qk(0)
            ln_d(1)
            cut_qk(1)
            for g in range(4):
                maxima(0, g)
            copy_mt(0, 0)
            for g in range(4, 8):
                maxima(0, g)
            copy_mt(0, 1)

            def step(b, n, prep, ahead):
                if prep:
                    spread_sc(b + 2)
                    ln_a(b + 2)
                if ahead:
                    maxima(b + 1, 0)
                    maxima(b + 1, 1)
                normalise(b, 0)
                if prep:
                    ln_b(b + 2)
                if ahead:
                    maxima(b + 1, 2)
                    maxima(b + 1, 3)
                normalise(b, 1)
                if prep:
                    ln_c(b + 2)
                if ahead:
                    maxima(b + 1, 4)
                    copy_mt(b + 1, 0)
                    maxima(b + 1, 5)
                normalise(b, 2)
                if prep:
                    ln_d(b + 2)
                if ahead:
                    maxima(b + 1, 6)
                    maxima(b + 1, 7)
                normalise(b, 3)
                if prep:
                    cut_qk(b + 2)
                attention_out(b)
                ln2(b)
                if ahead:
                    copy_mt(b + 1, 1)

            steps(dve, step)

            g_v = modb[:, :, GA:, :]
            sign, size = (t[:].rearrange("p (b c d) -> p b c d", b=B, c=2) for t in (h2t, h3t))
            dve.wait_ge(mod_ready, after(mod_ready, 2 * B))
            dve.tensor_scalar(sign, g_v, 0.0, 2.0, ALU.is_ge, ALU.mult).then_inc(gate_step, 1)
            dve.scalar_tensor_tensor(out=size, in0=g_v, scalar=-1.0, in1=g_v, op0=ALU.mult, op1=ALU.max
                                     ).then_inc(gate_step, 1)
            dve.wait_ge(gate_step, after(gate_step, 2))
            dve.tensor_scalar(size, size, 0.25, None, ALU.max).then_inc(gate_step, 1)
            dve.wait_ge(gate_step, after(gate_step, 3))
            dve.scalar_tensor_tensor(out=g_v, in0=sign, scalar=1.0, in1=size, op0=ALU.subtract, op1=ALU.mult
                                     ).then_inc(gate_step, 1)
            dve.wait_ge(ln2_root, after(ln2_root, B))
            with dve.Fori(0, NG // 2) as i:
                for n in range(2):
                    g = 2 * i + n
                    dve.wait_ge(t2_done, after(t2_done, 2 * i))
                    for k in range(GT):
                        t = GT * g + k
                        m = standard(xh2[n][:, k, :], res[:, ds(t, 1), :], mean2[:, ds(t, 1)], rs2[:, ds(t, 1)])
                    m.then_inc(xh2_ready, 1)

            dve.wait_ge(t2_done, after(t2_done, NG))
            dve.wait_ge(gate_step, after(gate_step, 4))
            with dve.Fori(0, NG // 2) as i:
                for n in range(2):
                    g = 2 * i + n
                    dve.wait_ge(w2_done, after(w2_done, g + 1))
                    dve.wait_ge(resb_ready, after(resb_ready, g + 1))
                    tiles = xs[:, ds(GT * g, GT), :]
                    dve.tensor_tensor(comb[:], bk[6][:].rearrange("p (k d) -> p k d", k=GT), resb[:], ALU.add
                                      ).then_inc(comb_step, 1)
                    dve.wait_ge(comb_step, after(comb_step, 3 * g + 1))
                    ga = modb[:, ds(2 * g, 2), GA:GA + 1, :].broadcast_to([P, 2, TPB, D])
                    comb_v = comb[:].rearrange("p (b k) d -> p b k d", b=2)
                    dve.tensor_tensor(comb_v, comb_v, ga, ALU.mult).then_inc(comb_step, 1)
                    dve.wait_ge(comb_step, after(comb_step, 3 * g + 2))
                    dve.tensor_tensor(tiles, tiles, comb[:], ALU.add).then_inc(comb_step, 1)
                    dve.wait_ge(comb_step, after(comb_step, 3 * g + 3))
                    stats(lambda k: xs[:, ds(GT * g + k, 1), :], ln3_step, 13 * g, GT, st, mv, ve[:, 0:GT])
                    dve.wait_ge(ln3_root, after(ln3_root, g + 1))
                    dve.wait_ge(t3_done, after(t3_done, 2 * i))
                    for k in range(GT):
                        standard(xh2[n][:, k, :], xs[:, ds(GT * g + k, 1), :], mv[:, k, 0:1], rs[:, k:k + 1]
                                 ).then_inc(ln3_step, 1)

            did = [0]

            def link(ins):
                did[0] += 1
                ins.then_inc(rt_step, 1)
                dve.wait_ge(rt_step, after(rt_step, did[0]))

            lo_e = [P, NT, E]

            def per_token(t):
                return t[:].rearrange("p (t o) -> p t o", o=1).broadcast_to(lo_e)

            z, ex, wz, fb, mask = rt
            dve.wait_ge(late_loaded, after(late_loaded, 144))
            dve.tensor_copy(selwb[:], selwf[:]).then_inc(consts, 1)
            dve.reciprocal(rtemp[:], temps[:]).then_inc(consts, 1)
            dve.wait_ge(consts, after(consts, 13))
            dve.wait_ge(router_done, after(router_done, NG))
            logits = bk[7][:, 0:NT * E].rearrange("p (t e) -> p t e", e=E)
            link(dve.tensor_scalar(z[:], logits, rtemp[:], None, ALU.mult))
            dve.wait_ge(rt_exp, after(rt_exp, 1))
            link(dve.tensor_scalar(ex[:], ex[:], 1.0, None, ALU.add))
            link(dve.reciprocal(mask[:], ex[:]))
            link(dve.tensor_scalar(ex[:], mask[:], ZONE_LOW, None, ALU.is_ge))
            link(dve.tensor_scalar(wz[:], mask[:], ZONE_MID, None, ALU.subtract))
            link(dve.scalar_tensor_tensor(out=z[:], in0=wz[:], scalar=-1.0, in1=wz[:], op0=ALU.mult,
                                          op1=ALU.max))
            assert did[0] == RT_DIST
            link(dve.scalar_tensor_tensor(out=ex[:], in0=mask[:], scalar=ZONE_HIGH, in1=ex[:],
                                          op0=ALU.is_le, op1=ALU.mult))
            dve.wait_ge(rt_exp, after(rt_exp, 3))
            link(dve.tensor_tensor(wz[:], wz[:], ex[:], ALU.mult))
            link(dve.tensor_reduce(rsm[0][:], wz[:], AX_X, ALU.add))
            lo_f = [P, NT, E, E]
            fb_e = fb[:].rearrange("p t (e o) -> p t e o", o=1).broadcast_to(lo_f)
            fb_f = fb[:].rearrange("p t (o f) -> p t o f", o=1).broadcast_to(lo_f)
            link(dve.tensor_tensor(rc[0][:], fb_f, fb_e, ALU.is_gt))
            link(dve.tensor_tensor(rc[1][:], fb_f, fb_e, ALU.is_equal))
            link(dve.tensor_tensor(rc[1][:], rc[1][:], earl[:].rearrange("p (o e) f -> p o e f", o=1)
                                   .broadcast_to(lo_f), ALU.mult))
            link(dve.tensor_tensor(rc[0][:], rc[0][:], rc[1][:], ALU.add))
            link(dve.tensor_reduce(mask[:], rc[0][:], AX_X, ALU.add))
            link(dve.scalar_tensor_tensor(out=fb[:], in0=mask[:], scalar=1.5, in1=fb[:], op0=ALU.is_lt,
                                          op1=ALU.mult))
            link(dve.tensor_reduce(rsm[1][:], fb[:], AX_X, ALU.add))
            link(dve.tensor_scalar(rsm[1][:], rsm[1][:], 1e-8, None, ALU.max))
            link(dve.reciprocal(rsm[2][:], rsm[1][:]))
            link(dve.tensor_tensor(fb[:], fb[:], per_token(rsm[2]), ALU.mult))
            link(dve.tensor_scalar(rsm[1][:], rsm[0][:], 1e-8, None, ALU.is_lt))
            link(dve.tensor_scalar(rsm[2][:], rsm[0][:], 1e-8, None, ALU.is_ge))
            link(dve.tensor_tensor(fb[:], fb[:], per_token(rsm[1]), ALU.mult))
            link(dve.tensor_tensor(wz[:], wz[:], per_token(rsm[2]), ALU.mult))
            link(dve.tensor_tensor(wz[:], wz[:], fb[:], ALU.add))
            link(dve.tensor_reduce(rsm[0][:], wz[:], AX_X, ALU.add))
            link(dve.tensor_scalar(rsm[0][:], rsm[0][:], 1e-8, None, ALU.max))
            link(dve.reciprocal(rsm[1][:], rsm[0][:]))
            link(dve.tensor_tensor(wz[:], wz[:], per_token(rsm[1]), ALU.mult))
            link(dve.tensor_copy(wp[:, :, 0, :], wz[:]))
            link(dve.tensor_tensor(fb[:], wz[:], wp[:, :, 0, :], ALU.subtract))
            link(dve.tensor_copy(wp[:, :, 1, :], fb[:]))
            link(dve.tensor_tensor(wp[:, :, 2, :], fb[:], wp[:, :, 1, :], ALU.subtract))
            assert did[0] == RT_PARTS, did[0]
            dve.wait_ge(wt_done, after(wt_done, 1))
            for j in range(2):
                dve.tensor_copy(wt[:, 8 * P * j:8 * P * (j + 1)], bk[6 + j][0:3 * E, :].bitcast(BF16)
                                ).then_inc(wt_ready, 1)

            def weigh(g, e):
                dve.wait_ge(silu_done, after(silu_done, E * g + e + 1))
                dve.wait_ge(wb_done, after(wb_done, E * g + e + 1))
                dve.wait_ge(hh_ready, after(hh_ready, E * g + e))
                dve.tensor_tensor(sw[:], sg[e % 2][:], bk[4 + e % 2][:], ALU.mult).then_inc(sw_done, 1)
                dve.wait_ge(sw_done, after(sw_done, E * g + e + 1))
                dve.wait_ge(up_done, after(up_done, E * g + e + 1))
                dve.wait_ge(down_done, after(down_done, E * g + e - 1)) if e else dve.wait_ge(down_done, after(down_done, E * g))
                dve.tensor_tensor(hh[e % 2][:], sw[:], bk[2 + e % 2][:], ALU.mult).then_inc(hh_ready, 1)

            with dve.Fori(0, NG // 2) as i:
                for n in range(2):
                    g = 2 * i + n
                    for e in range(E):
                        weigh(g, e)
                    dve.wait_ge(down_done, after(down_done, E * g + E))
                    dve.wait_ge(out_stored, after(out_stored, 16 * 2 * i))
                    gb = modb[:, ds(2 * g, 2), GB:GB + 1, :].broadcast_to([P, 2, TPB, D])
                    fin_v = fin[n][:].rearrange("p (b k) d -> p b k d", b=2)
                    dve.tensor_tensor(fin_v, bk[6][:].rearrange("p (b k d) -> p b k d", b=2, k=TPB), gb, ALU.mult
                                      ).then_inc(fin_step, 1)
                    dve.wait_ge(fin_step, after(fin_step, 2 * g + 1))
                    dve.tensor_tensor(fin[n][:], fin[n][:], xs[:, ds(GT * g, GT), :], ALU.add
                                      ).then_inc(fin_step, 1)


RT_DIST = 6
RT_PARTS = 32


def kernel(**inputs):
    import numpy as np
    import concourse.bacc as bacc
    from concourse.bass_utils import run_bass_kernel_spmd

    a = {k.removeprefix("L0_").removeprefix("attn_").removeprefix("ffn_"): np.asarray(v)
         for k, v in inputs.items()}
    ramp = np.linspace(0.0, 1.0, WIN // 2, dtype=np.float32)
    alpha = np.ones((2, WIN, 2, 2, 2), np.float32)
    vmask = np.ones((P, 2, 2), np.float32)
    for sel in range(2):
        for eo in range(2):
            for half in range(2):
                w = 4 * sel + 2 * half + eo
                if w > 0:
                    alpha[:, :WIN // 2, eo, sel, half] = ramp
                if w < B - 1:
                    alpha[:, WIN // 2:, eo, sel, half] = 1 - ramp
    vmask[:PAD, 0, 0] = 0
    vmask[P - PAD:, 1, 1] = 0
    mones = np.zeros((2, 2, P), np.float32)
    mones[:, 0, :WIN] = 1
    mones[:, 1, WIN:] = 1
    selw = np.zeros((3, E, E, P), np.float32)
    for e in range(E):
        selw[:, e, e, :] = 1
    wmod = a["wmod"].reshape(D, 6, D)[:, [1, 0, 2, 5, 3, 4], :].reshape(D, 6 * D)
    arrays = {
        "x": a["hidden_states"],
        "wqkvp": np.concatenate([a["wq"], a["wk"], a["wv"], a["wproj"]], axis=1),
        "w1": a["w1"], "w2": a["w2"], "wg": a["Wg"], "wu": a["Wu"], "wd": a["Wd"], "wr": a["Wr"],
        "temp": a["temperature"],
        "c_t": a["c"].T, "wmod": wmod,
        "cols": np.stack([a["ln1_g"], a["ln1_b"], a["bq"], a["bk"], a["bv"], a["ln2_g"], a["ln2_b"],
                          *a["b1"].reshape(FF, P)], axis=1),
        "rows": np.concatenate([a["bproj"], a["b2"]])[None],
        "ident": np.eye(P, dtype=np.float32),
        "alpha": alpha.reshape(P, 2, 4),
        "vmask": vmask,
        "mones": mones.reshape(4, P),
        "selw": selw.reshape(3 * E, E, P),
        "earlier": np.tril(np.ones((E, E), np.float32), -1)[None],
    }
    arrays = {f"in_{k}": np.ascontiguousarray(v) for k, v in arrays.items()}
    nc = bacc.Bacc("TRN2", target_bir_lowering=False, num_devices=1)
    args = [nc.dram_tensor(k, v.shape, mybir.dt.from_np(v.dtype), kind="ExternalInput").ap()
            for k, v in arrays.items()]
    args.append(nc.dram_tensor("out_x", (B, S, D), F32, kind="ExternalOutput").ap())
    build(nc, *args)
    return run_bass_kernel_spmd(nc, [arrays], core_ids=[0]).results[0]["out_x"]
```

```python
from contextlib import ExitStack

import concourse.bass as bass
from concourse import mybir
from concourse.alu_op_type import AluOpType as ALU

F32 = mybir.dt.float32
BF16 = mybir.dt.bfloat16
ACT = mybir.ActivationFunctionType
AX_X = mybir.AxisListType.X

P = 128
B, S, D = 8, 256, 128
TPB = S // P
NT = B * TPB
NH, HD = 16, 8
H2 = NH // 2
WIN = 64
PAD = WIN // 4
LINE = S + 2 * PAD
TERMS = 6
ROWS = HD * TERMS
VC = 2 * HD
FF = 4
E = 8
GT = 4
NG = NT // GT
GW = GT * P
EPS = 1e-5
SCALE = float(HD) ** -0.5
CA, SA, GA, GB = range(4)
LN1G, LN1B, BQ, BK, BV, LN2G, LN2B, B1 = range(8)
ZONE_MID = 0.36787944117144233
ZONE_LOW = 0.21231792754821915
ZONE_HIGH = 0.5


def build(nc, x, wqkvp, w1, w2, wg, wu, wd, wr, temp, c_t, wmod, cols, rows, ident, alpha, vmask,
          mones, selw, earlier, out):
    ctx = ExitStack()

    def sb(name, shape, dt=F32):
        return ctx.enter_context(nc.sbuf_tensor(name, shape, dt))

    def sem(name):
        return ctx.enter_context(nc.semaphore(name))

    ahead_by = {}

    def counts_from(s, n):
        ahead_by[s.name] = n
        return s

    def after(s, n):
        return (max(n, 0) if isinstance(n, int) else n) + ahead_by.get(s.name, 0)

    def apart(eng):
        eng.sem_inc(waits_met, 1)

    def ds(i, n):
        return slice(i, i + n) if isinstance(i, int) else bass.ds(i, n)

    with ctx:
        wa = sb("wa", [P, 4, D])
        w1s = sb("w1s", [P, FF, P])
        w2s = sb("w2s", [P, FF, D])
        wgs = sb("wgs", [P, E, P])
        wus = sb("wus", [P, E, P])
        wds = sb("wds", [P, E, D])
        wrs = sb("wrs", [P, E])
        temps = sb("temps", [P, 1])
        rtemp = sb("rtemp", [P, 1])
        cts = sb("cts", [P, B])
        wms = sb("wms", [P, 6, D])
        col = sb("col", [P, 7 + FF])
        row = sb("row", [P, 2, D])
        idf = sb("idf", [P, P])
        idb = sb("idb", [P, P], BF16)
        alph = sb("alph", [P, 2, 4])
        vmsk = sb("vmsk", [P, 2, 2])
        monesf = sb("monesf", [4, P])
        monesb = sb("monesb", [4, P], BF16)
        selwf = sb("selwf", [3 * E, E, P])
        selwb = sb("selwb", [3 * E, E, P], BF16)
        earl = sb("earl", [P, E, E])
        bqs = sb("bqs", [P, 1])
        mhalf = sb("mhalf", [P, NT])
        sce = sb("sce", [P, 4, B])
        scb = sb("scb", [P, B, P])
        modb = sb("modb", [P, B, 4, D])
        modt = sb("modt", [P, 2, B])
        xs = sb("xs", [P, NT, D])
        res = sb("res", [P, NT, D])
        st = sb("st", [P, GT, 6])
        mv = sb("mv", [P, GT, 2])
        ve = sb("ve", [P, GT])
        rs = sb("rs", [P, GT])
        xh = sb("xh", [P, TPB, D])
        h1 = sb("h1", [P, TPB, D])
        x1h = sb("x1h", [P, TPB, D])
        st2 = sb("st2", [P, TPB, 6])
        mv2 = sb("mv2", [P, TPB, 2])
        mean2 = sb("mean2", [P, NT])
        ve2 = sb("ve2", [P, NT])
        rs2 = sb("rs2", [P, NT])
        x1t = [sb(f"x1t{i}", [P, LINE]) for i in range(2)]
        x1v = [sb(f"x1v{i}", [P, LINE]) for i in range(2)]
        qk = sb("qk", [P, 2, LINE])
        qkr = sb("qkr", [P, 2, LINE])
        parts = sb("parts", [P, 3, 2, LINE], BF16)
        qst = [sb(f"qst{i}", [P, H2, LINE], BF16) for i in range(2)]
        kst = [sb(f"kst{i}", [P, H2, LINE], BF16) for i in range(2)]
        nm = sb("nm", [P, 8, H2])
        mp = sb("mp", [P, 2, 4 * H2], BF16)
        mt = sb("mt", [2 * 4 * H2, P], BF16)
        mrow = [sb(f"mrow{i}", [4, 8 * H2, WIN], BF16) for i in range(2)]
        prob = [sb(f"prob{i}", [P, H2, 2, WIN]) for i in range(2)]
        vb = [sb(f"vb{i}", [P, 2, NH, 2, 2, VC]) for i in range(2)]
        pvs = sb("pvs", [P, H2 // 2, P])
        rsum = sb("rsum", [P, H2, 4])
        fac = sb("fac", [P, H2, 4])
        ctxn = sb("ctxn", [P, 2, 2, D])
        ctxt = sb("ctxt", [P, S])
        xh2 = [sb(f"xh2{i}", [P, GT, D]) for i in range(2)]
        h2t = sb("h2t", [P, NT * P])
        gt = sb("gt", [P, FF, GW])
        resb = sb("resb", [P, GT, D])
        comb = sb("comb", [P, GT, D])
        h3t = sb("h3t", [P, NT * P])
        wt = sb("wt", [3 * E, NT * P], BF16)
        rt = [sb(f"rt{i}", [P, NT, E]) for i in range(5)]
        rc = [sb(f"rc{i}", [P, NT, E, E]) for i in range(2)]
        rsm = [sb(f"rsm{i}", [P, NT]) for i in range(3)]
        wp = sb("wp", [P, NT, 3, E], BF16)
        sg = [sb(f"sg{i}", [P, GW]) for i in range(2)]
        sw = sb("sw", [P, GW])
        hh = [sb(f"hh{i}", [P, GW]) for i in range(2)]
        fin = [sb(f"fin{i}", [P, GT, D]) for i in range(2)]

        bk = [ctx.enter_context(nc.psum_tensor(f"bank{i}", [P, 512], F32)) for i in range(8)]
        psa, psb, (psv, pst), (w0b, w1b) = bk[0:2], bk[2:4], bk[4:6], bk[6:8]

        scr = nc.dram_tensor("stack_scratch", [B, P, TERMS, 2, LINE], BF16, kind="Internal").ap()
        scr_rows = scr.rearrange("b (r h d) t k n -> b r k (d t) h n", r=2, h=H2)

        waits_met = sem("waits_met")
        x_first, x_rest = sem("x_first"), sem("x_rest")
        c_loaded, small_loaded, wa_loaded = sem("c_loaded"), sem("small_loaded"), sem("wa_loaded")
        late_loaded = sem("late_loaded")
        consts = sem("consts")
        consts_pool = sem("consts_pool")
        sc_step, sc_exp = sem("sc_step"), sem("sc_exp")
        scb_ready = sem("scb_ready")
        mod_done = sem("mod_done")
        mod_ready = sem("mod_ready")
        modt_done, modt_ready = sem("modt_done"), sem("modt_ready")
        ln_dve, ln_pool = sem("ln_dve"), sem("ln_pool")
        xt_done = sem("xt_done")
        x1t_ready = sem("x1t_ready")
        x1v_ready = sem("x1v_ready")
        qk_done, qk_ready = sem("qk_done"), sem("qk_ready")
        parts_step = sem("parts_step")
        scr_written = sem("scr_written")
        stack_ready = sem("stack_ready")
        v_done, v_ready = sem("v_done"), sem("v_ready")
        a_done, max_done = sem("a_done"), sem("max_done")
        mp_step = sem("mp_step")
        mt_done, mt_ready = sem("mt_done"), sem("mt_ready")
        mrow_ready = sem("mrow_ready")
        b_done, exp_done = sem("b_done"), sem("exp_done")
        pv_done = sem("pv_done")
        pvs_ready, pt_done = sem("pvs_ready"), sem("pt_done")
        norm_step = sem("norm_step")
        ctx_done, ctxt_ready = sem("ctx_done"), sem("ctxt_ready")
        proj_done, att_ready = sem("proj_done"), sem("att_ready")
        ln2_step, ln2_root = sem("ln2_step"), sem("ln2_root")
        gate_step = sem("gate_step")
        xh2_ready = sem("xh2_ready")
        t2_done, h2t_ready = sem("t2_done"), sem("h2t_ready")
        w1_done, gelu_done = sem("w1_done"), sem("gelu_done")
        w2_done = sem("w2_done")
        resb_ready = sem("resb_ready")
        comb_step = sem("comb_step")
        ln3_step, ln3_root = sem("ln3_step"), sem("ln3_root")
        t3_done, h3t_ready = sem("t3_done"), sem("h3t_ready")
        router_done = sem("router_done")
        rt_step, rt_exp = sem("rt_step"), sem("rt_exp")
        wt_done, wt_ready = sem("wt_done"), sem("wt_ready")
        gate_done, up_done, wb_done = sem("gate_done"), sem("up_done"), sem("wb_done")
        silu_done, sw_done, hh_ready = sem("silu_done"), sem("sw_done"), sem("hh_ready")
        down_done = sem("down_done")
        fin_step = sem("fin_step")
        out_stored = sem("out_stored")

        ahead = [att_ready, ctxt_ready, proj_done, ctx_done, norm_step, exp_done, pv_done, pvs_ready, pt_done, ln2_step, h2t_ready, t2_done,
                 gelu_done, comb_step, w2_done, t3_done, silu_done, hh_ready, fin_step, sw_done, down_done]
        for s in ahead:
            counts_from(s, 1)
        counts_from(out_stored, 16)

        block = ctx.enter_context(nc.Block())

        def steps(eng, step):
            with eng.Fori(0, (B - 4) // 2) as i:
                for n in range(2):
                    step(2 * i + n, n, True, True, True)
            step(B - 4, 0, True, True, True)
            step(B - 3, 1, False, True, True)
            step(B - 2, 0, False, False, True)
            step(B - 1, 1, False, False, False)

        @block.sync
        def _(sp):
            def write_parts(b):
                sp.wait_ge(parts_step, after(parts_step, 3 * (b + 1)))
                apart(sp)
                dst = scr[ds(b, 1)].rearrange("b p t k n -> (b p) t k n")
                for t0, n, k, src in ((0, 3, 0, parts[:, 0:1, 0, :].broadcast_to([P, 3, LINE])),
                                      (3, 2, 0, parts[:, 1:2, 0, :].broadcast_to([P, 2, LINE])),
                                      (5, 1, 0, parts[:, 2:3, 0, :]),
                                      (0, 3, 1, parts[:, :, 1, :]),
                                      (3, 2, 1, parts[:, 0:2, 1, :]),
                                      (5, 1, 1, parts[:, 0:1, 1, :])):
                    sp.dma_start(dst[:, t0:t0 + n, k, :], src).then_inc(scr_written, 16)

            def read_stacks(b, n):
                sp.wait_ge(scr_written, after(scr_written, 96 * (b + 1)))
                apart(sp)
                sp.wait_ge(b_done, after(b_done, 8 * (b - 1)))
                apart(sp)
                for k, stack in enumerate((qst[n], kst[n])):
                    for r in range(2):
                        src = scr_rows[ds(b, 1), r, k].rearrange("b r h n -> (b r) h n")
                        sp.dma_start(stack[64 * r:64 * r + ROWS], src).then_inc(stack_ready, 16)

            def write_mrow(b, n, hf):
                sp.wait_ge(mt_ready, after(mt_ready, 2 * b + hf + 1))
                apart(sp)
                for part in range(2):
                    for half in range(2):
                        r = 2 * part + half
                        sp.dma_start(mrow[n][r:r + 1, 32 * hf:32 * hf + 32, :],
                                     mt[32 * part:32 * part + 32, WIN * half:WIN * half + WIN]
                                     ).then_inc(mrow_ready, 16)

            x_v = x.rearrange("b (k p) d -> p (b k) d", p=P)
            sp.dma_start(xs[:, 0:2], x_v[:, 0:2]).then_inc(x_first, 16)
            sp.dma_start(cts[:], c_t).then_inc(c_loaded, 16)
            sp.dma_start(wms[:], wmod.rearrange("p (c d) -> p c d", c=6)).then_inc(c_loaded, 16)
            for dst, src in ((col, cols), (row, rows.rearrange("o (r d) -> o r d", r=2).broadcast_to([P, 2, D])),
                             (idf, ident)):
                sp.dma_start(dst[:], src).then_inc(small_loaded, 16)
            sp.dma_start(xs[:, 2:NT], x_v[:, 2:NT]).then_inc(x_rest, 16)
            sp.dma_start(wa[:], wqkvp.rearrange("p (c d) -> p c d", c=4)).then_inc(wa_loaded, 16)
            for dst, src in ((alph, alpha), (vmsk, vmask), (monesf, mones)):
                sp.dma_start(dst[:], src).then_inc(small_loaded, 16)

            write_parts(0)
            read_stacks(0, 0)
            write_parts(1)
            write_mrow(0, 0, 0)
            write_mrow(0, 0, 1)
            read_stacks(1, 1)
            for dst, src in ((w1s, w1.rearrange("p (c d) -> p c d", c=FF)),
                             (w2s, w2.rearrange("(c p) d -> p c d", p=P)),
                             (wgs, wg.rearrange("e p i -> p e i")), (wus, wu.rearrange("e p i -> p e i")),
                             (wds, wd.rearrange("e p i -> p e i")), (wrs, wr),
                             (temps, temp.rearrange("(o n) -> o n", o=1).broadcast_to([P, 1])),
                             (selwf, selw), (earl, earlier.rearrange("o e f -> o e f").broadcast_to([P, E, E]))):
                sp.dma_start(dst[:], src).then_inc(late_loaded, 16)

            def step(b, n, norm, prep, ahead):
                if ahead:
                    write_mrow(b + 1, 1 - n, 0)
                if prep:
                    write_parts(b + 2)
                    read_stacks(b + 2, n)
                if ahead:
                    write_mrow(b + 1, 1 - n, 1)

            steps(sp, step)

            out_v = out.rearrange("b (k p) d -> p (b k) d", p=P)
            with sp.Fori(0, NG // 2) as i:
                for n in range(2):
                    g = 2 * i + n
                    sp.wait_ge(fin_step, after(fin_step, 2 * g + 2))
                    apart(sp)
                    sp.dma_start(out_v[:, ds(GT * g, GT)], fin[n][:]).then_inc(out_stored, 16)
            sp.wait_ge(out_stored, after(out_stored, 16 * NG))

        @block.tensor
        def _(pe):
            def modulation(b, bank):
                pe.wait_ge(scb_ready, after(scb_ready, 1 if b < 2 else 2))
                if b >= 6:
                    pe.wait_ge(mod_ready, after(mod_ready, 2 * (b - 5)))
                pe.matmul(bank[:], scb[:, b, :], wms[:, 0:4, :], start=True, stop=True).then_inc(mod_done, 1)

            def transpose_x(b):
                pe.wait_ge(ln_dve, after(ln_dve, 14 * (b + 1)))
                for k in range(TPB):
                    m = pe.transpose(w0b[:, k * P:(k + 1) * P], x1h[:, k, :], idf[:])
                m.then_inc(xt_done, 1)

            def project_qk(b, n):
                pe.wait_ge(x1t_ready, after(x1t_ready, 2 * (b + 1)))
                pe.matmul(w0b[:, 0:LINE], wa[:, 0, :], x1t[n][:], start=True, stop=True)
                pe.matmul(w1b[:, 0:LINE], wa[:, 1, :], x1t[n][:], start=True, stop=True
                          ).then_inc(qk_done, 1)

            def project_v(b, n):
                pe.wait_ge(x1v_ready, after(x1v_ready, b + 1))
                for eo in range(2):
                    for sel in range(2):
                        j, at = 2 * eo + sel, 32 * eo + P * sel
                        m = pe.matmul(w0b[:, j * P:(j + 1) * P], x1v[n][:, at:at + P], wa[:, 2, :],
                                      start=True, stop=True)
                m.then_inc(v_done, 1)

            def spans(g):
                eo, par, sel = g // 4, g // 2 % 2, g % 2
                return par, [(half, 32 * (4 * sel + 2 * half + eo)) for half in range(2)]

            def scores_a(b, n, g):
                pe.wait_ge(stack_ready, after(stack_ready, 64 * (b + 1)))
                if g == 0:
                    pe.wait_ge(mt_ready, after(mt_ready, 2 * b))
                elif g == 1:
                    pe.wait_ge(att_ready, after(att_ready, b - 1))
                else:
                    pe.wait_ge(max_done, after(max_done, 8 * b + g - 1))
                apart(pe)
                par, halves = spans(g)
                rows_ = slice(64 * par, 64 * par + ROWS)
                for h2 in range(H2):
                    for half, at in halves:
                        m = pe.matmul(psa[g % 2][WIN * half:WIN * half + WIN, WIN * h2:WIN * h2 + WIN],
                                      qst[n][rows_, h2, at:at + WIN], kst[n][rows_, h2, at:at + WIN],
                                      start=True, stop=True)
                m.then_inc(a_done, 1)

            def scores_b(b, n, g):
                pe.wait_ge(mrow_ready, after(mrow_ready, 128 * b + 64 * (g // 4 + 1)))
                if g:
                    pe.wait_ge(exp_done, after(exp_done, 8 * b + g - 1))
                par, halves = spans(g)
                bank = psb[g % 2]
                pe.matmul(bank[:], monesb[:], mrow[n][:, H2 * g:H2 * g + H2, :], start=True, stop=False,
                          skip_group_check=True)
                rows_ = slice(64 * par, 64 * par + ROWS)
                for h2 in range(H2):
                    for half, at in halves:
                        m = pe.matmul(bank[WIN * half:WIN * half + WIN, WIN * h2:WIN * h2 + WIN],
                                      kst[n][rows_, h2, at:at + WIN], qst[n][rows_, h2, at:at + WIN],
                                      start=False, stop=True, skip_group_check=True)
                m.then_inc(b_done, 1)

            def transpose_m(b, hf, bank):
                pe.wait_ge(mp_step, after(mp_step, 4 * b + 2 * hf + 2))
                apart(pe)
                pe.transpose(bank[0:64, 0:64].bitcast(BF16), mp[:].rearrange("p a c -> p (a c)"), idb[:]
                             ).then_inc(mt_done, 1)

            def probs_v(b, n, gp):
                pe.wait_ge(exp_done, after(exp_done, 8 * b + 2 * gp + 2))
                pe.wait_ge(v_ready, after(v_ready, 4 * (b + 1)))
                pe.wait_ge(pvs_ready, after(pvs_ready, 4 * b + gp))
                eo, par = gp // 2, gp % 2
                for h2 in range(H2):
                    m = pe.matmul(psv[WIN * (h2 % 2):WIN * (h2 % 2) + WIN, P * (h2 // 2):P * (h2 // 2) + P],
                                  vb[n][:, eo, H2 * par + h2, :, :, :], prob[gp % 2][:, h2, :, :],
                                  start=True, stop=True)
                m.then_inc(pv_done, 1)

            def turn_sums(b, gp):
                pe.wait_ge(pvs_ready, after(pvs_ready, 4 * b + gp + 1))
                pe.wait_ge(norm_step, after(norm_step, 4 * (4 * b + gp)))
                for k in range(H2 // 2):
                    m = pe.transpose(pst[:, k * P:(k + 1) * P], pvs[:, k, :], idf[:])
                m.then_inc(pt_done, 1)

            def gather_context(b):
                pe.wait_ge(norm_step, after(norm_step, 16 * (b + 1)))
                for eo in range(2):
                    for half in range(2):
                        at = 32 * eo + WIN * half
                        dst = w1b[:, at:at + 2 * P].rearrange("p (s q) -> p s q", s=2)[:, :, 0:WIN]
                        m = pe.matmul(dst, ctxn[:, eo, half, :], idf[:], start=(eo == half == 0), stop=True,
                                      skip_group_check=True)
                m.then_inc(ctx_done, 1)

            def project_out(b, b_next):
                pe.wait_ge(ctxt_ready, after(ctxt_ready, b + 1))
                pe.wait_ge(max_done, after(max_done, 8 * b + 16) if b_next else after(max_done, 8 * B))
                for k in range(TPB):
                    m = pe.matmul(psa[1][:, k * P:(k + 1) * P], ctxt[:, k * P:(k + 1) * P], wa[:, 3, :],
                                  start=True, stop=True)
                m.then_inc(proj_done, 1)

            for s in ahead:
                pe.sem_inc(s, 1)
            pe.sem_inc(out_stored, 16)
            pe.wait_ge(c_loaded, after(c_loaded, 32))
            modulation(0, bk[0])
            modulation(1, bk[1])
            pe.wait_ge(sc_step, after(sc_step, 3))
            for j in range(2):
                m = pe.matmul(w0b[:, B * j:B * j + B], wms[:, 4 + j, :], sce[:, 3, :], start=True, stop=True)
            m.then_inc(modt_done, 1)
            for b in range(2, 6):
                modulation(b, bk[b])
            pe.wait_ge(small_loaded, after(small_loaded, 96))
            pe.wait_ge(wa_loaded, after(wa_loaded, 16))
            pe.wait_ge(consts, after(consts, 3))
            pe.wait_ge(modt_ready, after(modt_ready, 2))
            transpose_x(0)
            modulation(6, bk[0])
            project_qk(0, 0)
            modulation(7, bk[1])
            pe.wait_ge(qk_ready, after(qk_ready, 4))
            project_v(0, 0)
            pe.wait_ge(v_ready, after(v_ready, 4))
            transpose_x(1)
            project_qk(1, 1)
            pe.wait_ge(mod_ready, after(mod_ready, 2 * B))
            for g in range(5):
                scores_a(0, 0, g)
            pe.wait_ge(qk_ready, after(qk_ready, 8))
            transpose_m(0, 0, w1b)
            for g in range(5, 8):
                scores_a(0, 0, g)
            project_v(1, 1)
            transpose_m(0, 1, psa[0])
            scores_b(0, 0, 0)
            scores_b(0, 0, 1)

            def step(b, n, norm, prep, ahead):
                def a(g):
                    if ahead:
                        scores_a(b + 1, 1 - n, g)

                scores_b(b, n, 2)
                probs_v(b, n, 0)
                a(0)
                scores_b(b, n, 3)
                turn_sums(b, 0)
                a(1)
                if prep:
                    pe.wait_ge(v_ready, after(v_ready, 4 * (b + 2)))
                    transpose_x(b + 2)
                scores_b(b, n, 4)
                a(2)
                probs_v(b, n, 1)
                if prep:
                    pe.wait_ge(ctxt_ready, after(ctxt_ready, b))
                    project_qk(b + 2, n)
                a(3)
                scores_b(b, n, 5)
                turn_sums(b, 1)
                a(4)
                if ahead:
                    if prep:
                        pe.wait_ge(qk_ready, after(qk_ready, 4 * (b + 3)))
                    else:
                        pe.wait_ge(v_ready, after(v_ready, 4 * (b + 2)))
                        pe.wait_ge(ctxt_ready, after(ctxt_ready, b))
                    transpose_m(b + 1, 0, w1b)
                scores_b(b, n, 6)
                probs_v(b, n, 2)
                a(5)
                scores_b(b, n, 7)
                turn_sums(b, 2)
                a(6)
                probs_v(b, n, 3)
                a(7)
                if ahead:
                    scores_b(b + 1, 1 - n, 0)
                turn_sums(b, 3)
                if prep:
                    project_v(b + 2, n)
                if ahead:
                    pe.wait_ge(mt_ready, after(mt_ready, 2 * b + 3))
                else:
                    pe.wait_ge(ctxt_ready, after(ctxt_ready, b))
                gather_context(b)
                if ahead:
                    scores_b(b + 1, 1 - n, 1)
                    transpose_m(b + 1, 1, psa[0])
                project_out(b, ahead)

            steps(pe, step)

            with pe.Fori(0, NG // 2) as i:
                for n in range(2):
                    g = 2 * i + n
                    pe.wait_ge(xh2_ready, after(xh2_ready, g + 1))
                    pe.wait_ge(h2t_ready, after(h2t_ready, 2 * i))
                    for k in range(GT):
                        m = pe.transpose(psa[n][:, k * P:(k + 1) * P], xh2[n][:, k, :], idf[:])
                    m.then_inc(t2_done, 1)

            pe.wait_ge(late_loaded, after(late_loaded, 144))
            pe.wait_ge(norm_step, after(norm_step, 16 * B))
            with pe.Fori(0, NG) as g:
                pe.wait_ge(h2t_ready, after(h2t_ready, g + 1))
                for c in range(FF):
                    pe.wait_ge(gelu_done, after(gelu_done, FF * g))
                    pe.matmul(bk[2 + c][:], w1s[:, c, :], h2t[:, ds(GW * g, GW)], start=True, stop=True
                              ).then_inc(w1_done, 1)
                pe.wait_ge(comb_step, after(comb_step, 3 * g))
                pe.wait_ge(att_ready, after(att_ready, B))
                for c in range(FF):
                    pe.wait_ge(gelu_done, after(gelu_done, FF * g + c + 1))
                    for k in range(GT):
                        m = pe.matmul(bk[6][:, k * P:(k + 1) * P], gt[:, c, k * P:(k + 1) * P], w2s[:, c, :],
                                      start=(c == 0 and k == 0), stop=(c == FF - 1), skip_group_check=True)
                m.then_inc(w2_done, 1)

            def router(g):
                pe.wait_ge(h3t_ready, after(h3t_ready, 2 * (g + 1)))
                for k in range(GT):
                    t = GT * g + k
                    m = pe.matmul(bk[7][:, E * t:E * t + E], h3t[:, t * P:(t + 1) * P], wrs[:], start=True, stop=True)
                m.then_inc(router_done, 1)

            for g in range(NG):
                pe.wait_ge(ln3_step, after(ln3_step, 13 * (g + 1)))
                if g >= 2:
                    pe.wait_ge(h3t_ready, after(h3t_ready, 2 * (g - 1)))
                for k in range(GT):
                    m = pe.transpose(psa[g % 2][:, k * P:(k + 1) * P], xh2[g % 2][:, k, :], idf[:])
                m.then_inc(t3_done, 1)
                if g:
                    router(g - 1)
            router(NG - 1)

            pe.wait_ge(rt_step, after(rt_step, RT_PARTS))
            wt_ps = [bk[6].bitcast(BF16), bk[7].bitcast(BF16)]
            for t in range(NT):
                m = pe.transpose(wt_ps[t // 8][0:3 * E, (t % 8) * P:(t % 8 + 1) * P],
                                 wp[:, t, :, :].rearrange("p a e -> p (a e)"), idb[:])
            m.then_inc(wt_done, 1)
            pe.wait_ge(wt_ready, after(wt_ready, 2))

            def down(g, e):
                pe.wait_ge(hh_ready, after(hh_ready, E * g + e + 1))
                if e == 0:
                    pe.wait_ge(fin_step, after(fin_step, 2 * g))
                for k in range(GT):
                    m = pe.matmul(bk[6][:, k * P:(k + 1) * P], hh[e % 2][:, k * P:(k + 1) * P], wds[:, e, :],
                                  start=(e == 0 and k == 0), stop=(e == E - 1), skip_group_check=True)
                m.then_inc(down_done, 1)

            with pe.Fori(0, NG) as g:
                for e in range(E):
                    tokens = h3t[:, ds(GW * g, GW)]
                    pe.wait_ge(silu_done, after(silu_done, E * g + e - 1)) if e else pe.wait_ge(silu_done, after(silu_done, E * g))
                    pe.matmul(bk[e % 2][:], wgs[:, e, :], tokens, start=True, stop=True).then_inc(gate_done, 1)
                    pe.wait_ge(hh_ready, after(hh_ready, E * g + e - 1)) if e else pe.wait_ge(hh_ready, after(hh_ready, E * g))
                    apart(pe)
                    pe.matmul(bk[4 + e % 2][:], selwb[:, e, :], wt[:, ds(GW * g, GW)], start=True, stop=True
                              ).then_inc(wb_done, 1)
                    pe.matmul(bk[2 + e % 2][:], wus[:, e, :], tokens, start=True, stop=True).then_inc(up_done, 1)
                    if e:
                        down(g, e - 1)
                down(g, E - 1)

        @block.scalar
        def _(act):
            def copy_mod(b, bank):
                act.wait_ge(mod_done, after(mod_done, b + 1))
                act.activation(modb[:, ds(b, 1), CA, :], bank[:, 0:D], ACT.Identity, bias=1.0).then_inc(mod_ready, 1)
                act.activation(modb[:, ds(b, 1), SA:, :], bank[:, D:4 * D], ACT.Copy).then_inc(mod_ready, 1)

            def copy_xt(b, n):
                act.wait_ge(xt_done, after(xt_done, b + 1))
                act.wait_ge(qk_done, after(qk_done, b - 1))
                act.activation(x1t[n][:, PAD:PAD + S], w0b[:, 0:S], ACT.Identity, bias=col[:, LN1B:LN1B + 1],
                               scale=col[:, LN1G:LN1G + 1]).then_inc(x1t_ready, 1)
                ends = w0b[:, 0:2 * (S - PAD)].rearrange("p (a c) -> p a c", a=2)[:, :, 0:PAD]
                pads = x1t[n][:].rearrange("p (a c) -> p a c", a=2)
                act.activation(pads[:, 0, 0:PAD], ends[:, 0, :], ACT.Identity, bias=col[:, LN1B:LN1B + 1],
                               scale=col[:, LN1G:LN1G + 1])
                act.activation(pads[:, 1, LINE // 2 - PAD:], ends[:, 1, :], ACT.Identity,
                               bias=col[:, LN1B:LN1B + 1], scale=col[:, LN1G:LN1G + 1]).then_inc(x1t_ready, 1)

            def copy_qk(b):
                act.wait_ge(qk_done, after(qk_done, b + 1))
                act.wait_ge(parts_step, after(parts_step, 3 * b))
                act.wait_ge(scr_written, after(scr_written, 96 * b))
                act.activation(qk[:, 0, :], w0b[:, 0:LINE], ACT.Identity, bias=bqs[:], scale=SCALE
                               ).then_inc(qk_ready, 1)
                act.activation(parts[:, 0, 0, :], w0b[:, 0:LINE], ACT.Identity, bias=bqs[:], scale=SCALE
                               ).then_inc(qk_ready, 1)
                act.activation(qk[:, 1, :], w1b[:, 0:LINE], ACT.Identity, bias=col[:, BK:BK + 1]
                               ).then_inc(qk_ready, 1)
                act.activation(parts[:, 0, 1, :], w1b[:, 0:LINE], ACT.Identity, bias=col[:, BK:BK + 1]
                               ).then_inc(qk_ready, 1)

            def copy_v(b, n):
                act.wait_ge(v_done, after(v_done, b + 1))
                act.wait_ge(pv_done, after(pv_done, 4 * (b - 1)))
                for eo in range(2):
                    for half in range(2):
                        p = slice(WIN * half, WIN * half + WIN)
                        src = w0b[p, 2 * P * eo:2 * P * (eo + 1)].rearrange("p (s h d) -> p s h d", s=2, d=HD)
                        dst = vb[n][p, eo, :, :, half, 0:HD].rearrange("p h s d -> p s h d")
                        act.activation(dst, src, ACT.Copy).then_inc(v_ready, 1)

            def exp(b, n, g):
                act.wait_ge(b_done, after(b_done, 8 * b + g + 1))
                act.wait_ge(pv_done, after(pv_done, 4 * b + g // 2 - 1))
                act.activation(prob[g // 2 % 2][:, :, g % 2, :], psb[g % 2][:].rearrange("p (h q) -> p h q", h=H2),
                               ACT.Exp).then_inc(exp_done, 1)

            def copy_pv(b, gp):
                act.wait_ge(pv_done, after(pv_done, 4 * b + gp + 1))
                act.wait_ge(pt_done, after(pt_done, 4 * b + gp))
                act.activation(pvs[:], psv[:].rearrange("p (k q) -> p k q", q=P), ACT.Copy).then_inc(pvs_ready, 1)

            act.wait_ge(c_loaded, after(c_loaded, 32))
            act.activation(sce[:, 0, :], cts[:], ACT.Exp, scale=-1.0).then_inc(sc_exp, 1)
            copy_mod(0, bk[0])
            copy_mod(1, bk[1])
            act.wait_ge(modt_done, after(modt_done, 1))
            act.activation(modt[:, 0, :], w0b[:, 0:B], ACT.Copy).then_inc(modt_ready, 1)
            act.activation(modt[:, 1, :], w0b[:, B:2 * B], ACT.Identity, bias=1.0).then_inc(modt_ready, 1)
            copy_mod(2, bk[2])
            copy_mod(3, bk[3])
            act.wait_ge(small_loaded, after(small_loaded, 96))
            act.wait_ge(consts, after(consts, 11))
            act.wait_ge(consts_pool, after(consts_pool, 5))
            copy_xt(0, 0)
            copy_mod(4, bk[4])
            copy_qk(0)
            copy_v(0, 0)
            copy_mod(5, bk[5])
            copy_xt(1, 1)
            copy_mod(6, bk[0])
            copy_mod(7, bk[1])
            copy_qk(1)
            copy_v(1, 1)
            exp(0, 0, 0)
            exp(0, 0, 1)

            def step(b, n, norm, prep, ahead):
                exp(b, n, 2)
                copy_pv(b, 0)
                exp(b, n, 3)
                if prep:
                    copy_xt(b + 2, n)
                exp(b, n, 4)
                copy_pv(b, 1)
                if prep:
                    copy_qk(b + 2)
                exp(b, n, 5)
                exp(b, n, 6)
                copy_pv(b, 2)
                exp(b, n, 7)
                copy_pv(b, 3)
                if ahead:
                    exp(b + 1, 1 - n, 0)
                act.wait_ge(ctx_done, after(ctx_done, b + 1))
                act.wait_ge(proj_done, after(proj_done, b))
                act.activation(ctxt[:], w1b[:, PAD:PAD + S], ACT.Identity, bias=col[:, BV:BV + 1]
                               ).then_inc(ctxt_ready, 1)
                if ahead:
                    exp(b + 1, 1 - n, 1)
                if prep:
                    copy_v(b + 2, n)

            steps(act, step)

            act.wait_ge(gate_step, after(gate_step, 4))
            with act.Fori(0, NG // 2) as i:
                for n in range(2):
                    g = 2 * i + n
                    act.wait_ge(t2_done, after(t2_done, g + 1))
                    act.activation(h2t[:, ds(GW * g, GW)], psa[n][:], ACT.Identity, bias=col[:, LN2B:LN2B + 1],
                                   scale=col[:, LN2G:LN2G + 1]).then_inc(h2t_ready, 1)

            with act.Fori(0, NG) as g:
                act.wait_ge(w2_done, after(w2_done, g))
                for c in range(FF):
                    act.wait_ge(w1_done, after(w1_done, FF * g + c + 1))
                    act.activation(gt[:, c, :], bk[2 + c][:], ACT.Gelu, bias=col[:, B1 + c:B1 + c + 1]
                                   ).then_inc(gelu_done, 1)

            for g in range(NG):
                act.wait_ge(t3_done, after(t3_done, g + 1))
                for j in range(2):
                    b = 2 * g + j
                    act.activation(h3t[:, S * b:S * (b + 1)], psa[g % 2][:, S * j:S * (j + 1)], ACT.Identity,
                                   bias=modt[:, 0, b:b + 1], scale=modt[:, 1, b:b + 1]).then_inc(h3t_ready, 1)

            act.wait_ge(rt_step, after(rt_step, 1))
            act.activation(rt[1][:], rt[0][:], ACT.Exp, scale=-1.0).then_inc(rt_exp, 1)
            act.wait_ge(rt_step, after(rt_step, RT_DIST))
            act.activation(rt[2][:], rt[0][:], ACT.Exp, scale=-1.0 / 0.1).then_inc(rt_exp, 1)
            act.activation(rt[3][:], rt[0][:], ACT.Exp, scale=-1.0 / 0.3).then_inc(rt_exp, 1)

            with act.Fori(0, NG) as g:
                for e in range(E):
                    act.wait_ge(gate_done, after(gate_done, E * g + e + 1))
                    act.wait_ge(sw_done, after(sw_done, E * g + e - 1)) if e else act.wait_ge(sw_done, after(sw_done, E * g))
                    act.activation(sg[e % 2][:], bk[e % 2][:], ACT.Silu).then_inc(silu_done, 1)

        @block.gpsimd
        def _(pool):
            def root(dst, src, n, s):
                pool.tensor_tensor(dst, src, mhalf[:, 0:n], ALU.pow).then_inc(s, 1)

            def two(ap):
                return ap.rearrange("p (o d) -> p o d", o=1).broadcast_to([P, TPB, D])

            def norm_x(b):
                pool.wait_ge(ln_dve, after(ln_dve, 14 * b + 5))
                root(rs[:, 0:TPB], ve[:, 0:TPB], TPB, ln_pool)
                pool.wait_ge(ln_dve, after(ln_dve, 14 * b + 7))
                pool.wait_ge(mod_ready, after(mod_ready, 2 * (b + 1)))
                pool.tensor_tensor(h1[:], xh[:], modb[:, ds(b, 1), CA, :].broadcast_to([P, TPB, D]), ALU.mult
                                   ).then_inc(ln_pool, 1)
                pool.wait_ge(ln_pool, after(ln_pool, 5 * b + 2))
                pool.tensor_tensor(h1[:], h1[:], modb[:, ds(b, 1), SA, :].broadcast_to([P, TPB, D]), ALU.add
                                   ).then_inc(ln_pool, 1)
                pool.wait_ge(ln_pool, after(ln_pool, 5 * b + 3))
                pool.tensor_tensor(res[:, ds(TPB * b, TPB), :], h1[:], two(row[:, 0, :]), ALU.add
                                   ).then_inc(ln_pool, 1)
                pool.wait_ge(ln_dve, after(ln_dve, 14 * b + 12))
                root(rs[:, 0:TPB], ve[:, 0:TPB], TPB, ln_pool)

            def copy_x1v(b, n):
                pool.wait_ge(x1t_ready, after(x1t_ready, 2 * (b + 1)))
                pool.wait_ge(v_done, after(v_done, b - 1))
                apart(pool)
                pool.tensor_copy(x1v[n][:, PAD:PAD + S], x1t[n][:, PAD:PAD + S]).then_inc(x1v_ready, 1)

            def cut_m(b, hf):
                pool.wait_ge(max_done, after(max_done, 8 * b + 4 * hf + 4))
                pool.wait_ge(mt_done, after(mt_done, 2 * b + hf))
                apart(pool)
                src = nm[:, 4 * hf:4 * hf + 4, :].rearrange("p g h -> p (g h)")
                pool.tensor_copy(mp[:, 0, :], src).then_inc(mp_step, 1)
                pool.wait_ge(mp_step, after(mp_step, 4 * b + 2 * hf + 1))
                pool.tensor_tensor(mp[:, 1, :], src, mp[:, 0, :], ALU.subtract).then_inc(mp_step, 1)

            pool.memset(mhalf[:], -0.5).then_inc(consts_pool, 1)
            pool.memset(x1v[0][:], 0.0).then_inc(consts_pool, 1)
            pool.memset(x1v[1][:], 0.0).then_inc(consts_pool, 1)
            pool.memset(vb[0][:], 0.0).then_inc(consts_pool, 1)
            pool.memset(vb[1][:], 0.0).then_inc(consts_pool, 1)
            pool.wait_ge(consts_pool, after(consts_pool, 5))
            pool.wait_ge(small_loaded, after(small_loaded, 96))
            norm_x(0)
            norm_x(1)
            copy_x1v(0, 0)
            copy_x1v(1, 1)
            cut_m(0, 0)
            norm_x(2)
            cut_m(0, 1)

            def step(b, n, norm, prep, ahead):
                if norm:
                    norm_x(b + 3)
                if ahead:
                    cut_m(b + 1, 0)
                if prep:
                    copy_x1v(b + 2, n)
                if ahead:
                    cut_m(b + 1, 1)
                pool.wait_ge(ln2_step, after(ln2_step, 6 * (b + 1)))
                pool.tensor_tensor(rs2[:, ds(TPB * b, TPB)], ve2[:, ds(TPB * b, TPB)], mhalf[:, 0:TPB], ALU.pow
                                   ).then_inc(ln2_root, 1)

            steps(pool, step)

            pool.wait_ge(att_ready, after(att_ready, B))
            with pool.Fori(0, NG) as g:
                pool.wait_ge(comb_step, after(comb_step, 3 * g))
                pool.tensor_tensor(resb[:], res[:, ds(GT * g, GT), :],
                                   row[:, 1:2, :].broadcast_to([P, GT, D]), ALU.add).then_inc(resb_ready, 1)
                pool.wait_ge(ln3_step, after(ln3_step, 13 * g + 9))
                root(rs[:, 0:GT], ve[:, 0:GT], GT, ln3_root)

        @block.vector
        def _(dve):
            def stats(src_of, s, base, n, st_, mv_, ve_):
                apart(dve)
                for k in range(n):
                    dve.bn_stats(st_[:, k, :], src_of(k)).then_inc(s, 1)
                dve.wait_ge(s, after(s, base + n))
                apart(dve)
                for k in range(n):
                    dve.bn_aggr(mv_[:, k, :], st_[:, k, :]).then_inc(s, 1)
                dve.wait_ge(s, after(s, base + 2 * n))
                dve.tensor_scalar(ve_, mv_[:, 0:n, 1], EPS, None, ALU.add).then_inc(s, 1)

            def standard(dst, src, mean, r):
                return dve.tensor_scalar(dst, src, mean, r, ALU.subtract, ALU.mult)

            def ln_a(b):
                stats(lambda k: xs[:, ds(TPB * b + k, 1), :], ln_dve, 14 * b, TPB, st, mv, ve[:, 0:TPB])

            def ln_b(b):
                dve.wait_ge(ln_pool, after(ln_pool, 5 * b + 1))
                for k in range(TPB):
                    standard(xh[:, k, :], xs[:, ds(TPB * b + k, 1), :], mv[:, k, 0:1], rs[:, k:k + 1]
                             ).then_inc(ln_dve, 1)

            def ln_c(b):
                dve.wait_ge(ln_dve, after(ln_dve, 14 * b + 7))
                dve.wait_ge(ln_pool, after(ln_pool, 5 * b + 3))
                stats(lambda k: h1[:, k, :], ln_dve, 14 * b + 7, TPB, st, mv, ve[:, 0:TPB])

            def ln_d(b):
                dve.wait_ge(ln_pool, after(ln_pool, 5 * b + 5))
                dve.wait_ge(xt_done, after(xt_done, b))
                for k in range(TPB):
                    standard(x1h[:, k, :], h1[:, k, :], mv[:, k, 0:1], rs[:, k:k + 1]).then_inc(ln_dve, 1)

            def spread_sc(b0, n):
                dve.tensor_copy(scb[:, b0:b0 + n, :],
                                sce[:, 3, b0:b0 + n].rearrange("p (b o) -> p b o", o=1).broadcast_to([P, n, P])
                                ).then_inc(scb_ready, 1)

            def cut_qk(b, half):
                if half == 0:
                    dve.wait_ge(qk_ready, after(qk_ready, 4 * (b + 1)))
                    dve.tensor_tensor(qkr[:], qk[:], parts[:, 0], ALU.subtract).then_inc(parts_step, 1)
                else:
                    dve.wait_ge(parts_step, after(parts_step, 3 * b + 1))
                    dve.tensor_copy(parts[:, 1], qkr[:]).then_inc(parts_step, 1)
                    dve.wait_ge(parts_step, after(parts_step, 3 * b + 2))
                    dve.tensor_tensor(parts[:, 2], qkr[:], parts[:, 1], ALU.subtract).then_inc(parts_step, 1)

            def maxima(b, g):
                dve.wait_ge(a_done, after(a_done, 8 * b + g + 1))
                dve.wait_ge(mp_step, after(mp_step, 4 * (b - 1) + 2 * (g // 4) + 2))
                dve.tensor_reduce(nm[:, g, :], psa[g % 2][:].rearrange("p (h k) -> p h k", h=H2), AX_X, ALU.max,
                                  negate=True).then_inc(max_done, 1)

            def copy_mt(b, hf):
                dve.wait_ge(mt_done, after(mt_done, 2 * b + hf + 1))
                dve.wait_ge(mrow_ready, after(mrow_ready, 64 * (2 * b + hf)))
                dve.tensor_copy(mt[:], (psa[0] if hf else w1b)[0:64, 0:64].bitcast(BF16)).then_inc(mt_ready, 1)

            def normalise(b, gp):
                dve.wait_ge(pt_done, after(pt_done, 4 * b + gp + 1))
                eo, par = gp // 2, gp % 2
                base = 16 * b + 4 * gp
                sums = pst[:].rearrange("p (h w v) -> p h w v", h=H2, v=VC)
                dve.wait_ge(norm_step, after(norm_step, base))
                dve.reciprocal(rsum[:], sums[:, :, :, HD]).then_inc(norm_step, 1)
                dve.wait_ge(norm_step, after(norm_step, base + 1))
                dve.tensor_tensor(fac[:], rsum[:], alph[:, eo:eo + 1, :].broadcast_to([P, H2, 4]), ALU.mult
                                  ).then_inc(norm_step, 1)
                dve.wait_ge(norm_step, after(norm_step, base + 2))
                dve.wait_ge(ctx_done, after(ctx_done, b))
                for sel in range(2):
                    p = slice(WIN * sel, WIN * sel + WIN)
                    dst = ctxn[p, eo, :, WIN * par:WIN * par + WIN].rearrange("p f (h d) -> p f h d", d=HD)
                    src = sums[p, :, 2 * sel:2 * sel + 2, 0:HD].rearrange("p h f d -> p f h d")
                    f = fac[p, :, 2 * sel:2 * sel + 2].rearrange("p h (f o) -> p f h o", o=1)
                    dve.tensor_tensor(dst, src, f.broadcast_to([WIN, 2, H2, HD]), ALU.mult
                                      ).then_inc(norm_step, 1)

            def attention_out(b):
                dve.wait_ge(proj_done, after(proj_done, b + 1))
                dve.wait_ge(ln_pool, after(ln_pool, 5 * b + 4))
                tiles = res[:, ds(TPB * b, TPB), :]
                dve.tensor_tensor(tiles, psa[1][:, 0:S].rearrange("p (k d) -> p k d", k=TPB), tiles, ALU.add
                                  ).then_inc(att_ready, 1)

            def ln2(b):
                dve.wait_ge(att_ready, after(att_ready, b + 1))
                dve.wait_ge(ln2_step, after(ln2_step, 6 * b))
                stats(lambda k: res[:, ds(TPB * b + k, 1), :], ln2_step, 6 * b, TPB, st2, mv2,
                      ve2[:, ds(TPB * b, TPB)])
                dve.tensor_copy(mean2[:, ds(TPB * b, TPB)], mv2[:, :, 0]).then_inc(ln2_step, 1)

            dve.wait_ge(sc_exp, after(sc_exp, 1))
            dve.tensor_scalar(sce[:, 1, :], sce[:, 0, :], 1.0, None, ALU.add).then_inc(sc_step, 1)
            dve.wait_ge(sc_step, after(sc_step, 1))
            dve.reciprocal(sce[:, 2, :], sce[:, 1, :]).then_inc(sc_step, 1)
            dve.wait_ge(sc_step, after(sc_step, 2))
            dve.tensor_tensor(sce[:, 3, :], sce[:, 2, :], cts[:], ALU.mult).then_inc(sc_step, 1)
            dve.wait_ge(sc_step, after(sc_step, 3))
            spread_sc(0, 2)
            dve.wait_ge(x_first, after(x_first, 16))
            ln_a(0)
            spread_sc(2, B - 2)
            dve.wait_ge(consts_pool, after(consts_pool, 1))
            ln_b(0)
            dve.wait_ge(small_loaded, after(small_loaded, 96))
            dve.tensor_copy(idb[:], idf[:]).then_inc(consts, 1)
            dve.tensor_copy(monesb[:], monesf[:]).then_inc(consts, 1)
            dve.tensor_scalar(bqs[:], col[:, BQ:BQ + 1], SCALE, None, ALU.mult).then_inc(consts, 1)
            ln_c(0)
            dve.wait_ge(consts_pool, after(consts_pool, 5))
            for n in range(2):
                for half in range(2):
                    p = slice(WIN * half, WIN * half + WIN)
                    for sel in range(2):
                        dve.tensor_copy(vb[n][p, :, :, sel, half, HD],
                                        vmsk[p, :, sel:sel + 1].broadcast_to([WIN, 2, NH])).then_inc(consts, 1)
            ln_d(0)
            dve.wait_ge(x_rest, after(x_rest, 16))
            ln_a(1)
            ln_b(1)
            ln_c(1)
            cut_qk(0, 0)
            cut_qk(0, 1)
            ln_d(1)
            cut_qk(1, 0)
            cut_qk(1, 1)
            for g in range(5):
                maxima(0, g)
            copy_mt(0, 0)
            ln_a(2)
            ln_b(2)
            ln_c(2)
            ln_d(2)
            for g in range(5, 8):
                maxima(0, g)
            copy_mt(0, 1)

            def step(b, n, norm, prep, ahead):
                def maxima_next(g):
                    if ahead:
                        maxima(b + 1, g)

                if norm:
                    ln_a(b + 3)
                maxima_next(0)
                normalise(b, 0)
                if norm:
                    ln_b(b + 3)
                maxima_next(1)
                maxima_next(2)
                if norm:
                    ln_c(b + 3)
                maxima_next(3)
                normalise(b, 1)
                maxima_next(4)
                if ahead:
                    copy_mt(b + 1, 0)
                if prep:
                    cut_qk(b + 2, 0)
                    cut_qk(b + 2, 1)
                maxima_next(5)
                normalise(b, 2)
                if norm:
                    ln_d(b + 3)
                maxima_next(6)
                maxima_next(7)
                normalise(b, 3)
                if ahead:
                    copy_mt(b + 1, 1)
                attention_out(b)
                ln2(b)

            steps(dve, step)

            g_v = modb[:, :, GA:, :]
            sign, size = (t[:].rearrange("p (b c d) -> p b c d", b=B, c=2) for t in (h2t, h3t))
            dve.wait_ge(mod_ready, after(mod_ready, 2 * B))
            dve.tensor_scalar(sign, g_v, 0.0, 2.0, ALU.is_ge, ALU.mult).then_inc(gate_step, 1)
            dve.scalar_tensor_tensor(out=size, in0=g_v, scalar=-1.0, in1=g_v, op0=ALU.mult, op1=ALU.max
                                     ).then_inc(gate_step, 1)
            dve.wait_ge(gate_step, after(gate_step, 2))
            dve.tensor_scalar(size, size, 0.25, None, ALU.max).then_inc(gate_step, 1)
            dve.wait_ge(gate_step, after(gate_step, 3))
            dve.scalar_tensor_tensor(out=g_v, in0=sign, scalar=1.0, in1=size, op0=ALU.subtract, op1=ALU.mult
                                     ).then_inc(gate_step, 1)
            dve.wait_ge(ln2_root, after(ln2_root, B))
            with dve.Fori(0, NG // 2) as i:
                for n in range(2):
                    g = 2 * i + n
                    dve.wait_ge(t2_done, after(t2_done, 2 * i))
                    for k in range(GT):
                        t = GT * g + k
                        m = standard(xh2[n][:, k, :], res[:, ds(t, 1), :], mean2[:, ds(t, 1)], rs2[:, ds(t, 1)])
                    m.then_inc(xh2_ready, 1)

            dve.wait_ge(t2_done, after(t2_done, NG))
            dve.wait_ge(gate_step, after(gate_step, 4))
            with dve.Fori(0, NG // 2) as i:
                for n in range(2):
                    g = 2 * i + n
                    dve.wait_ge(w2_done, after(w2_done, g + 1))
                    dve.wait_ge(resb_ready, after(resb_ready, g + 1))
                    tiles = xs[:, ds(GT * g, GT), :]
                    dve.tensor_tensor(comb[:], bk[6][:].rearrange("p (k d) -> p k d", k=GT), resb[:], ALU.add
                                      ).then_inc(comb_step, 1)
                    dve.wait_ge(comb_step, after(comb_step, 3 * g + 1))
                    ga = modb[:, ds(2 * g, 2), GA:GA + 1, :].broadcast_to([P, 2, TPB, D])
                    comb_v = comb[:].rearrange("p (b k) d -> p b k d", b=2)
                    dve.tensor_tensor(comb_v, comb_v, ga, ALU.mult).then_inc(comb_step, 1)
                    dve.wait_ge(comb_step, after(comb_step, 3 * g + 2))
                    dve.tensor_tensor(tiles, tiles, comb[:], ALU.add).then_inc(comb_step, 1)
                    dve.wait_ge(comb_step, after(comb_step, 3 * g + 3))
                    stats(lambda k: xs[:, ds(GT * g + k, 1), :], ln3_step, 13 * g, GT, st, mv, ve[:, 0:GT])
                    dve.wait_ge(ln3_root, after(ln3_root, g + 1))
                    dve.wait_ge(t3_done, after(t3_done, 2 * i))
                    for k in range(GT):
                        standard(xh2[n][:, k, :], xs[:, ds(GT * g + k, 1), :], mv[:, k, 0:1], rs[:, k:k + 1]
                                 ).then_inc(ln3_step, 1)

            did = [0]

            def link(ins):
                did[0] += 1
                ins.then_inc(rt_step, 1)
                dve.wait_ge(rt_step, after(rt_step, did[0]))

            lo_e = [P, NT, E]

            def per_token(t):
                return t[:].rearrange("p (t o) -> p t o", o=1).broadcast_to(lo_e)

            z, ex, wz, fb, mask = rt
            dve.wait_ge(late_loaded, after(late_loaded, 144))
            dve.tensor_copy(selwb[:], selwf[:]).then_inc(consts, 1)
            dve.reciprocal(rtemp[:], temps[:]).then_inc(consts, 1)
            dve.wait_ge(consts, after(consts, 13))
            dve.wait_ge(router_done, after(router_done, NG))
            logits = bk[7][:, 0:NT * E].rearrange("p (t e) -> p t e", e=E)
            link(dve.tensor_scalar(z[:], logits, rtemp[:], None, ALU.mult))
            dve.wait_ge(rt_exp, after(rt_exp, 1))
            link(dve.tensor_scalar(ex[:], ex[:], 1.0, None, ALU.add))
            link(dve.reciprocal(mask[:], ex[:]))
            link(dve.tensor_scalar(ex[:], mask[:], ZONE_LOW, None, ALU.is_ge))
            link(dve.tensor_scalar(wz[:], mask[:], ZONE_MID, None, ALU.subtract))
            link(dve.scalar_tensor_tensor(out=z[:], in0=wz[:], scalar=-1.0, in1=wz[:], op0=ALU.mult,
                                          op1=ALU.max))
            assert did[0] == RT_DIST
            link(dve.scalar_tensor_tensor(out=ex[:], in0=mask[:], scalar=ZONE_HIGH, in1=ex[:],
                                          op0=ALU.is_le, op1=ALU.mult))
            dve.wait_ge(rt_exp, after(rt_exp, 3))
            link(dve.tensor_tensor(wz[:], wz[:], ex[:], ALU.mult))
            link(dve.tensor_reduce(rsm[0][:], wz[:], AX_X, ALU.add))
            lo_f = [P, NT, E, E]
            fb_e = fb[:].rearrange("p t (e o) -> p t e o", o=1).broadcast_to(lo_f)
            fb_f = fb[:].rearrange("p t (o f) -> p t o f", o=1).broadcast_to(lo_f)
            link(dve.tensor_tensor(rc[0][:], fb_f, fb_e, ALU.is_gt))
            link(dve.tensor_tensor(rc[1][:], fb_f, fb_e, ALU.is_equal))
            link(dve.tensor_tensor(rc[1][:], rc[1][:], earl[:].rearrange("p (o e) f -> p o e f", o=1)
                                   .broadcast_to(lo_f), ALU.mult))
            link(dve.tensor_tensor(rc[0][:], rc[0][:], rc[1][:], ALU.add))
            link(dve.tensor_reduce(mask[:], rc[0][:], AX_X, ALU.add))
            link(dve.scalar_tensor_tensor(out=fb[:], in0=mask[:], scalar=1.5, in1=fb[:], op0=ALU.is_lt,
                                          op1=ALU.mult))
            link(dve.tensor_reduce(rsm[1][:], fb[:], AX_X, ALU.add))
            link(dve.tensor_scalar(rsm[1][:], rsm[1][:], 1e-8, None, ALU.max))
            link(dve.reciprocal(rsm[2][:], rsm[1][:]))
            link(dve.tensor_tensor(fb[:], fb[:], per_token(rsm[2]), ALU.mult))
            link(dve.tensor_scalar(rsm[1][:], rsm[0][:], 1e-8, None, ALU.is_lt))
            link(dve.tensor_scalar(rsm[2][:], rsm[0][:], 1e-8, None, ALU.is_ge))
            link(dve.tensor_tensor(fb[:], fb[:], per_token(rsm[1]), ALU.mult))
            link(dve.tensor_tensor(wz[:], wz[:], per_token(rsm[2]), ALU.mult))
            link(dve.tensor_tensor(wz[:], wz[:], fb[:], ALU.add))
            link(dve.tensor_reduce(rsm[0][:], wz[:], AX_X, ALU.add))
            link(dve.tensor_scalar(rsm[0][:], rsm[0][:], 1e-8, None, ALU.max))
            link(dve.reciprocal(rsm[1][:], rsm[0][:]))
            link(dve.tensor_tensor(wz[:], wz[:], per_token(rsm[1]), ALU.mult))
            link(dve.tensor_copy(wp[:, :, 0, :], wz[:]))
            link(dve.tensor_tensor(fb[:], wz[:], wp[:, :, 0, :], ALU.subtract))
            link(dve.tensor_copy(wp[:, :, 1, :], fb[:]))
            link(dve.tensor_tensor(wp[:, :, 2, :], fb[:], wp[:, :, 1, :], ALU.subtract))
            assert did[0] == RT_PARTS, did[0]
            dve.wait_ge(wt_done, after(wt_done, 1))
            for j in range(2):
                dve.tensor_copy(wt[:, 8 * P * j:8 * P * (j + 1)], bk[6 + j][0:3 * E, :].bitcast(BF16)
                                ).then_inc(wt_ready, 1)

            def weigh(g, e):
                dve.wait_ge(silu_done, after(silu_done, E * g + e + 1))
                dve.wait_ge(wb_done, after(wb_done, E * g + e + 1))
                dve.wait_ge(hh_ready, after(hh_ready, E * g + e))
                dve.tensor_tensor(sw[:], sg[e % 2][:], bk[4 + e % 2][:], ALU.mult).then_inc(sw_done, 1)
                dve.wait_ge(sw_done, after(sw_done, E * g + e + 1))
                dve.wait_ge(up_done, after(up_done, E * g + e + 1))
                dve.wait_ge(down_done, after(down_done, E * g + e - 1)) if e else dve.wait_ge(down_done, after(down_done, E * g))
                dve.tensor_tensor(hh[e % 2][:], sw[:], bk[2 + e % 2][:], ALU.mult).then_inc(hh_ready, 1)

            with dve.Fori(0, NG // 2) as i:
                for n in range(2):
                    g = 2 * i + n
                    for e in range(E):
                        weigh(g, e)
                    dve.wait_ge(down_done, after(down_done, E * g + E))
                    dve.wait_ge(out_stored, after(out_stored, 16 * 2 * i))
                    gb = modb[:, ds(2 * g, 2), GB:GB + 1, :].broadcast_to([P, 2, TPB, D])
                    fin_v = fin[n][:].rearrange("p (b k) d -> p b k d", b=2)
                    dve.tensor_tensor(fin_v, bk[6][:].rearrange("p (b k d) -> p b k d", b=2, k=TPB), gb, ALU.mult
                                      ).then_inc(fin_step, 1)
                    dve.wait_ge(fin_step, after(fin_step, 2 * g + 1))
                    dve.tensor_tensor(fin[n][:], fin[n][:], xs[:, ds(GT * g, GT), :], ALU.add
                                      ).then_inc(fin_step, 1)


RT_DIST = 6
RT_PARTS = 32


def kernel(**inputs):
    import numpy as np
    import concourse.bacc as bacc
    from concourse.bass_utils import run_bass_kernel_spmd

    a = {k.removeprefix("L0_").removeprefix("attn_").removeprefix("ffn_"): np.asarray(v)
         for k, v in inputs.items()}
    ramp = np.linspace(0.0, 1.0, WIN // 2, dtype=np.float32)
    alpha = np.ones((2, WIN, 2, 2, 2), np.float32)
    vmask = np.ones((P, 2, 2), np.float32)
    for sel in range(2):
        for eo in range(2):
            for half in range(2):
                w = 4 * sel + 2 * half + eo
                if w > 0:
                    alpha[:, :WIN // 2, eo, sel, half] = ramp
                if w < S // (WIN // 2) - 1:
                    alpha[:, WIN // 2:, eo, sel, half] = 1 - ramp
    vmask[:PAD, 0, 0] = 0
    vmask[P - PAD:, 1, 1] = 0
    mones = np.zeros((2, 2, P), np.float32)
    mones[:, 0, :WIN] = 1
    mones[:, 1, WIN:] = 1
    selw = np.zeros((3, E, E, P), np.float32)
    for e in range(E):
        selw[:, e, e, :] = 1
    wmod = a["wmod"].reshape(D, 6, D)[:, [1, 0, 2, 5, 3, 4], :].reshape(D, 6 * D)
    arrays = {
        "x": a["hidden_states"],
        "wqkvp": np.concatenate([a["wq"], a["wk"], a["wv"], a["wproj"]], axis=1),
        "w1": a["w1"], "w2": a["w2"], "wg": a["Wg"], "wu": a["Wu"], "wd": a["Wd"], "wr": a["Wr"],
        "temp": a["temperature"],
        "c_t": a["c"].T, "wmod": wmod,
        "cols": np.stack([a["ln1_g"], a["ln1_b"], a["bq"], a["bk"], a["bv"], a["ln2_g"], a["ln2_b"],
                          *a["b1"].reshape(FF, P)], axis=1),
        "rows": np.concatenate([a["bproj"], a["b2"]])[None],
        "ident": np.eye(P, dtype=np.float32),
        "alpha": alpha.reshape(P, 2, 4),
        "vmask": vmask,
        "mones": mones.reshape(4, P),
        "selw": selw.reshape(3 * E, E, P),
        "earlier": np.tril(np.ones((E, E), np.float32), -1)[None],
    }
    arrays = {f"in_{k}": np.ascontiguousarray(v) for k, v in arrays.items()}
    nc = bacc.Bacc("TRN2", target_bir_lowering=False, num_devices=1)
    args = [nc.dram_tensor(k, v.shape, mybir.dt.from_np(v.dtype), kind="ExternalInput").ap()
            for k, v in arrays.items()]
    args.append(nc.dram_tensor("out_x", (B, S, D), F32, kind="ExternalOutput").ap())
    build(nc, *args)
    return run_bass_kernel_spmd(nc, [arrays], core_ids=[0]).results[0]["out_x"]
```

```python
from contextlib import ExitStack

import concourse.bass as bass
from concourse import mybir
from concourse.alu_op_type import AluOpType as ALU

F32 = mybir.dt.float32
BF16 = mybir.dt.bfloat16
F32R = mybir.dt.float32r
ACT = mybir.ActivationFunctionType
AX_X = mybir.AxisListType.X

P = 128
B, S, D = 8, 256, 128
TPB = S // P
NT = B * TPB
NH, HD = 16, 8
H2 = NH // 2
WIN = 64
PAD = WIN // 4
LINE = S + 2 * PAD
TERMS = 6
ROWS = HD * TERMS
VC = 2 * HD
FF = 4
E = 8
GT = 4
NG = NT // GT
GW = GT * P
LAG = 6
PIECES = 4
EPS = 1e-5
SCALE = float(HD) ** -0.5
CA, SA, GA, GB = range(4)
LN1G, LN1B, BQ, BK, BV, LN2G, LN2B, B1 = range(8)
ZONE_MID = 0.36787944117144233
ZONE_LOW = 0.21231792754821915
ZONE_HIGH = 0.5


def build(nc, x, wqkvp, w1, w2, wg, wu, wd, wr, temp, c_t, wmod, cols, rows, ident, alpha, vmask,
          mones, earlier, out):
    ctx = ExitStack()

    def sb(name, shape, dt=F32):
        return ctx.enter_context(nc.sbuf_tensor(name, shape, dt))

    def sem(name):
        return ctx.enter_context(nc.semaphore(name))

    ahead_by = {}

    def counts_from(s, n):
        ahead_by[s.name] = n
        return s

    def after(s, n):
        return (max(n, 0) if isinstance(n, int) else n) + ahead_by.get(s.name, 0)

    def apart(eng):
        eng.sem_inc(waits_met, 1)

    def ds(i, n):
        return slice(i, i + n) if isinstance(i, int) else bass.ds(i, n)

    with ctx:
        wa = sb("wa", [P, 4, D])
        w1s = sb("w1s", [P, FF, P])
        w2s = sb("w2s", [P, FF, D])
        wgs = sb("wgs", [P, E, P])
        wus = sb("wus", [P, E, P])
        wds = sb("wds", [P, E, D])
        wrs = sb("wrs", [P, E])
        temps = sb("temps", [P, 1])
        rtemp = sb("rtemp", [P, 1])
        cts = sb("cts", [P, B])
        wms = sb("wms", [P, 6, D])
        col = sb("col", [P, 7 + FF])
        row = sb("row", [P, 2, D])
        idf = sb("idf", [P, P])
        idb = sb("idb", [P, P], BF16)
        alph = sb("alph", [P, 2, 4])
        vmsk = sb("vmsk", [P, 2, 2])
        monesf = sb("monesf", [4, P])
        monesb = sb("monesb", [4, P], BF16)
        earl = sb("earl", [P, E, E])
        bqs = sb("bqs", [P, 1])
        mhalf = sb("mhalf", [P, NT])
        sce = sb("sce", [P, 4, B])
        scb = sb("scb", [P, B, P])
        modb = sb("modb", [P, B, 4, D])
        modt = sb("modt", [P, 2, B])
        xs = sb("xs", [P, NT, D])
        res = sb("res", [P, NT, D])
        st = sb("st", [P, GT, 6])
        mv = sb("mv", [P, GT, 2])
        ve = sb("ve", [P, GT])
        rs = sb("rs", [P, GT])
        xh = sb("xh", [P, TPB, D])
        h1 = sb("h1", [P, TPB, D])
        x1h = sb("x1h", [P, TPB, D])
        x1t = [sb(f"x1t{i}", [P, LINE]) for i in range(2)]
        x1v = [sb(f"x1v{i}", [P, LINE]) for i in range(2)]
        qk = sb("qk", [P, 2, LINE])
        qkr = sb("qkr", [P, 2, LINE])
        parts = sb("parts", [P, 3, 2, LINE], BF16)
        qst = [sb(f"qst{i}", [P, H2, LINE], BF16) for i in range(2)]
        kst = [sb(f"kst{i}", [P, H2, LINE], BF16) for i in range(2)]
        nm = sb("nm", [P, 8, H2])
        mp = sb("mp", [P, 2, 4 * H2], BF16)
        mt = sb("mt", [2 * 4 * H2, P], BF16)
        prob = [sb(f"prob{i}", [P, H2, 2, WIN]) for i in range(2)]
        pvs = sb("pvs", [P, H2 // 2, P])
        rsum = sb("rsum", [P, H2, 4])
        fac = sb("fac", [P, H2, 4])
        ctxn = sb("ctxn", [P, 2, 2, D])
        ctxt = sb("ctxt", [P, S])
        xh2 = [sb(f"xh2{i}", [P, GT, D]) for i in range(2)]
        h2t = sb("h2t", [P, NT * P])
        gt = sb("gt", [P, FF, GW])
        resb = sb("resb", [P, GT, D])
        comb = sb("comb", [P, GT, D])
        h3t = sb("h3t", [P, NT * P])
        rt = [sb(f"rt{i}", [P, NT, E]) for i in range(5)]
        rc = [sb(f"rc{i}", [P, NT, E, E]) for i in range(2)]
        rsm = [sb(f"rsm{i}", [P, NT]) for i in range(3)]
        sg = [sb(f"sg{i}", [P, GW]) for i in range(2)]
        hh = [sb(f"hh{i}", [P, GW]) for i in range(E)]
        acc = sb("acc", [P, GT, D])
        fin = sb("fin", [P, GT, D])

        with ExitStack() as attention:
            mrow = [attention.enter_context(nc.sbuf_tensor(f"mrow{i}", [4, 8 * H2, WIN], BF16)) for i in range(2)]
            vb = [attention.enter_context(nc.sbuf_tensor(f"vb{i}", [P, 2, NH, 2, 2, VC], F32)) for i in range(2)]
        wpart = sb("wpart", [P, 2, E, P], F32R)
        wrest = sb("wrest", [P, 2, E, P], F32R)
        h3part = sb("h3part", [P, NT * P], F32R)
        h3rest = sb("h3rest", [P, NT * P], F32R)

        bk = [ctx.enter_context(nc.psum_tensor(f"bank{i}", [P, 512], F32)) for i in range(8)]
        psa, psb, (psv, pst), (w0b, w1b) = bk[0:2], bk[2:4], bk[4:6], bk[6:8]

        scr = nc.dram_tensor("stack_scratch", [B, P, TERMS, 2, LINE], BF16, kind="Internal").ap()
        scr_rows = scr.rearrange("b (r h d) t k n -> b r k (d t) h n", r=2, h=H2)

        waits_met = sem("waits_met")
        x_first, x_rest = sem("x_first"), sem("x_rest")
        c_loaded, small_loaded, wa_loaded = sem("c_loaded"), sem("small_loaded"), sem("wa_loaded")
        late_loaded = sem("late_loaded")
        consts = sem("consts")
        consts_pool = sem("consts_pool")
        sc_step, sc_exp = sem("sc_step"), sem("sc_exp")
        scb_ready = sem("scb_ready")
        mod_done = sem("mod_done")
        mod_ready = sem("mod_ready")
        modt_done, modt_ready = sem("modt_done"), sem("modt_ready")
        ln_dve, ln_pool = sem("ln_dve"), sem("ln_pool")
        xt_done = sem("xt_done")
        x1t_ready = sem("x1t_ready")
        x1v_ready = sem("x1v_ready")
        qk_done, qk_ready = sem("qk_done"), sem("qk_ready")
        parts_step = sem("parts_step")
        q_written, k_written = sem("q_written"), sem("k_written")
        stack_ready = sem("stack_ready")
        v_done, v_ready = sem("v_done"), sem("v_ready")
        a_done, max_done = sem("a_done"), sem("max_done")
        mp_step = sem("mp_step")
        mt_done, mt_ready = sem("mt_done"), sem("mt_ready")
        mrow_ready = sem("mrow_ready")
        b_done, exp_done = sem("b_done"), sem("exp_done")
        pv_done = sem("pv_done")
        pvs_ready, pt_done = sem("pvs_ready"), sem("pt_done")
        norm_step = sem("norm_step")
        ctx_done, ctxt_ready = sem("ctx_done"), sem("ctxt_ready")
        proj_done, att_ready = sem("proj_done"), sem("att_ready")
        ln2_step, ln2_root = sem("ln2_step"), sem("ln2_root")
        gate_step = sem("gate_step")
        xh2_ready = sem("xh2_ready")
        t2_done, h2t_ready = sem("t2_done"), sem("h2t_ready")
        w1_done, gelu_done = sem("w1_done"), sem("gelu_done")
        w2_done = sem("w2_done")
        resb_ready = sem("resb_ready")
        comb_step = sem("comb_step")
        ln3_step, ln3_root = sem("ln3_step"), sem("ln3_root")
        t3_done, h3t_ready = sem("t3_done"), sem("h3t_ready")
        h3rest_ready = sem("h3rest_ready")
        wpart_ready, wrest_ready = sem("wpart_ready"), sem("wrest_ready")
        router_done = sem("router_done")
        rt_step, rt_exp = sem("rt_step"), sem("rt_exp")
        gate_done, up_done = sem("gate_done"), sem("up_done")
        silu_done, hh_ready = sem("silu_done"), sem("hh_ready")
        down_done = sem("down_done")
        acc_step = sem("acc_step")
        fin_step = sem("fin_step")
        out_stored = sem("out_stored")

        ahead = [att_ready, ctxt_ready, proj_done, ctx_done, norm_step, exp_done, pv_done, pvs_ready, pt_done,
                 h2t_ready, t2_done]
        for s in ahead:
            counts_from(s, 1)
        counts_from(out_stored, 16)

        def finish(eng, g):
            eng.wait_ge(acc_step, after(acc_step, GT * E * (g + 1)))
            eng.wait_ge(out_stored, after(out_stored, 16 * g))
            gb = modb[:, ds(2 * g, 2), GB:GB + 1, :].broadcast_to([P, 2, TPB, D])
            eng.tensor_tensor(fin[:].rearrange("p (b k) d -> p b k d", b=2),
                              acc[:].rearrange("p (b k) d -> p b k d", b=2), gb, ALU.mult).then_inc(fin_step, 1)
            eng.wait_ge(fin_step, after(fin_step, 2 * g + 1))
            eng.tensor_tensor(fin[:], fin[:], xs[:, ds(GT * g, GT), :], ALU.add).then_inc(fin_step, 1)

        block = ctx.enter_context(nc.Block())

        def group_normed(norm, prep, ahead):
            return None if norm else 0 if prep else 1 if ahead else 2

        def steps(eng, step):
            with eng.Fori(0, (B - 4) // 2) as i:
                for n in range(2):
                    step(2 * i + n, n, True, True, True)
            step(B - 4, 0, True, True, True)
            step(B - 3, 1, False, True, True)
            step(B - 2, 0, False, False, True)
            step(B - 1, 1, False, False, False)

        @block.sync
        def _(sp):
            def write_parts(b):
                sp.wait_ge(parts_step, after(parts_step, 3 * (b + 1)))
                apart(sp)
                dst = scr[ds(b, 1)].rearrange("b p t k n -> (b p) t k n")
                for t0, n, k, src in ((0, 3, 0, parts[:, 0:1, 0, :].broadcast_to([P, 3, LINE])),
                                      (3, 2, 0, parts[:, 1:2, 0, :].broadcast_to([P, 2, LINE])),
                                      (5, 1, 0, parts[:, 2:3, 0, :]),
                                      (0, 3, 1, parts[:, :, 1, :]),
                                      (3, 2, 1, parts[:, 0:2, 1, :]),
                                      (5, 1, 1, parts[:, 0:1, 1, :])):
                    sp.dma_start(dst[:, t0:t0 + n, k, :], src).then_inc((q_written, k_written)[k], 16)

            def read_stacks(b, n):
                sp.wait_ge(b_done, after(b_done, 8 * (b - 1)))
                apart(sp)
                for k, (stack, written) in enumerate(((qst[n], q_written), (kst[n], k_written))):
                    sp.wait_ge(written, after(written, 48 * (b + 1)))
                    apart(sp)
                    for r in range(2):
                        src = scr_rows[ds(b, 1), r, k].rearrange("b r h n -> (b r) h n")
                        sp.dma_start(stack[64 * r:64 * r + ROWS], src).then_inc(stack_ready, 16)

            def write_mrow(b, n, hf):
                sp.wait_ge(mt_ready, after(mt_ready, 2 * b + hf + 1))
                apart(sp)
                for part in range(2):
                    for half in range(2):
                        r = 2 * part + half
                        sp.dma_start(mrow[n][r:r + 1, 32 * hf:32 * hf + 32, :],
                                     mt[32 * part:32 * part + 32, WIN * half:WIN * half + WIN]
                                     ).then_inc(mrow_ready, 16)

            x_v = x.rearrange("b (k p) d -> p (b k) d", p=P)
            sp.dma_start(xs[:, 0:2], x_v[:, 0:2]).then_inc(x_first, 16)
            sp.dma_start(cts[:], c_t).then_inc(c_loaded, 16)
            sp.dma_start(wms[:], wmod.rearrange("p (c d) -> p c d", c=6)).then_inc(c_loaded, 16)
            for dst, src in ((col, cols), (row, rows.rearrange("o (r d) -> o r d", r=2).broadcast_to([P, 2, D])),
                             (idf, ident)):
                sp.dma_start(dst[:], src).then_inc(small_loaded, 16)
            sp.dma_start(xs[:, 2:NT], x_v[:, 2:NT]).then_inc(x_rest, 16)
            sp.dma_start(wa[:], wqkvp.rearrange("p (c d) -> p c d", c=4)).then_inc(wa_loaded, 16)
            for dst, src in ((alph, alpha), (vmsk, vmask), (monesf, mones)):
                sp.dma_start(dst[:], src).then_inc(small_loaded, 16)

            write_parts(0)
            read_stacks(0, 0)
            write_parts(1)
            write_mrow(0, 0, 0)
            read_stacks(1, 1)
            for dst, src in ((w1s, w1.rearrange("p (c d) -> p c d", c=FF)),
                             (w2s, w2.rearrange("(c p) d -> p c d", p=P)),
                             (wgs, wg.rearrange("e p i -> p e i")), (wus, wu.rearrange("e p i -> p e i")),
                             (wds, wd.rearrange("e p i -> p e i")), (wrs, wr),
                             (temps, temp.rearrange("(o n) -> o n", o=1).broadcast_to([P, 1])),
                             (earl, earlier.rearrange("o e f -> o e f").broadcast_to([P, E, E]))):
                sp.dma_start(dst[:], src).then_inc(late_loaded, 16)

            def step(b, n, norm, prep, ahead):
                write_mrow(b, n, 1)
                if ahead:
                    write_mrow(b + 1, 1 - n, 0)
                if prep:
                    write_parts(b + 2)
                    read_stacks(b + 2, n)

            steps(sp, step)

            out_v = out.rearrange("b (k p) d -> p (b k) d", p=P)
            with sp.Fori(0, NG) as g:
                sp.wait_ge(fin_step, after(fin_step, 2 * g + 2))
                apart(sp)
                sp.dma_start(out_v[:, ds(GT * g, GT)], fin[:]).then_inc(out_stored, 16)
            sp.wait_ge(out_stored, after(out_stored, 16 * NG))

        @block.tensor
        def _(pe):
            def modulation(b, bank):
                pe.wait_ge(scb_ready, after(scb_ready, 1 if b < 2 else 2))
                if b == 6:
                    pe.wait_ge(mod_ready, after(mod_ready, 2 * (b - 1)))
                pe.matmul(bank[:], scb[:, b, :], wms[:, 0:4, :], start=True, stop=True).then_inc(mod_done, 1)

            def transpose_x(b):
                pe.wait_ge(ln_dve, after(ln_dve, 14 * (b + 1)))
                for k in range(TPB):
                    m = pe.transpose(w0b[:, k * P:(k + 1) * P], x1h[:, k, :], idf[:])
                m.then_inc(xt_done, 1)

            def project_qk(b, n):
                pe.wait_ge(x1t_ready, after(x1t_ready, 2 * (b + 1)))
                pe.matmul(w0b[:, 0:LINE], wa[:, 0, :], x1t[n][:], start=True, stop=True)
                pe.matmul(w1b[:, 0:LINE], wa[:, 1, :], x1t[n][:], start=True, stop=True
                          ).then_inc(qk_done, 1)

            def project_v(b, n, eo):
                pe.wait_ge(x1v_ready, after(x1v_ready, b + 1))
                for sel in range(2):
                    j, at = 2 * eo + sel, 32 * eo + P * sel
                    m = pe.matmul(w0b[:, j * P:(j + 1) * P], x1v[n][:, at:at + P], wa[:, 2, :],
                                  start=True, stop=True)
                m.then_inc(v_done, 1)

            def spans(g):
                eo, par, sel = g // 4, g // 2 % 2, g % 2
                return par, [(half, 32 * (4 * sel + 2 * half + eo)) for half in range(2)]

            def scores_a(b, n, g):
                pe.wait_ge(stack_ready, after(stack_ready, 64 * (b + 1)))
                if g == 0:
                    pe.wait_ge(mt_ready, after(mt_ready, 2 * b))
                else:
                    pe.wait_ge(max_done, after(max_done, 8 * b + g - 1))
                apart(pe)
                par, halves = spans(g)
                rows_ = slice(64 * par, 64 * par + ROWS)
                for h2 in range(H2):
                    for half, at in halves:
                        m = pe.matmul(psa[g % 2][WIN * half:WIN * half + WIN, WIN * h2:WIN * h2 + WIN],
                                      qst[n][rows_, h2, at:at + WIN], kst[n][rows_, h2, at:at + WIN],
                                      start=True, stop=True)
                m.then_inc(a_done, 1)

            def scores_b(b, n, g):
                pe.wait_ge(mrow_ready, after(mrow_ready, 128 * b + 64 * (g // 4 + 1)))
                if g:
                    pe.wait_ge(exp_done, after(exp_done, 8 * b + g - 1))
                par, halves = spans(g)
                bank = psb[g % 2]
                pe.matmul(bank[:], monesb[:], mrow[n][:, H2 * g:H2 * g + H2, :], start=True, stop=False,
                          skip_group_check=True)
                rows_ = slice(64 * par, 64 * par + ROWS)
                for h2 in range(H2):
                    for half, at in halves:
                        m = pe.matmul(bank[WIN * half:WIN * half + WIN, WIN * h2:WIN * h2 + WIN],
                                      kst[n][rows_, h2, at:at + WIN], qst[n][rows_, h2, at:at + WIN],
                                      start=False, stop=True, skip_group_check=True)
                m.then_inc(b_done, 1)

            def transpose_m(b, hf, bank):
                pe.wait_ge(mp_step, after(mp_step, 4 * b + 2 * hf + 2))
                apart(pe)
                pe.transpose(bank[0:64, 0:64].bitcast(BF16), mp[:].rearrange("p a c -> p (a c)"), idb[:]
                             ).then_inc(mt_done, 1)

            def probs_v(b, n, gp):
                pe.wait_ge(exp_done, after(exp_done, 8 * b + 2 * gp + 2))
                pe.wait_ge(v_ready, after(v_ready, 4 * (b + 1)))
                pe.wait_ge(pvs_ready, after(pvs_ready, 4 * b + gp))
                eo, par = gp // 2, gp % 2
                for h2 in range(H2):
                    m = pe.matmul(psv[WIN * (h2 % 2):WIN * (h2 % 2) + WIN, P * (h2 // 2):P * (h2 // 2) + P],
                                  vb[n][:, eo, H2 * par + h2, :, :, :], prob[gp % 2][:, h2, :, :],
                                  start=True, stop=True)
                m.then_inc(pv_done, 1)

            def turn_sums(b, gp):
                pe.wait_ge(pvs_ready, after(pvs_ready, 4 * b + gp + 1))
                pe.wait_ge(norm_step, after(norm_step, 4 * (4 * b + gp)))
                for k in range(H2 // 2):
                    m = pe.transpose(pst[:, k * P:(k + 1) * P], pvs[:, k, :], idf[:])
                m.then_inc(pt_done, 1)

            def gather_context(b):
                pe.wait_ge(norm_step, after(norm_step, 16 * (b + 1)))
                for eo in range(2):
                    for half in range(2):
                        at = 32 * eo + WIN * half
                        dst = w1b[:, at:at + 2 * P].rearrange("p (s q) -> p s q", s=2)[:, :, 0:WIN]
                        m = pe.matmul(dst, ctxn[:, eo, half, :], idf[:], start=(eo == half == 0), stop=True,
                                      skip_group_check=True)
                m.then_inc(ctx_done, 1)

            def project_out(b):
                pe.wait_ge(ctxt_ready, after(ctxt_ready, b + 1))
                for k in range(TPB):
                    m = pe.matmul(w1b[:, k * P:(k + 1) * P], ctxt[:, k * P:(k + 1) * P], wa[:, 3, :],
                                  start=True, stop=True)
                m.then_inc(proj_done, 1)

            def turn_tokens(g):
                pe.wait_ge(xh2_ready, after(xh2_ready, g + 1))
                if g == 0:
                    pe.wait_ge(mt_ready, after(mt_ready, 2 * B))
                elif g == 1:
                    pe.wait_ge(max_done, after(max_done, 8 * B))
                else:
                    pe.wait_ge(h2t_ready, after(h2t_ready, g - 1))
                for k in range(GT):
                    m = pe.transpose(psa[g % 2][:, k * P:(k + 1) * P], xh2[g % 2][:, k, :], idf[:])
                m.then_inc(t2_done, 1)

            def first(g, c):
                pe.wait_ge(h2t_ready, after(h2t_ready, g + 1))
                if g:
                    pe.wait_ge(gelu_done, after(gelu_done, FF * (g - 1) + c + 1))
                elif c < 2:
                    pe.wait_ge(exp_done, after(exp_done, 8 * B))
                elif c == 2:
                    pe.wait_ge(norm_step, after(norm_step, 16 * B))
                pe.matmul(bk[2 + c][:], w1s[:, c, :], h2t[:, GW * g:GW * (g + 1)], start=True, stop=True
                          ).then_inc(w1_done, 1)

            for s in ahead:
                pe.sem_inc(s, 1)
            pe.sem_inc(out_stored, 16)
            pe.wait_ge(c_loaded, after(c_loaded, 32))
            modulation(0, bk[0])
            modulation(1, bk[1])
            pe.wait_ge(sc_step, after(sc_step, 3))
            for j in range(2):
                m = pe.matmul(w0b[:, B * j:B * j + B], wms[:, 4 + j, :], sce[:, 3, :], start=True, stop=True)
            m.then_inc(modt_done, 1)
            modulation(2, bk[2])
            pe.wait_ge(small_loaded, after(small_loaded, 96))
            pe.wait_ge(wa_loaded, after(wa_loaded, 16))
            pe.wait_ge(consts, after(consts, 3))
            pe.wait_ge(modt_ready, after(modt_ready, 2))
            transpose_x(0)
            project_qk(0, 0)
            modulation(3, bk[3])
            pe.wait_ge(qk_ready, after(qk_ready, 4))
            transpose_x(1)
            project_qk(1, 1)
            modulation(4, bk[4])
            pe.wait_ge(qk_ready, after(qk_ready, 8))
            project_v(0, 0, 0)
            project_v(0, 0, 1)
            for g in range(5):
                scores_a(0, 0, g)
            transpose_m(0, 0, w1b)
            for g in range(5, 8):
                scores_a(0, 0, g)
            pe.wait_ge(v_ready, after(v_ready, 4))
            project_v(1, 1, 0)
            project_v(1, 1, 1)
            modulation(5, bk[5])
            modulation(6, bk[4])
            pe.wait_ge(mt_ready, after(mt_ready, 1))
            modulation(7, w1b)
            scores_b(0, 0, 0)
            scores_b(0, 0, 1)
            pe.wait_ge(mod_ready, after(mod_ready, 2 * B))

            def step(b, n, norm, prep, ahead):
                def a(g):
                    if ahead:
                        scores_a(b + 1, 1 - n, g)

                scores_b(b, n, 2)
                pe.wait_ge(max_done, after(max_done, 8 * (b + 1)))
                transpose_m(b, 1, psa[0])
                probs_v(b, n, 0)
                scores_b(b, n, 3)
                a(0)
                turn_sums(b, 0)
                a(1)
                if prep:
                    pe.wait_ge(v_ready, after(v_ready, 4 * (b + 2)))
                    transpose_x(b + 2)
                a(2)
                if not ahead:
                    turn_tokens(0)
                probs_v(b, n, 1)
                if prep:
                    pe.wait_ge(att_ready, after(att_ready, b))
                    project_qk(b + 2, n)
                a(3)
                scores_b(b, n, 4)
                scores_b(b, n, 5)
                turn_sums(b, 1)
                a(4)
                if ahead:
                    if prep:
                        pe.wait_ge(qk_ready, after(qk_ready, 4 * (b + 3)))
                    else:
                        pe.wait_ge(v_ready, after(v_ready, 4 * (b + 2)))
                        pe.wait_ge(att_ready, after(att_ready, b))
                    transpose_m(b + 1, 0, w1b)
                else:
                    turn_tokens(1)
                probs_v(b, n, 2)
                scores_b(b, n, 6)
                a(5)
                scores_b(b, n, 7)
                turn_sums(b, 2)
                a(6)
                if not ahead:
                    turn_tokens(2)
                probs_v(b, n, 3)
                if ahead:
                    scores_b(b + 1, 1 - n, 0)
                else:
                    pe.wait_ge(late_loaded, after(late_loaded, 128))
                    first(0, 0)
                turn_sums(b, 3)
                if prep:
                    project_v(b + 2, n, 0)
                    project_v(b + 2, n, 1)
                if ahead:
                    pe.wait_ge(mt_ready, after(mt_ready, 2 * b + 3))
                else:
                    first(0, 1)
                    pe.wait_ge(att_ready, after(att_ready, b))
                a(7)
                gather_context(b)
                if ahead:
                    scores_b(b + 1, 1 - n, 1)
                else:
                    first(0, 2)
                project_out(b)

            steps(pe, step)

            def second(g, c):
                if c == 0 and g:
                    pe.wait_ge(comb_step, after(comb_step, 3 * g - 2))
                pe.wait_ge(gelu_done, after(gelu_done, FF * g + c + 1))
                for k in range(GT):
                    m = pe.matmul(bk[6][:, k * P:(k + 1) * P], gt[:, c, k * P:(k + 1) * P], w2s[:, c, :],
                                  start=(c == 0 and k == 0), stop=(c == FF - 1), skip_group_check=True)
                m.then_inc(w2_done, 1)

            def turn_normed(g, bank):
                pe.wait_ge(ln3_step, after(ln3_step, 13 * (g + 1)))
                if g < 2:
                    pe.wait_ge(h2t_ready, after(h2t_ready, NG))
                for k in range(GT):
                    m = pe.transpose(bank[:, k * P:(k + 1) * P], xh2[g % 2][:, k, :], idf[:])
                m.then_inc(t3_done, 1)

            def router(g):
                pe.wait_ge(h3t_ready, after(h3t_ready, 4 * (g + 1)))
                for k in range(GT):
                    t = GT * g + k
                    m = pe.matmul(bk[7][:, E * t:E * t + E], h3t[:, t * P:(t + 1) * P], wrs[:], start=True, stop=True)
                m.then_inc(router_done, 1)

            def by_parts(bank, w, g, e):
                tokens, tokens_rest = h3part[:, ds(GW * g, GW)], h3rest[:, ds(GW * g, GW)]
                pe.matmul(bank[:], wpart[:, w, e, :], tokens_rest, start=True, stop=False)
                pe.matmul(bank[:], wrest[:, w, e, :], tokens, start=False, stop=False)
                return pe.matmul(bank[:], wpart[:, w, e, :], tokens, start=False, stop=True)

            def gate_up(g, e):
                u = E * g + e
                if e == 0:
                    pe.wait_ge(h3rest_ready, after(h3rest_ready, g + 1))
                pe.wait_ge(silu_done, after(silu_done, u - 1))
                by_parts(bk[e % 2], 0, g, e).then_inc(gate_done, 1)
                pe.wait_ge(hh_ready, after(hh_ready, u - 1))
                by_parts(bk[2 + e % 2], 1, g, e).then_inc(up_done, 1)

            def down(u, e):
                pe.wait_ge(hh_ready, after(hh_ready, u + 1))
                pe.wait_ge(acc_step, after(acc_step, GT * (u - 1)))
                for k in range(GT):
                    m = pe.matmul(bk[4 + e % 2][:, k * P:(k + 1) * P], hh[e][:, k * P:(k + 1) * P], wds[:, e, :],
                                  start=True, stop=True)
                m.then_inc(down_done, 1)

            first(0, 3)
            for g in range(NG):
                for c in range(FF):
                    if g < NG - 1:
                        first(g + 1, c)
                    second(g, c)
                    if c == 2 and g == NG - 1:
                        router(1)
                if g == 0:
                    turn_tokens(NG - 1)
                elif g < NG - 1:
                    turn_normed(g - 1, psa[g - 1])
                if g == 2:
                    router(0)

            pe.wait_ge(wrest_ready, after(wrest_ready, PIECES))
            for u in range(E * NG):
                gate_up(u // E, u % E)
                for v in downs_after(u):
                    down(v, v % E)
                if u == 1:
                    turn_normed(NG - 2, bk[4])
                elif u == 3:
                    router(NG - 2)
                elif u == E + 3:
                    turn_normed(NG - 1, bk[6])
                elif u == E + 5:
                    router(NG - 1)

        @block.scalar
        def _(act):
            def copy_mod(b, bank):
                act.wait_ge(mod_done, after(mod_done, b + 1))
                act.activation(modb[:, ds(b, 1), CA, :], bank[:, 0:D], ACT.Identity, bias=1.0).then_inc(mod_ready, 1)
                act.activation(modb[:, ds(b, 1), SA:, :], bank[:, D:4 * D], ACT.Copy).then_inc(mod_ready, 1)

            def copy_xt(b, n):
                act.wait_ge(xt_done, after(xt_done, b + 1))
                act.wait_ge(qk_done, after(qk_done, b - 1))
                act.activation(x1t[n][:, PAD:PAD + S], w0b[:, 0:S], ACT.Identity, bias=col[:, LN1B:LN1B + 1],
                               scale=col[:, LN1G:LN1G + 1]).then_inc(x1t_ready, 1)
                ends = w0b[:, 0:2 * (S - PAD)].rearrange("p (a c) -> p a c", a=2)[:, :, 0:PAD]
                pads = x1t[n][:].rearrange("p (a c) -> p a c", a=2)
                act.activation(pads[:, 0, 0:PAD], ends[:, 0, :], ACT.Identity, bias=col[:, LN1B:LN1B + 1],
                               scale=col[:, LN1G:LN1G + 1])
                act.activation(pads[:, 1, LINE // 2 - PAD:], ends[:, 1, :], ACT.Identity,
                               bias=col[:, LN1B:LN1B + 1], scale=col[:, LN1G:LN1G + 1]).then_inc(x1t_ready, 1)

            def copy_qk(b):
                act.wait_ge(qk_done, after(qk_done, b + 1))
                act.wait_ge(parts_step, after(parts_step, 3 * b))
                act.wait_ge(q_written, after(q_written, 48 * b))
                act.wait_ge(k_written, after(k_written, 48 * b))
                act.activation(qk[:, 0, :], w0b[:, 0:LINE], ACT.Identity, bias=bqs[:], scale=SCALE
                               ).then_inc(qk_ready, 1)
                act.activation(parts[:, 0, 0, :], w0b[:, 0:LINE], ACT.Identity, bias=bqs[:], scale=SCALE
                               ).then_inc(qk_ready, 1)
                act.activation(qk[:, 1, :], w1b[:, 0:LINE], ACT.Identity, bias=col[:, BK:BK + 1]
                               ).then_inc(qk_ready, 1)
                act.activation(parts[:, 0, 1, :], w1b[:, 0:LINE], ACT.Identity, bias=col[:, BK:BK + 1]
                               ).then_inc(qk_ready, 1)

            def copy_v(b, n):
                act.wait_ge(v_done, after(v_done, 2 * (b + 1)))
                act.wait_ge(pv_done, after(pv_done, 4 * (b - 1)))
                for eo in range(2):
                    for half in range(2):
                        p = slice(WIN * half, WIN * half + WIN)
                        src = w0b[p, 2 * P * eo:2 * P * (eo + 1)].rearrange("p (s h d) -> p s h d", s=2, d=HD)
                        dst = vb[n][p, eo, :, :, half, 0:HD].rearrange("p h s d -> p s h d")
                        act.activation(dst, src, ACT.Copy).then_inc(v_ready, 1)

            def exp(b, n, g):
                act.wait_ge(b_done, after(b_done, 8 * b + g + 1))
                act.wait_ge(pv_done, after(pv_done, 4 * b + g // 2 - 1))
                act.activation(prob[g // 2 % 2][:, :, g % 2, :], psb[g % 2][:].rearrange("p (h q) -> p h q", h=H2),
                               ACT.Exp).then_inc(exp_done, 1)

            def copy_pv(b, gp):
                act.wait_ge(pv_done, after(pv_done, 4 * b + gp + 1))
                act.wait_ge(pt_done, after(pt_done, 4 * b + gp))
                act.activation(pvs[:], psv[:].rearrange("p (k q) -> p k q", q=P), ACT.Copy).then_inc(pvs_ready, 1)

            def copy_h2t(g):
                act.wait_ge(t2_done, after(t2_done, g + 1))
                act.activation(h2t[:, GW * g:GW * (g + 1)], psa[g % 2][:], ACT.Identity,
                               bias=col[:, LN2B:LN2B + 1], scale=col[:, LN2G:LN2G + 1]).then_inc(h2t_ready, 1)

            act.wait_ge(c_loaded, after(c_loaded, 32))
            act.activation(sce[:, 0, :], cts[:], ACT.Exp, scale=-1.0).then_inc(sc_exp, 1)
            copy_mod(0, bk[0])
            copy_mod(1, bk[1])
            act.wait_ge(modt_done, after(modt_done, 1))
            act.activation(modt[:, 0, :], w0b[:, 0:B], ACT.Copy).then_inc(modt_ready, 1)
            act.activation(modt[:, 1, :], w0b[:, B:2 * B], ACT.Identity, bias=1.0).then_inc(modt_ready, 1)
            copy_mod(2, bk[2])
            act.wait_ge(small_loaded, after(small_loaded, 96))
            act.wait_ge(consts, after(consts, 11))
            act.wait_ge(consts_pool, after(consts_pool, 5))
            copy_xt(0, 0)
            copy_qk(0)
            copy_mod(3, bk[3])
            copy_xt(1, 1)
            copy_qk(1)
            copy_mod(4, bk[4])
            copy_v(0, 0)
            copy_v(1, 1)
            copy_mod(5, bk[5])
            copy_mod(6, bk[4])
            copy_mod(7, w1b)
            exp(0, 0, 0)
            exp(0, 0, 1)

            def step(b, n, norm, prep, ahead):
                exp(b, n, 2)
                copy_pv(b, 0)
                exp(b, n, 3)
                if prep:
                    copy_xt(b + 2, n)
                if not ahead:
                    copy_h2t(0)
                copy_pv(b, 1)
                if prep:
                    copy_qk(b + 2)
                exp(b, n, 4)
                exp(b, n, 5)
                if not ahead:
                    copy_h2t(1)
                copy_pv(b, 2)
                exp(b, n, 6)
                exp(b, n, 7)
                copy_pv(b, 3)
                if not ahead:
                    copy_h2t(2)
                if ahead:
                    exp(b + 1, 1 - n, 0)
                act.wait_ge(ctx_done, after(ctx_done, b + 1))
                act.wait_ge(proj_done, after(proj_done, b))
                act.activation(ctxt[:], w1b[:, PAD:PAD + S], ACT.Identity, bias=col[:, BV:BV + 1]
                               ).then_inc(ctxt_ready, 1)
                if ahead:
                    exp(b + 1, 1 - n, 1)
                if prep:
                    copy_v(b + 2, n)

            steps(act, step)

            def copy_h3t(g, bank):
                act.wait_ge(t3_done, after(t3_done, g + 1))
                for j in range(2):
                    b = 2 * g + j
                    for dst in (h3t[:, S * b:S * (b + 1)], h3part[:, S * b:S * (b + 1)]):
                        act.activation(dst, bank[:, S * j:S * (j + 1)], ACT.Identity, bias=modt[:, 0, b:b + 1],
                                       scale=modt[:, 1, b:b + 1]).then_inc(h3t_ready, 1)

            def weight_part(i):
                w, e = i // 2, E // 2 * (i % 2)
                act.activation(wpart[:, w, e:e + E // 2, :], (wgs, wus)[w][:, e:e + E // 2, :],
                               ACT.Copy).then_inc(wpart_ready, 1)

            def silu(u, e):
                act.wait_ge(gate_done, after(gate_done, u + 1))
                act.wait_ge(hh_ready, after(hh_ready, u - 1))
                act.activation(sg[e % 2][:], bk[e % 2][:], ACT.Silu).then_inc(silu_done, 1)

            for g in range(NG):
                for c in range(FF):
                    act.wait_ge(w1_done, after(w1_done, FF * g + c + 1))
                    act.wait_ge(w2_done, after(w2_done, FF * (g - 1) + c + 1))
                    act.activation(gt[:, c, :], bk[2 + c][:], ACT.Gelu, bias=col[:, B1 + c:B1 + c + 1]
                                   ).then_inc(gelu_done, 1)
                    if g == 0 and c == 3:
                        act.wait_ge(late_loaded, after(late_loaded, 128))
                        weight_part(0)
                    if g == 1 and c > 0:
                        weight_part(c)
                    if g == 3 and c == 3:
                        copy_h3t(1, psa[1])
                    if g == 1 and c == 1:
                        copy_h2t(NG - 1)
                if g == 2:
                    copy_h3t(0, psa[0])
            def routing_exps(part, j):
                tiles = slice(*ROUTED[part])
                act.wait_ge(rt_step, after(rt_step, RT_ALL * part + (RT_DIST if j else 1)))
                for dst, factor in ((2, -1.0 / 0.1), (3, -1.0 / 0.3)) if j else ((1, -1.0),):
                    act.activation(rt[dst][:, tiles], rt[0][:, tiles], ACT.Exp, scale=factor).then_inc(rt_exp, 1)

            routing_exps(0, 0)
            routing_exps(0, 1)
            for e in range(E):
                silu(e, e)
                if e == 1:
                    copy_h3t(NG - 2, bk[4])
            for e in range(E):
                silu(E + e, e)
                if e == 4:
                    copy_h3t(NG - 1, bk[6])
                elif e == 6:
                    routing_exps(1, 0)
                elif e == 7:
                    routing_exps(1, 1)
            with act.Fori(2, NG) as g:
                for e in range(E):
                    silu(E * g + e, e)

        @block.gpsimd
        def _(pool):
            def root(dst, src, n, s):
                pool.tensor_tensor(dst, src, mhalf[:, 0:n], ALU.pow).then_inc(s, 1)

            def two(ap):
                return ap.rearrange("p (o d) -> p o d", o=1).broadcast_to([P, TPB, D])

            def first_root_x(b):
                pool.wait_ge(ln_dve, after(ln_dve, 14 * b + 5))
                root(rs[:, 0:TPB], ve[:, 0:TPB], TPB, ln_pool)

            def norm_x(b):
                pool.wait_ge(ln_dve, after(ln_dve, 14 * b + 7))
                pool.wait_ge(mod_ready, after(mod_ready, 2 * (b + 1)))
                pool.tensor_tensor(h1[:], xh[:], modb[:, ds(b, 1), CA, :].broadcast_to([P, TPB, D]), ALU.mult
                                   ).then_inc(ln_pool, 1)
                pool.wait_ge(ln_pool, after(ln_pool, 5 * b + 2))
                pool.tensor_tensor(h1[:], h1[:], modb[:, ds(b, 1), SA, :].broadcast_to([P, TPB, D]), ALU.add
                                   ).then_inc(ln_pool, 1)
                pool.wait_ge(ln_pool, after(ln_pool, 5 * b + 3))
                pool.tensor_tensor(res[:, ds(TPB * b, TPB), :], h1[:], two(row[:, 0, :]), ALU.add
                                   ).then_inc(ln_pool, 1)

            def second_root_x(b):
                pool.wait_ge(ln_dve, after(ln_dve, 14 * b + 12))
                root(rs[:, 0:TPB], ve[:, 0:TPB], TPB, ln_pool)

            def root_tokens(g):
                pool.wait_ge(ln2_step, after(ln2_step, 9 * (g + 1)))
                root(rs[:, 0:GT], ve[:, 0:GT], GT, ln2_root)

            def copy_x1v(b, n):
                pool.wait_ge(x1t_ready, after(x1t_ready, 2 * (b + 1)))
                pool.wait_ge(v_done, after(v_done, 2 * (b - 1)))
                apart(pool)
                pool.tensor_copy(x1v[n][:, PAD:PAD + S], x1t[n][:, PAD:PAD + S]).then_inc(x1v_ready, 1)

            def cut_m(b, hf):
                pool.wait_ge(max_done, after(max_done, 8 * b + 4 * hf + 4))
                pool.wait_ge(mt_done, after(mt_done, 2 * b + hf))
                apart(pool)
                src = nm[:, 4 * hf:4 * hf + 4, :].rearrange("p g h -> p (g h)")
                pool.tensor_copy(mp[:, 0, :], src).then_inc(mp_step, 1)
                pool.wait_ge(mp_step, after(mp_step, 4 * b + 2 * hf + 1))
                pool.tensor_tensor(mp[:, 1, :], src, mp[:, 0, :], ALU.subtract).then_inc(mp_step, 1)

            pool.memset(mhalf[:], -0.5).then_inc(consts_pool, 1)
            pool.memset(x1v[0][:], 0.0).then_inc(consts_pool, 1)
            pool.memset(x1v[1][:], 0.0).then_inc(consts_pool, 1)
            pool.memset(vb[0][:], 0.0).then_inc(consts_pool, 1)
            pool.memset(vb[1][:], 0.0).then_inc(consts_pool, 1)
            pool.wait_ge(consts_pool, after(consts_pool, 5))
            pool.wait_ge(small_loaded, after(small_loaded, 96))
            first_root_x(0)
            norm_x(0)
            second_root_x(0)
            first_root_x(1)
            norm_x(1)
            second_root_x(1)
            copy_x1v(0, 0)
            first_root_x(2)
            norm_x(2)
            second_root_x(2)
            copy_x1v(1, 1)
            cut_m(0, 0)
            cut_m(0, 1)

            def step(b, n, norm, prep, ahead):
                group = group_normed(norm, prep, ahead)
                if norm:
                    first_root_x(b + 3)
                if ahead:
                    cut_m(b + 1, 0)
                if group is not None:
                    root_tokens(group)
                if prep:
                    copy_x1v(b + 2, n)
                if norm:
                    norm_x(b + 3)
                    second_root_x(b + 3)
                if ahead:
                    cut_m(b + 1, 1)

            steps(pool, step)

            def token_rest(g):
                pool.wait_ge(h3t_ready, after(h3t_ready, 4 * (g + 1)))
                tokens = slice(GW * g, GW * (g + 1))
                pool.tensor_tensor(h3rest[:, tokens], h3t[:, tokens], h3part[:, tokens].bitcast(F32), ALU.subtract
                                   ).then_inc(h3rest_ready, 1)

            def weight_rest(i):
                w, e = i // 2, E // 2 * (i % 2)
                pool.wait_ge(wpart_ready, after(wpart_ready, i + 1))
                pool.tensor_tensor(wrest[:, w, e:e + E // 2, :], (wgs, wus)[w][:, e:e + E // 2, :],
                                   wpart[:, w, e:e + E // 2, :].bitcast(F32), ALU.subtract).then_inc(wrest_ready, 1)

            def bias_residual(g):
                pool.wait_ge(comb_step, after(comb_step, 3 * g - 2))
                pool.tensor_tensor(resb[:], res[:, GT * g:GT * (g + 1), :],
                                   row[:, 1:2, :].broadcast_to([P, GT, D]), ALU.add).then_inc(resb_ready, 1)

            root_tokens(NG - 1)
            bias_residual(0)
            weight_rest(0)
            def root_normed(g):
                pool.wait_ge(ln3_step, after(ln3_step, 13 * g + 9))
                root(rs[:, 0:GT], ve[:, 0:GT], GT, ln3_root)

            root_normed(0)
            bias_residual(1)
            weight_rest(1)
            weight_rest(2)
            root_normed(1)
            bias_residual(2)
            weight_rest(3)
            token_rest(0)
            root_normed(2)
            bias_residual(3)
            token_rest(1)
            root_normed(3)
            token_rest(2)
            token_rest(3)
            pool.wait_ge(gate_step, after(gate_step, 8))
            with pool.Fori(0, NG - 1) as g:
                finish(pool, g)

        @block.vector
        def _(dve):
            def stats(src_of, s, base, n, st_, mv_, ve_):
                apart(dve)
                for k in range(n):
                    dve.bn_stats(st_[:, k, :], src_of(k)).then_inc(s, 1)
                dve.wait_ge(s, after(s, base + n))
                apart(dve)
                for k in range(n):
                    dve.bn_aggr(mv_[:, k, :], st_[:, k, :]).then_inc(s, 1)
                dve.wait_ge(s, after(s, base + 2 * n))
                dve.tensor_scalar(ve_, mv_[:, 0:n, 1], EPS, None, ALU.add).then_inc(s, 1)

            def standard(dst, src, mean, r):
                return dve.tensor_scalar(dst, src, mean, r, ALU.subtract, ALU.mult)

            def ln_a(b):
                stats(lambda k: xs[:, ds(TPB * b + k, 1), :], ln_dve, 14 * b, TPB, st, mv, ve[:, 0:TPB])

            def ln_b(b):
                dve.wait_ge(ln_pool, after(ln_pool, 5 * b + 1))
                for k in range(TPB):
                    standard(xh[:, k, :], xs[:, ds(TPB * b + k, 1), :], mv[:, k, 0:1], rs[:, k:k + 1]
                             ).then_inc(ln_dve, 1)

            def ln_c(b):
                dve.wait_ge(ln_dve, after(ln_dve, 14 * b + 7))
                dve.wait_ge(ln_pool, after(ln_pool, 5 * b + 3))
                stats(lambda k: h1[:, k, :], ln_dve, 14 * b + 7, TPB, st, mv, ve[:, 0:TPB])

            def ln_d(b):
                dve.wait_ge(ln_pool, after(ln_pool, 5 * b + 5))
                dve.wait_ge(xt_done, after(xt_done, b))
                for k in range(TPB):
                    standard(x1h[:, k, :], h1[:, k, :], mv[:, k, 0:1], rs[:, k:k + 1]).then_inc(ln_dve, 1)

            def spread_sc(b0, n):
                dve.tensor_copy(scb[:, b0:b0 + n, :],
                                sce[:, 3, b0:b0 + n].rearrange("p (b o) -> p b o", o=1).broadcast_to([P, n, P])
                                ).then_inc(scb_ready, 1)

            def cut_qk(b, half):
                if half == 0:
                    dve.wait_ge(qk_ready, after(qk_ready, 4 * (b + 1)))
                    dve.tensor_tensor(qkr[:], qk[:], parts[:, 0], ALU.subtract).then_inc(parts_step, 1)
                else:
                    dve.wait_ge(parts_step, after(parts_step, 3 * b + 1))
                    dve.tensor_copy(parts[:, 1], qkr[:]).then_inc(parts_step, 1)
                    dve.wait_ge(parts_step, after(parts_step, 3 * b + 2))
                    dve.tensor_tensor(parts[:, 2], qkr[:], parts[:, 1], ALU.subtract).then_inc(parts_step, 1)

            def maxima(b, g):
                dve.wait_ge(a_done, after(a_done, 8 * b + g + 1))
                dve.wait_ge(mp_step, after(mp_step, 4 * (b - 1) + 2 * (g // 4) + 2))
                dve.tensor_reduce(nm[:, g, :], psa[g % 2][:].rearrange("p (h k) -> p h k", h=H2), AX_X, ALU.max,
                                  negate=True).then_inc(max_done, 1)

            def copy_mt(b, hf):
                dve.wait_ge(mt_done, after(mt_done, 2 * b + hf + 1))
                dve.wait_ge(mrow_ready, after(mrow_ready, 64 * (2 * b + hf)))
                dve.tensor_copy(mt[:], (psa[0] if hf else w1b)[0:64, 0:64].bitcast(BF16)).then_inc(mt_ready, 1)

            def normalise(b, gp):
                dve.wait_ge(pt_done, after(pt_done, 4 * b + gp + 1))
                eo, par = gp // 2, gp % 2
                base = 16 * b + 4 * gp
                sums = pst[:].rearrange("p (h w v) -> p h w v", h=H2, v=VC)
                dve.wait_ge(norm_step, after(norm_step, base))
                dve.reciprocal(rsum[:], sums[:, :, :, HD]).then_inc(norm_step, 1)
                dve.wait_ge(norm_step, after(norm_step, base + 1))
                dve.tensor_tensor(fac[:], rsum[:], alph[:, eo:eo + 1, :].broadcast_to([P, H2, 4]), ALU.mult
                                  ).then_inc(norm_step, 1)
                dve.wait_ge(norm_step, after(norm_step, base + 2))
                dve.wait_ge(ctx_done, after(ctx_done, b))
                for sel in range(2):
                    p = slice(WIN * sel, WIN * sel + WIN)
                    dst = ctxn[p, eo, :, WIN * par:WIN * par + WIN].rearrange("p f (h d) -> p f h d", d=HD)
                    src = sums[p, :, 2 * sel:2 * sel + 2, 0:HD].rearrange("p h f d -> p f h d")
                    f = fac[p, :, 2 * sel:2 * sel + 2].rearrange("p h (f o) -> p f h o", o=1)
                    dve.tensor_tensor(dst, src, f.broadcast_to([WIN, 2, H2, HD]), ALU.mult
                                      ).then_inc(norm_step, 1)

            def attention_out(b):
                dve.wait_ge(proj_done, after(proj_done, b + 1))
                dve.wait_ge(ln_pool, after(ln_pool, 5 * b + 4))
                tiles = res[:, ds(TPB * b, TPB), :]
                dve.tensor_tensor(tiles, w1b[:, 0:S].rearrange("p (k d) -> p k d", k=TPB), tiles, ALU.add
                                  ).then_inc(att_ready, 1)

            def ln2_stats(g):
                dve.wait_ge(att_ready, after(att_ready, 2 * (g + 1)))
                stats(lambda k: res[:, GT * g + k, :], ln2_step, 9 * g, GT, st, mv, ve[:, 0:GT])

            def normed_tokens(g):
                dve.wait_ge(ln2_root, after(ln2_root, g + 1))
                dve.wait_ge(t2_done, after(t2_done, g - 1))
                for k in range(GT):
                    t = GT * g + k
                    m = standard(xh2[g % 2][:, k, :], res[:, t, :], mv[:, k, 0:1], rs[:, k:k + 1])
                m.then_inc(xh2_ready, 1)

            def gate(c):
                dve.wait_ge(mod_ready, after(mod_ready, 2 * B))
                g_v, step_ = modb[:, :, c, :], 4 * (c - GA)
                size = rc[0][:].rearrange("p t e f -> p (t e f)").rearrange("p (b d) -> p b d", b=B)
                dve.scalar_tensor_tensor(out=size, in0=g_v, scalar=-1.0, in1=g_v, op0=ALU.mult, op1=ALU.max
                                         ).then_inc(gate_step, 1)
                dve.wait_ge(gate_step, after(gate_step, step_ + 1))
                dve.tensor_scalar(size, size, 0.25, None, ALU.max).then_inc(gate_step, 1)
                dve.tensor_scalar(g_v, g_v, 0.0, 2.0, ALU.is_ge, ALU.mult).then_inc(gate_step, 1)
                dve.wait_ge(gate_step, after(gate_step, step_ + 3))
                dve.scalar_tensor_tensor(out=g_v, in0=g_v, scalar=1.0, in1=size, op0=ALU.subtract, op1=ALU.mult
                                         ).then_inc(gate_step, 1)
                dve.wait_ge(gate_step, after(gate_step, step_ + 4))

            dve.wait_ge(sc_exp, after(sc_exp, 1))
            dve.tensor_scalar(sce[:, 1, :], sce[:, 0, :], 1.0, None, ALU.add).then_inc(sc_step, 1)
            dve.wait_ge(sc_step, after(sc_step, 1))
            dve.reciprocal(sce[:, 2, :], sce[:, 1, :]).then_inc(sc_step, 1)
            dve.wait_ge(sc_step, after(sc_step, 2))
            dve.tensor_tensor(sce[:, 3, :], sce[:, 2, :], cts[:], ALU.mult).then_inc(sc_step, 1)
            dve.wait_ge(sc_step, after(sc_step, 3))
            spread_sc(0, 2)
            dve.wait_ge(x_first, after(x_first, 16))
            ln_a(0)
            spread_sc(2, B - 2)
            dve.wait_ge(consts_pool, after(consts_pool, 1))
            ln_b(0)
            dve.wait_ge(small_loaded, after(small_loaded, 96))
            dve.tensor_copy(idb[:], idf[:]).then_inc(consts, 1)
            dve.tensor_copy(monesb[:], monesf[:]).then_inc(consts, 1)
            dve.tensor_scalar(bqs[:], col[:, BQ:BQ + 1], SCALE, None, ALU.mult).then_inc(consts, 1)
            ln_c(0)
            dve.wait_ge(consts_pool, after(consts_pool, 5))
            for n in range(2):
                for half in range(2):
                    p = slice(WIN * half, WIN * half + WIN)
                    for sel in range(2):
                        dve.tensor_copy(vb[n][p, :, :, sel, half, HD],
                                        vmsk[p, :, sel:sel + 1].broadcast_to([WIN, 2, NH])).then_inc(consts, 1)
            ln_d(0)
            dve.wait_ge(x_rest, after(x_rest, 16))
            ln_a(1)
            ln_b(1)
            ln_c(1)
            cut_qk(0, 0)
            cut_qk(0, 1)
            ln_d(1)
            ln_a(2)
            ln_b(2)
            cut_qk(1, 0)
            cut_qk(1, 1)
            ln_c(2)
            ln_d(2)
            for g in range(5):
                maxima(0, g)
            copy_mt(0, 0)
            for g in range(5, 8):
                maxima(0, g)

            def step(b, n, norm, prep, ahead):
                def maxima_next(g):
                    if ahead:
                        maxima(b + 1, g)

                copy_mt(b, 1)
                group = group_normed(norm, prep, ahead)
                maxima_next(0)
                maxima_next(1)
                normalise(b, 0)
                if norm:
                    ln_a(b + 3)
                maxima_next(2)
                maxima_next(3)
                if group is not None:
                    ln2_stats(group)
                if norm:
                    ln_b(b + 3)
                if prep:
                    cut_qk(b + 2, 0)
                if ahead:
                    copy_mt(b + 1, 0)
                if prep:
                    cut_qk(b + 2, 1)
                normalise(b, 1)
                if group is not None:
                    normed_tokens(group)
                maxima_next(4)
                if not ahead:
                    gate(GA)
                if norm:
                    ln_c(b + 3)
                maxima_next(5)
                normalise(b, 2)
                maxima_next(6)
                normalise(b, 3)
                maxima_next(7)
                if norm:
                    ln_d(b + 3)
                attention_out(b)
                if not ahead:
                    ln2_stats(NG - 1)

            steps(dve, step)

            normed_tokens(NG - 1)
            gate(GB)

            def combine(g):
                dve.wait_ge(w2_done, after(w2_done, FF * (g + 1)))
                dve.wait_ge(resb_ready, after(resb_ready, g + 1))
                tiles = xs[:, GT * g:GT * (g + 1), :]
                dve.tensor_tensor(comb[:], bk[6][:].rearrange("p (k d) -> p k d", k=GT), resb[:], ALU.add
                                  ).then_inc(comb_step, 1)
                dve.wait_ge(comb_step, after(comb_step, 3 * g + 1))
                ga = modb[:, 2 * g:2 * g + 2, GA:GA + 1, :].broadcast_to([P, 2, TPB, D])
                comb_v = comb[:].rearrange("p (b k) d -> p b k d", b=2)
                dve.tensor_tensor(comb_v, comb_v, ga, ALU.mult).then_inc(comb_step, 1)
                dve.wait_ge(comb_step, after(comb_step, 3 * g + 2))
                dve.tensor_tensor(tiles, tiles, comb[:], ALU.add).then_inc(comb_step, 1)
                dve.wait_ge(comb_step, after(comb_step, 3 * g + 3))

            def ln3_stats(g):
                stats(lambda k: xs[:, GT * g + k, :], ln3_step, 13 * g, GT, st, mv, ve[:, 0:GT])

            def ln3_out(g, beside=range(0)):
                dve.wait_ge(ln3_root, after(ln3_root, g + 1))
                if g < 2:
                    dve.wait_ge(t2_done, after(t2_done, NG))
                else:
                    dve.wait_ge(t3_done, after(t3_done, g - 1))
                for k in range(GT):
                    standard(xh2[g % 2][:, k, :], xs[:, GT * g + k, :], mv[:, k, 0:1], rs[:, k:k + 1]
                             ).then_inc(ln3_step, 1)
                    for step in beside[len(beside) * k // GT:len(beside) * (k + 1) // GT]:
                        route(0, step)

            def product(u, e):
                dve.wait_ge(silu_done, after(silu_done, u + 1))
                dve.wait_ge(up_done, after(up_done, u + 1))
                dve.wait_ge(down_done, after(down_done, u - E + 1))
                dve.tensor_tensor(hh[e][:], sg[e % 2][:], bk[2 + e % 2][:], ALU.mult).then_inc(hh_ready, 1)

            def per_token(t, shape):
                return t.rearrange("p (t o) -> p t o", o=1).broadcast_to(shape)

            def route(part, step):
                t0, t1 = ROUTED[part]
                z, ex, wz, fb, inh = [t[:, t0:t1] for t in rt]
                rank = inh
                larger, equal = [t[:, t0:t1] for t in rc]
                sum_z, sum_1, sum_2 = [t[:, t0:t1] for t in rsm]
                by_e, by_pair = [P, t1 - t0, E], [P, t1 - t0, E, E]
                dve.wait_ge(rt_step, after(rt_step, RT_ALL * part + step - 1))
                if step == 1:
                    dve.wait_ge(router_done, after(router_done, -(-t1 // GT)))
                    logits = bk[7][:, E * t0:E * t1].rearrange("p (t e) -> p t e", e=E)
                    m = dve.tensor_scalar(z, logits, rtemp[:], None, ALU.mult)
                elif step == 2:
                    dve.wait_ge(rt_exp, after(rt_exp, 3 * part + 1))
                    m = dve.tensor_scalar(ex, ex, 1.0, None, ALU.add)
                elif step == 3:
                    m = dve.reciprocal(inh, ex)
                elif step == 4:
                    m = dve.tensor_scalar(ex, inh, ZONE_LOW, None, ALU.is_ge)
                elif step == 5:
                    m = dve.tensor_scalar(wz, inh, ZONE_MID, None, ALU.subtract)
                elif step == RT_DIST:
                    m = dve.scalar_tensor_tensor(out=z, in0=wz, scalar=-1.0, in1=wz, op0=ALU.mult, op1=ALU.max)
                elif step == 7:
                    m = dve.scalar_tensor_tensor(out=ex, in0=inh, scalar=ZONE_HIGH, in1=ex, op0=ALU.is_le,
                                                 op1=ALU.mult)
                elif step == 8:
                    dve.wait_ge(rt_exp, after(rt_exp, 3 * part + 3))
                    m = dve.tensor_tensor(wz, wz, ex, ALU.mult)
                elif step == 9:
                    m = dve.tensor_reduce(sum_z, wz, AX_X, ALU.add)
                elif step == 10:
                    fb_e = fb.rearrange("p t (e o) -> p t e o", o=1).broadcast_to(by_pair)
                    fb_f = fb.rearrange("p t (o f) -> p t o f", o=1).broadcast_to(by_pair)
                    m = dve.tensor_tensor(larger, fb_f, fb_e, ALU.subtract)
                elif step == 11:
                    before = earl[:].rearrange("p (o e) f -> p o e f", o=1).broadcast_to(by_pair)
                    m = dve.scalar_tensor_tensor(out=equal, in0=larger, scalar=0.0, in1=before, op0=ALU.is_ge,
                                                 op1=ALU.mult)
                elif step == 12:
                    m = dve.scalar_tensor_tensor(out=larger, in0=larger, scalar=0.0, in1=equal, op0=ALU.is_gt,
                                                 op1=ALU.max)
                elif step == 13:
                    m = dve.tensor_reduce(rank, larger, AX_X, ALU.add)
                elif step == 14:
                    m = dve.scalar_tensor_tensor(out=fb, in0=rank, scalar=1.5, in1=fb, op0=ALU.is_lt, op1=ALU.mult)
                elif step == 15:
                    m = dve.tensor_reduce(sum_1, fb, AX_X, ALU.add)
                elif step == 16:
                    m = dve.tensor_scalar(sum_1, sum_1, 1e-8, None, ALU.max)
                elif step == 17:
                    m = dve.reciprocal(sum_2, sum_1)
                elif step == 18:
                    m = dve.tensor_tensor(fb, fb, per_token(sum_2, by_e), ALU.mult)
                elif step == 19:
                    m = dve.tensor_scalar(sum_1, sum_z, 1e-8, None, ALU.is_lt)
                elif step == 20:
                    m = dve.tensor_scalar(sum_2, sum_z, 1e-8, None, ALU.is_ge)
                elif step == 21:
                    m = dve.tensor_tensor(fb, fb, per_token(sum_1, by_e), ALU.mult)
                elif step == 22:
                    m = dve.tensor_tensor(wz, wz, per_token(sum_2, by_e), ALU.mult)
                elif step == 23:
                    m = dve.tensor_tensor(wz, wz, fb, ALU.add)
                elif step == 24:
                    m = dve.tensor_reduce(sum_z, wz, AX_X, ALU.add)
                elif step == 25:
                    m = dve.tensor_scalar(sum_z, sum_z, 1e-8, None, ALU.max)
                elif step == 26:
                    m = dve.reciprocal(sum_1, sum_z)
                elif step == RT_ALL:
                    m = dve.tensor_tensor(wz, wz, per_token(sum_1, by_e), ALU.mult)
                m.then_inc(rt_step, 1)

            def accumulate(g, e, beside=range(0)):
                u = E * g + e
                if e == 0:
                    dve.wait_ge(fin_step, after(fin_step, 2 * g - 1))
                dve.wait_ge(down_done, after(down_done, u + 1))
                dve.wait_ge(acc_step, after(acc_step, GT * u))
                for k in range(GT):
                    src, w = bk[4 + e % 2][:, k * P:(k + 1) * P], rt[2][:, ds(GT * g + k, 1), e]
                    if e == 0:
                        dve.tensor_scalar(acc[:, k, :], src, w, None, ALU.mult).then_inc(acc_step, 1)
                    else:
                        dve.scalar_tensor_tensor(out=acc[:, k, :], in0=src, scalar=w, in1=acc[:, k, :], op0=ALU.mult,
                                                 op1=ALU.add).then_inc(acc_step, 1)
                    for step in beside[len(beside) * k // GT:len(beside) * (k + 1) // GT]:
                        route(1, step)

            dve.wait_ge(late_loaded, after(late_loaded, 128))
            dve.reciprocal(rtemp[:], temps[:]).then_inc(consts, 1)
            dve.wait_ge(consts, after(consts, 12))
            for g in range(NG - 2):
                combine(g)
                ln3_stats(g)
                ln3_out(g)

            combine(NG - 2)
            ln3_stats(NG - 2)
            route(0, 1)
            ln3_out(NG - 2, range(2, RT_DIST + 1))
            for e, last in enumerate(FIRST_ROUTING):
                for step in range(FIRST_ROUTING[e - 1] + 1 if e else RT_DIST + 1, last + 1):
                    route(0, step)
                product(e, e)
            for step in range(FIRST_ROUTING[-1] + 1, RT_ALL + 1):
                route(0, step)
            dve.wait_ge(rt_step, after(rt_step, RT_ALL))
            for e in range(LAG, E):
                accumulate(0, e - LAG)
                if e == LAG:
                    combine(NG - 1)

            for u in range(E, E * NG):
                if u == E + 1:
                    ln3_stats(NG - 1)
                elif u == E + 2:
                    ln3_out(NG - 1)
                elif u == 2 * E + LAG:
                    dve.wait_ge(rt_step, after(rt_step, 2 * RT_ALL))
                product(u, u % E)
                for v in downs_after(u):
                    accumulate(v // E, v % E, SECOND_ROUTING.get(u, range(0)))
            finish(dve, NG - 1)


def downs_after(u):
    first = E * (NG - 1)
    if u < first:
        return range(u - LAG, u - LAG + 1) if u >= LAG else range(0)
    done = [first - LAG + n for n in CATCH_UP]
    return range(done[u - first], done[u - first + 1])


CATCH_UP = (0, 1, 3, 4, 6, 7, 9, 11, LAG + E)
ROUTED = ((0, NT // 2), (NT // 2, NT))
RT_DIST = 6
RT_ALL = 27
FIRST_ROUTING = (9, 10, 11, 12, 13, 15, 20, 24)
SECOND_ROUTING = {13: range(1, 2), 14: range(2, 5), 15: range(5, 8), 16: range(8, 11), 17: range(11, 13),
                  18: range(13, 16), 19: range(16, 20), 20: range(20, 24), 21: range(24, 28)}


def kernel(**inputs):
    import numpy as np
    import concourse.bacc as bacc
    from concourse.bass_utils import run_bass_kernel_spmd

    a = {k.removeprefix("L0_").removeprefix("attn_").removeprefix("ffn_"): np.asarray(v)
         for k, v in inputs.items()}
    ramp = np.linspace(0.0, 1.0, WIN // 2, dtype=np.float32)
    alpha = np.ones((2, WIN, 2, 2, 2), np.float32)
    vmask = np.ones((P, 2, 2), np.float32)
    for sel in range(2):
        for eo in range(2):
            for half in range(2):
                w = 4 * sel + 2 * half + eo
                if w > 0:
                    alpha[:, :WIN // 2, eo, sel, half] = ramp
                if w < S // (WIN // 2) - 1:
                    alpha[:, WIN // 2:, eo, sel, half] = 1 - ramp
    vmask[:PAD, 0, 0] = 0
    vmask[P - PAD:, 1, 1] = 0
    mones = np.zeros((2, 2, P), np.float32)
    mones[:, 0, :WIN] = 1
    mones[:, 1, WIN:] = 1
    wmod = a["wmod"].reshape(D, 6, D)[:, [1, 0, 2, 5, 3, 4], :].reshape(D, 6 * D)
    arrays = {
        "x": a["hidden_states"],
        "wqkvp": np.concatenate([a["wq"], a["wk"], a["wv"], a["wproj"]], axis=1),
        "w1": a["w1"], "w2": a["w2"], "wg": a["Wg"], "wu": a["Wu"], "wd": a["Wd"], "wr": a["Wr"],
        "temp": a["temperature"],
        "c_t": a["c"].T, "wmod": wmod,
        "cols": np.stack([a["ln1_g"], a["ln1_b"], a["bq"], a["bk"], a["bv"], a["ln2_g"], a["ln2_b"],
                          *a["b1"].reshape(FF, P)], axis=1),
        "rows": np.concatenate([a["bproj"], a["b2"]])[None],
        "ident": np.eye(P, dtype=np.float32),
        "alpha": alpha.reshape(P, 2, 4),
        "vmask": vmask,
        "mones": mones.reshape(4, P),
        "earlier": np.tril(np.ones((E, E), np.float32), -1)[None],
    }
    arrays = {f"in_{k}": np.ascontiguousarray(v) for k, v in arrays.items()}
    nc = bacc.Bacc("TRN2", target_bir_lowering=False, num_devices=1)
    args = [nc.dram_tensor(k, v.shape, mybir.dt.from_np(v.dtype), kind="ExternalInput").ap()
            for k, v in arrays.items()]
    args.append(nc.dram_tensor("out_x", (B, S, D), F32, kind="ExternalOutput").ap())
    build(nc, *args)
    return run_bass_kernel_spmd(nc, [arrays], core_ids=[0]).results[0]["out_x"]
```
